# Optimizing a Trainium2 kernel written in Bass

```python
import numpy as np
import jax
import jax.numpy as jnp

def _softmax(x, axis=-1):
    return jax.nn.softmax(x, axis=axis)

def _gelu(x):
    return jax.nn.gelu(x, approximate=True)

def _silu(x):
    return jax.nn.silu(x)

def _sigmoid(x):
    return jax.nn.sigmoid(x)

def _layernorm(x, axis=-1, eps=1e-05):
    m = jnp.mean(x, axis=axis, keepdims=True)
    v = jnp.var(x, axis=axis, keepdims=True)
    return (x - m) / jnp.sqrt(v + eps)

def _scatter_add(tgt, idx, src, axis=0):
    return tgt.at[idx].add(src)

def _segment_sum(src, seg, n):
    return jax.ops.segment_sum(src, seg, n)
kernel_name = 'mk_gnn_resnorm_d4_gnn_r32_543b36'

def setup_inputs(seed: int=0):
    np.random.seed(seed)
    _w = jnp.asarray

    def _rec_inputs():
        import jax
        import jax.numpy as jnp
        _gk = jax.random.key(seed)
        x = -0.0003713 + 1 * jax.random.normal(jax.random.fold_in(_gk, 1), (3125, 128), jnp.float32)
        src = jax.random.randint(jax.random.fold_in(_gk, 2), (100000,), 0, 3125, jnp.int32)
        dst = jnp.minimum((3125 * jax.random.uniform(jax.random.fold_in(_gk, 3), (100000,)) ** 2.0).astype(jnp.int32), 99999)
        _o = jnp.argsort(dst, stable=True)
        src = src[_o]
        dst = dst[_o]
        edge_attr_64 = -0.000128692 + 0.999872 * jax.random.normal(jax.random.fold_in(_gk, 13), (100000, 64), jnp.float32)
        return (x, src, dst, edge_attr_64)
    x, src, dst, edge_attr_64 = _rec_inputs()

    def _L0_gnn_setup():
        import jax, jax.numpy as jnp
        import numpy as np
        N_NODES = 3125
        N_EDGES = 20000
        NODE_DIM = 128
        EDGE_DIM = 64
        NUM_HEADS = 4
        EPS = 1e-06

        def _segment_softmax_aggregate(values, scores_mean, dst, num_nodes):
            max_scores = jax.ops.segment_max(scores_mean, dst, num_segments=num_nodes)
            max_scores = jnp.where(jnp.isneginf(max_scores), jnp.zeros_like(max_scores), max_scores)
            exp_scores = jnp.exp(scores_mean - max_scores[dst])
            sum_exp = jax.ops.segment_sum(exp_scores, dst, num_segments=num_nodes)
            attn_weights = exp_scores / (sum_exp[dst] + EPS)
            return jax.ops.segment_sum(values * attn_weights[:, None], dst, num_segments=num_nodes)
        key = jax.random.key(seed)
        ks = jax.random.split(key, 12)
        s_attn = 1.0 / np.sqrt(NODE_DIM + EDGE_DIM)
        s_ev = 1.0 / np.sqrt(EDGE_DIM)
        s_out = 1.0 / np.sqrt(NODE_DIM)
        return {'node_features': jax.random.normal(ks[0], (N_NODES, NODE_DIM), jnp.float32), 'edge_features': jax.random.normal(ks[1], (N_EDGES, EDGE_DIM), jnp.float32), 'attn_W': jax.random.uniform(ks[2], (NODE_DIM + EDGE_DIM, NUM_HEADS), jnp.float32, -s_attn, s_attn), 'attn_b': jax.random.uniform(ks[3], (NUM_HEADS,), jnp.float32, -s_attn, s_attn), 'ev_W': jax.random.uniform(ks[4], (EDGE_DIM, NODE_DIM), jnp.float32, -s_ev, s_ev), 'ev_b': jax.random.uniform(ks[5], (NODE_DIM,), jnp.float32, -s_ev, s_ev), 'out1_W': jax.random.uniform(ks[6], (NODE_DIM, NODE_DIM), jnp.float32, -s_out, s_out), 'out1_b': jax.random.uniform(ks[7], (NODE_DIM,), jnp.float32, -s_out, s_out), 'out2_W': jax.random.uniform(ks[8], (NODE_DIM, NODE_DIM), jnp.float32, -s_out, s_out), 'out2_b': jax.random.uniform(ks[9], (NODE_DIM,), jnp.float32, -s_out, s_out), 'edge_index': jax.random.randint(ks[10], (2, N_EDGES), 0, N_NODES, jnp.int64 if jax.config.jax_enable_x64 else jnp.int32)}
    _L0_gnn_all = _L0_gnn_setup()
    _L0_gnn_in = {k: v for k, v in _L0_gnn_all.items() if k in ('attn_W', 'attn_b', 'ev_W', 'ev_b', 'out1_W', 'out1_b', 'out2_W', 'out2_b')}
    del _L0_gnn_all

    def _L1_gnn_setup():
        import jax, jax.numpy as jnp
        import numpy as np
        N, E, DIM, ATTN, HID, B = (50000, 18750, 128, 64, 256, 64)

        def layernorm(x, g, b):
            m = x.mean(-1, keepdims=True)
            v = x.var(-1, keepdims=True)
            return (x - m) * jax.lax.rsqrt(v + 1e-05) * g + b

        def seg_mean(x, idx, num):
            s = jax.ops.segment_sum(x, idx, num_segments=num)
            c = jax.ops.segment_sum(jnp.ones((x.shape[0], 1), x.dtype), idx, num_segments=num)
            return s / jnp.maximum(c, 1.0)

        def _forward(X, g_token, Wg_in_w, Wg_in_b, ln1_g, ln1_b, eps, msg_w, msg_b, lin_w, lin_b, ln2_g, ln2_b, Wq, Wk, Wphi, Wy_w, Wy_b, We_w, We_b, ln3_g, ln3_b, ffn_w1, ffn_b1, ffn_w2, ffn_b2, edge_index, batch_idx, num_graphs):
            n = X.shape[0]
            src, dst = (edge_index[0], edge_index[1])
            g = g_token + seg_mean(X, batch_idx, num_graphs)
            X = X + (g @ Wg_in_w + Wg_in_b)[batch_idx]
            Xn = layernorm(X, ln1_g, ln1_b)
            msg = (Xn @ msg_w + msg_b)[dst]
            agg = jax.ops.segment_sum(msg, src, num_segments=n)
            X = X + jax.nn.relu(((1.0 + eps) * Xn + agg) @ lin_w + lin_b)
            Xn = layernorm(X, ln2_g, ln2_b)
            e = jnp.tanh((Xn @ Wq)[src] + (Xn @ Wk)[dst])
            scores = e @ Wphi
            exp_s = jnp.exp(scores - scores.max())
            denom = jax.ops.segment_sum(exp_s, src, num_segments=n)
            alpha = exp_s / (denom[src] + 1e-09)
            vmsg = alpha[:, None] * ((Xn @ Wy_w + Wy_b)[dst] + (e @ We_w + We_b))
            X = X + jax.ops.segment_sum(vmsg, src, num_segments=n)
            Xn = layernorm(X, ln3_g, ln3_b)
            return X + jax.nn.relu(Xn @ ffn_w1 + ffn_b1) @ ffn_w2 + ffn_b2
        ks = jax.random.split(jax.random.key(seed), 16)
        r = lambda i, shape: jax.random.normal(ks[i], shape, jnp.float32) * 0.05
        z = lambda d: jnp.zeros((d,), jnp.float32)
        o = lambda d: jnp.ones((d,), jnp.float32)
        return {'X': jax.random.normal(ks[0], (N, DIM), jnp.float32), 'edge_index': jax.random.randint(ks[1], (2, E), 0, N), 'batch_idx': jnp.sort(jax.random.randint(ks[2], (N,), 0, B)), 'num_graphs': B, 'g_token': r(3, (1, DIM)), 'Wg_in_w': r(4, (DIM, DIM)), 'Wg_in_b': z(DIM), 'ln1_g': o(DIM), 'ln1_b': z(DIM), 'eps': jnp.zeros((), jnp.float32), 'msg_w': r(5, (DIM, DIM)), 'msg_b': z(DIM), 'lin_w': r(6, (DIM, DIM)), 'lin_b': z(DIM), 'ln2_g': o(DIM), 'ln2_b': z(DIM), 'Wq': r(7, (DIM, ATTN)), 'Wk': r(8, (DIM, ATTN)), 'Wphi': r(9, (ATTN,)), 'Wy_w': r(10, (DIM, DIM)), 'Wy_b': z(DIM), 'We_w': r(11, (ATTN, DIM)), 'We_b': z(DIM), 'ln3_g': o(DIM), 'ln3_b': z(DIM), 'ffn_w1': r(12, (DIM, HID)), 'ffn_b1': z(HID), 'ffn_w2': r(13, (HID, DIM)), 'ffn_b2': z(DIM)}
    _L1_gnn_all = _L1_gnn_setup()
    _L1_gnn_in = {k: v for k, v in _L1_gnn_all.items() if k in ('g_token', 'Wg_in_w', 'Wg_in_b', 'ln1_g', 'ln1_b', 'eps', 'msg_w', 'msg_b', 'lin_w', 'lin_b', 'ln2_g', 'ln2_b', 'Wq', 'Wk', 'Wphi', 'Wy_w', 'Wy_b', 'We_w', 'We_b', 'ln3_g', 'ln3_b', 'ffn_w1', 'ffn_b1', 'ffn_w2', 'ffn_b2')}
    del _L1_gnn_all

    def _L2_gnn_setup():
        import jax, jax.numpy as jnp
        import numpy as np
        N_NODES = 50000
        N_EDGES = 25000
        HIDDEN = 128
        REL = 64

        def _layer_norm(x, gamma, beta, eps=1e-05):
            mu = jnp.mean(x, axis=-1, keepdims=True)
            var = jnp.mean(jnp.square(x - mu), axis=-1, keepdims=True)
            return (x - mu) * jax.lax.rsqrt(var + eps) * gamma + beta
        key = jax.random.key(seed)
        ks = jax.random.split(key, 12)
        s = lambda fan_in: 1.0 / np.sqrt(fan_in)
        inp = {'node_states': jax.random.normal(ks[0], (N_NODES, HIDDEN), dtype=jnp.float32), 'edge_index': jax.random.randint(ks[1], (2, N_EDGES), 0, N_NODES, dtype=jnp.int64), 'edge_rel_emb': jax.random.normal(ks[2], (N_EDGES, REL), dtype=jnp.float32), 'W1': jax.random.uniform(ks[3], (2 * HIDDEN + REL, HIDDEN), jnp.float32, -s(2 * HIDDEN + REL), s(2 * HIDDEN + REL)), 'b1': jax.random.uniform(ks[4], (HIDDEN,), jnp.float32, -s(2 * HIDDEN + REL), s(2 * HIDDEN + REL)), 'W2': jax.random.uniform(ks[5], (HIDDEN, HIDDEN), jnp.float32, -s(HIDDEN), s(HIDDEN)), 'b2': jax.random.uniform(ks[6], (HIDDEN,), jnp.float32, -s(HIDDEN), s(HIDDEN)), 'Wn': jax.random.uniform(ks[7], (HIDDEN, HIDDEN), jnp.float32, -s(HIDDEN), s(HIDDEN)), 'bn': jax.random.uniform(ks[8], (HIDDEN,), jnp.float32, -s(HIDDEN), s(HIDDEN)), 'gamma': jnp.ones((HIDDEN,), jnp.float32), 'beta': jnp.zeros((HIDDEN,), jnp.float32)}
        return inp
    _L2_gnn_all = _L2_gnn_setup()
    _L2_gnn_in = {k: v for k, v in _L2_gnn_all.items() if k in ('W1', 'b1', 'W2', 'b2', 'Wn', 'bn', 'gamma', 'beta')}
    del _L2_gnn_all

    def _L3_gnn_setup():
        import jax, jax.numpy as jnp
        import numpy as np
        N, E, D = (50000, 25000, 128)
        EPS_BN = 1e-05
        EPS_LN = 1e-05

        def _sage_conv(x, src, dst, w_self, w_neigh, b):
            n = x.shape[0]
            msg = x[src]
            agg = jax.ops.segment_sum(msg, dst, num_segments=n)
            deg = jax.ops.segment_sum(jnp.ones((src.shape[0],), x.dtype), dst, num_segments=n)
            h_neigh = agg / jnp.maximum(deg, 1.0)[:, None]
            return x @ w_self + h_neigh @ w_neigh + b

        def _batch_norm(x, gamma, beta):
            mu = jnp.mean(x, axis=0)
            var = jnp.mean(jnp.square(x - mu), axis=0)
            return (x - mu) * jax.lax.rsqrt(var + EPS_BN) * gamma + beta

        def _layer_norm(x, gamma, beta):
            mu = jnp.mean(x, axis=-1, keepdims=True)
            var = jnp.mean(jnp.square(x - mu), axis=-1, keepdims=True)
            return (x - mu) * jax.lax.rsqrt(var + EPS_LN) * gamma + beta
        key = jax.random.key(seed)
        ks = jax.random.split(key, 16)
        s = 1.0 / np.sqrt(D)
        inp = {'x': jax.random.normal(ks[0], (N, D), jnp.float32), 'src': jax.random.randint(ks[1], (E,), 0, N, jnp.int32), 'dst': jax.random.randint(ks[2], (E,), 0, N, jnp.int32), 'w1_self': jax.random.normal(ks[3], (D, D), jnp.float32) * s, 'w1_neigh': jax.random.normal(ks[4], (D, D), jnp.float32) * s, 'b1': jnp.zeros((D,), jnp.float32), 'w2_self': jax.random.normal(ks[5], (D, D), jnp.float32) * s, 'w2_neigh': jax.random.normal(ks[6], (D, D), jnp.float32) * s, 'b2': jnp.zeros((D,), jnp.float32), 'w3_self': jax.random.normal(ks[7], (D, D), jnp.float32) * s, 'w3_neigh': jax.random.normal(ks[8], (D, D), jnp.float32) * s, 'b3': jnp.zeros((D,), jnp.float32), 'bn1_g': jnp.ones((D,), jnp.float32), 'bn1_b': jnp.zeros((D,), jnp.float32), 'bn2_g': jnp.ones((D,), jnp.float32), 'bn2_b': jnp.zeros((D,), jnp.float32), 'ln_g': jnp.ones((D,), jnp.float32), 'ln_b': jnp.zeros((D,), jnp.float32)}
        return inp
    _L3_gnn_all = _L3_gnn_setup()
    _L3_gnn_in = {k: v for k, v in _L3_gnn_all.items() if k in ('w1_self', 'w1_neigh', 'b1', 'w2_self', 'w2_neigh', 'b2', 'w3_self', 'w3_neigh', 'b3', 'bn1_g', 'bn1_b', 'bn2_g', 'bn2_b', 'ln_g', 'ln_b')}
    del _L3_gnn_all
    return {'x': x, 'src': src, 'dst': dst, 'edge_attr_64': edge_attr_64, 'L0_gnn_attn_W': _L0_gnn_in['attn_W'], 'L0_gnn_attn_b': _L0_gnn_in['attn_b'], 'L0_gnn_ev_W': _L0_gnn_in['ev_W'], 'L0_gnn_ev_b': _L0_gnn_in['ev_b'], 'L0_gnn_out1_W': _L0_gnn_in['out1_W'], 'L0_gnn_out1_b': _L0_gnn_in['out1_b'], 'L0_gnn_out2_W': _L0_gnn_in['out2_W'], 'L0_gnn_out2_b': _L0_gnn_in['out2_b'], 'L1_gnn_g_token': _L1_gnn_in['g_token'], 'L1_gnn_Wg_in_w': _L1_gnn_in['Wg_in_w'], 'L1_gnn_Wg_in_b': _L1_gnn_in['Wg_in_b'], 'L1_gnn_ln1_g': _L1_gnn_in['ln1_g'], 'L1_gnn_ln1_b': _L1_gnn_in['ln1_b'], 'L1_gnn_eps': _L1_gnn_in['eps'], 'L1_gnn_msg_w': _L1_gnn_in['msg_w'], 'L1_gnn_msg_b': _L1_gnn_in['msg_b'], 'L1_gnn_lin_w': _L1_gnn_in['lin_w'], 'L1_gnn_lin_b': _L1_gnn_in['lin_b'], 'L1_gnn_ln2_g': _L1_gnn_in['ln2_g'], 'L1_gnn_ln2_b': _L1_gnn_in['ln2_b'], 'L1_gnn_Wq': _L1_gnn_in['Wq'], 'L1_gnn_Wk': _L1_gnn_in['Wk'], 'L1_gnn_Wphi': _L1_gnn_in['Wphi'], 'L1_gnn_Wy_w': _L1_gnn_in['Wy_w'], 'L1_gnn_Wy_b': _L1_gnn_in['Wy_b'], 'L1_gnn_We_w': _L1_gnn_in['We_w'], 'L1_gnn_We_b': _L1_gnn_in['We_b'], 'L1_gnn_ln3_g': _L1_gnn_in['ln3_g'], 'L1_gnn_ln3_b': _L1_gnn_in['ln3_b'], 'L1_gnn_ffn_w1': _L1_gnn_in['ffn_w1'], 'L1_gnn_ffn_b1': _L1_gnn_in['ffn_b1'], 'L1_gnn_ffn_w2': _L1_gnn_in['ffn_w2'], 'L1_gnn_ffn_b2': _L1_gnn_in['ffn_b2'], 'L2_gnn_W1': _L2_gnn_in['W1'], 'L2_gnn_b1': _L2_gnn_in['b1'], 'L2_gnn_W2': _L2_gnn_in['W2'], 'L2_gnn_b2': _L2_gnn_in['b2'], 'L2_gnn_Wn': _L2_gnn_in['Wn'], 'L2_gnn_bn': _L2_gnn_in['bn'], 'L2_gnn_gamma': _L2_gnn_in['gamma'], 'L2_gnn_beta': _L2_gnn_in['beta'], 'L3_gnn_w1_self': _L3_gnn_in['w1_self'], 'L3_gnn_w1_neigh': _L3_gnn_in['w1_neigh'], 'L3_gnn_b1': _L3_gnn_in['b1'], 'L3_gnn_w2_self': _L3_gnn_in['w2_self'], 'L3_gnn_w2_neigh': _L3_gnn_in['w2_neigh'], 'L3_gnn_b2': _L3_gnn_in['b2'], 'L3_gnn_w3_self': _L3_gnn_in['w3_self'], 'L3_gnn_w3_neigh': _L3_gnn_in['w3_neigh'], 'L3_gnn_b3': _L3_gnn_in['b3'], 'L3_gnn_bn1_g': _L3_gnn_in['bn1_g'], 'L3_gnn_bn1_b': _L3_gnn_in['bn1_b'], 'L3_gnn_bn2_g': _L3_gnn_in['bn2_g'], 'L3_gnn_bn2_b': _L3_gnn_in['bn2_b'], 'L3_gnn_ln_g': _L3_gnn_in['ln_g'], 'L3_gnn_ln_b': _L3_gnn_in['ln_b']}

def reference(x, src, dst, edge_attr_64, L0_gnn_attn_W, L0_gnn_attn_b, L0_gnn_ev_W, L0_gnn_ev_b, L0_gnn_out1_W, L0_gnn_out1_b, L0_gnn_out2_W, L0_gnn_out2_b, L1_gnn_g_token, L1_gnn_Wg_in_w, L1_gnn_Wg_in_b, L1_gnn_ln1_g, L1_gnn_ln1_b, L1_gnn_eps, L1_gnn_msg_w, L1_gnn_msg_b, L1_gnn_lin_w, L1_gnn_lin_b, L1_gnn_ln2_g, L1_gnn_ln2_b, L1_gnn_Wq, L1_gnn_Wk, L1_gnn_Wphi, L1_gnn_Wy_w, L1_gnn_Wy_b, L1_gnn_We_w, L1_gnn_We_b, L1_gnn_ln3_g, L1_gnn_ln3_b, L1_gnn_ffn_w1, L1_gnn_ffn_b1, L1_gnn_ffn_w2, L1_gnn_ffn_b2, L2_gnn_W1, L2_gnn_b1, L2_gnn_W2, L2_gnn_b2, L2_gnn_Wn, L2_gnn_bn, L2_gnn_gamma, L2_gnn_beta, L3_gnn_w1_self, L3_gnn_w1_neigh, L3_gnn_b1, L3_gnn_w2_self, L3_gnn_w2_neigh, L3_gnn_b2, L3_gnn_w3_self, L3_gnn_w3_neigh, L3_gnn_b3, L3_gnn_bn1_g, L3_gnn_bn1_b, L3_gnn_bn2_g, L3_gnn_bn2_b, L3_gnn_ln_g, L3_gnn_ln_b):
    import jax
    import jax.numpy as jnp

    def _L0_gnn_ref(node_features, edge_features, attn_W, attn_b, ev_W, ev_b, out1_W, out1_b, out2_W, out2_b, edge_index):
        import jax, jax.numpy as jnp
        import numpy as np
        N_NODES = 3125
        N_EDGES = 20000
        NODE_DIM = 128
        EDGE_DIM = 64
        NUM_HEADS = 4
        EPS = 1e-06

        def _segment_softmax_aggregate(values, scores_mean, dst, num_nodes):
            max_scores = jax.ops.segment_max(scores_mean, dst, num_segments=num_nodes)
            max_scores = jnp.where(jnp.isneginf(max_scores), jnp.zeros_like(max_scores), max_scores)
            exp_scores = jnp.exp(scores_mean - max_scores[dst])
            sum_exp = jax.ops.segment_sum(exp_scores, dst, num_segments=num_nodes)
            attn_weights = exp_scores / (sum_exp[dst] + EPS)
            return jax.ops.segment_sum(values * attn_weights[:, None], dst, num_segments=num_nodes)
        num_nodes = node_features.shape[0]
        dst = edge_index[1]
        h_dst = node_features[dst]
        attn_input = jnp.concatenate([h_dst, edge_features], axis=1)
        attn_scores = attn_input @ attn_W + attn_b
        scores_mean = attn_scores.mean(axis=1)
        edge_values = edge_features @ ev_W + ev_b
        messages = _segment_softmax_aggregate(edge_values, scores_mean, dst, num_nodes)
        update = jax.nn.relu(messages @ out1_W + out1_b) @ out2_W + out2_b
        return node_features + update

    def _L1_gnn_ref(X, edge_index, batch_idx, num_graphs, g_token, Wg_in_w, Wg_in_b, ln1_g, ln1_b, eps, msg_w, msg_b, lin_w, lin_b, ln2_g, ln2_b, Wq, Wk, Wphi, Wy_w, Wy_b, We_w, We_b, ln3_g, ln3_b, ffn_w1, ffn_b1, ffn_w2, ffn_b2):
        import jax, jax.numpy as jnp
        import numpy as np
        N, E, DIM, ATTN, HID, B = (50000, 18750, 128, 64, 256, 64)

        def layernorm(x, g, b):
            m = x.mean(-1, keepdims=True)
            v = x.var(-1, keepdims=True)
            return (x - m) * jax.lax.rsqrt(v + 1e-05) * g + b

        def seg_mean(x, idx, num):
            s = jax.ops.segment_sum(x, idx, num_segments=num)
            c = jax.ops.segment_sum(jnp.ones((x.shape[0], 1), x.dtype), idx, num_segments=num)
            return s / jnp.maximum(c, 1.0)

        def _forward(X, g_token, Wg_in_w, Wg_in_b, ln1_g, ln1_b, eps, msg_w, msg_b, lin_w, lin_b, ln2_g, ln2_b, Wq, Wk, Wphi, Wy_w, Wy_b, We_w, We_b, ln3_g, ln3_b, ffn_w1, ffn_b1, ffn_w2, ffn_b2, edge_index, batch_idx, num_graphs):
            n = X.shape[0]
            src, dst = (edge_index[0], edge_index[1])
            g = g_token + seg_mean(X, batch_idx, num_graphs)
            X = X + (g @ Wg_in_w + Wg_in_b)[batch_idx]
            Xn = layernorm(X, ln1_g, ln1_b)
            msg = (Xn @ msg_w + msg_b)[dst]
            agg = jax.ops.segment_sum(msg, src, num_segments=n)
            X = X + jax.nn.relu(((1.0 + eps) * Xn + agg) @ lin_w + lin_b)
            Xn = layernorm(X, ln2_g, ln2_b)
            e = jnp.tanh((Xn @ Wq)[src] + (Xn @ Wk)[dst])
            scores = e @ Wphi
            exp_s = jnp.exp(scores - scores.max())
            denom = jax.ops.segment_sum(exp_s, src, num_segments=n)
            alpha = exp_s / (denom[src] + 1e-09)
            vmsg = alpha[:, None] * ((Xn @ Wy_w + Wy_b)[dst] + (e @ We_w + We_b))
            X = X + jax.ops.segment_sum(vmsg, src, num_segments=n)
            Xn = layernorm(X, ln3_g, ln3_b)
            return X + jax.nn.relu(Xn @ ffn_w1 + ffn_b1) @ ffn_w2 + ffn_b2
        return _forward(X, g_token, Wg_in_w, Wg_in_b, ln1_g, ln1_b, eps, msg_w, msg_b, lin_w, lin_b, ln2_g, ln2_b, Wq, Wk, Wphi, Wy_w, Wy_b, We_w, We_b, ln3_g, ln3_b, ffn_w1, ffn_b1, ffn_w2, ffn_b2, edge_index, batch_idx, num_graphs)

    def _L2_gnn_ref(node_states, edge_index, edge_rel_emb, W1, b1, W2, b2, Wn, bn, gamma, beta):
        import jax, jax.numpy as jnp
        import numpy as np
        N_NODES = 50000
        N_EDGES = 25000
        HIDDEN = 128
        REL = 64

        def _layer_norm(x, gamma, beta, eps=1e-05):
            mu = jnp.mean(x, axis=-1, keepdims=True)
            var = jnp.mean(jnp.square(x - mu), axis=-1, keepdims=True)
            return (x - mu) * jax.lax.rsqrt(var + eps) * gamma + beta
        src, dst = (edge_index[0], edge_index[1])
        m_input = jnp.concatenate([node_states[src], node_states[dst], edge_rel_emb], axis=-1)
        h = jax.nn.relu(m_input @ W1 + b1)
        messages = jax.nn.relu(h @ W2 + b2)
        agg = jax.ops.segment_sum(messages, dst, num_segments=node_states.shape[0])
        updated = node_states + jax.nn.relu(agg @ Wn + bn)
        return _layer_norm(updated, gamma, beta)

    def _L3_gnn_ref(x, src, dst, w1_self, w1_neigh, b1, w2_self, w2_neigh, b2, w3_self, w3_neigh, b3, bn1_g, bn1_b, bn2_g, bn2_b, ln_g, ln_b):
        import jax, jax.numpy as jnp
        import numpy as np
        N, E, D = (50000, 25000, 128)
        EPS_BN = 1e-05
        EPS_LN = 1e-05

        def _sage_conv(x, src, dst, w_self, w_neigh, b):
            n = x.shape[0]
            msg = x[src]
            agg = jax.ops.segment_sum(msg, dst, num_segments=n)
            deg = jax.ops.segment_sum(jnp.ones((src.shape[0],), x.dtype), dst, num_segments=n)
            h_neigh = agg / jnp.maximum(deg, 1.0)[:, None]
            return x @ w_self + h_neigh @ w_neigh + b

        def _batch_norm(x, gamma, beta):
            mu = jnp.mean(x, axis=0)
            var = jnp.mean(jnp.square(x - mu), axis=0)
            return (x - mu) * jax.lax.rsqrt(var + EPS_BN) * gamma + beta

        def _layer_norm(x, gamma, beta):
            mu = jnp.mean(x, axis=-1, keepdims=True)
            var = jnp.mean(jnp.square(x - mu), axis=-1, keepdims=True)
            return (x - mu) * jax.lax.rsqrt(var + EPS_LN) * gamma + beta
        h = jax.nn.relu(_sage_conv(x, src, dst, w1_self, w1_neigh, b1))
        h = _batch_norm(h, bn1_g, bn1_b)
        h_res = h
        h = jax.nn.relu(_sage_conv(h, src, dst, w2_self, w2_neigh, b2))
        h = h + h_res
        h = _batch_norm(h, bn2_g, bn2_b)
        h = _sage_conv(h, src, dst, w3_self, w3_neigh, b3)
        return _layer_norm(h, ln_g, ln_b)
    edge_index = jnp.stack([src, dst])
    batch0 = jnp.zeros((3125,), jnp.int32)
    x = _layernorm(x + _L0_gnn_ref(x, edge_attr_64, L0_gnn_attn_W, L0_gnn_attn_b, L0_gnn_ev_W, L0_gnn_ev_b, L0_gnn_out1_W, L0_gnn_out1_b, L0_gnn_out2_W, L0_gnn_out2_b, edge_index), axis=-1)
    x = _layernorm(x + _L1_gnn_ref(x, edge_index, batch0, 64, L1_gnn_g_token, L1_gnn_Wg_in_w, L1_gnn_Wg_in_b, L1_gnn_ln1_g, L1_gnn_ln1_b, L1_gnn_eps, L1_gnn_msg_w, L1_gnn_msg_b, L1_gnn_lin_w, L1_gnn_lin_b, L1_gnn_ln2_g, L1_gnn_ln2_b, L1_gnn_Wq, L1_gnn_Wk, L1_gnn_Wphi, L1_gnn_Wy_w, L1_gnn_Wy_b, L1_gnn_We_w, L1_gnn_We_b, L1_gnn_ln3_g, L1_gnn_ln3_b, L1_gnn_ffn_w1, L1_gnn_ffn_b1, L1_gnn_ffn_w2, L1_gnn_ffn_b2), axis=-1)
    x = _layernorm(x + _L2_gnn_ref(x, edge_index, edge_attr_64, L2_gnn_W1, L2_gnn_b1, L2_gnn_W2, L2_gnn_b2, L2_gnn_Wn, L2_gnn_bn, L2_gnn_gamma, L2_gnn_beta), axis=-1)
    x = _layernorm(x + _L3_gnn_ref(x, src, dst, L3_gnn_w1_self, L3_gnn_w1_neigh, L3_gnn_b1, L3_gnn_w2_self, L3_gnn_w2_neigh, L3_gnn_b2, L3_gnn_w3_self, L3_gnn_w3_neigh, L3_gnn_b3, L3_gnn_bn1_g, L3_gnn_bn1_b, L3_gnn_bn2_g, L3_gnn_bn2_b, L3_gnn_ln_g, L3_gnn_ln_b), axis=-1)
    return x

_drawn_inputs = setup_inputs


def setup_inputs(seed=0):
    import zlib

    import numpy as np

    out = dict(_drawn_inputs(seed))
    spreads = {'L1_gnn_Wg_in_b': (0.0, 0.1),
     'L1_gnn_ln1_g': (1.0, 0.2),
     'L1_gnn_ln1_b': (0.0, 0.1),
     'L1_gnn_msg_b': (0.0, 0.1),
     'L1_gnn_lin_b': (0.0, 0.271),
     'L1_gnn_ln2_g': (1.0, 0.2),
     'L1_gnn_ln2_b': (0.0, 0.297),
     'L1_gnn_Wy_b': (0.0, 0.1),
     'L1_gnn_We_b': (0.0, 0.1),
     'L1_gnn_ln3_g': (1.0, 0.2),
     'L1_gnn_ln3_b': (0.0, 0.534),
     'L1_gnn_ffn_b1': (0.0, 0.305),
     'L1_gnn_ffn_b2': (0.0, 0.1),
     'L2_gnn_gamma': (1.0, 0.2),
     'L2_gnn_beta': (0.0, 0.1),
     'L3_gnn_b1': (0.0, 0.1),
     'L3_gnn_b2': (0.0, 0.286),
     'L3_gnn_b3': (0.0, 0.1),
     'L3_gnn_bn1_g': (1.0, 0.2),
     'L3_gnn_bn1_b': (0.0, 0.1),
     'L3_gnn_bn2_g': (1.0, 0.2),
     'L3_gnn_bn2_b': (0.0, 0.1),
     'L3_gnn_ln_g': (1.0, 0.2),
     'L3_gnn_ln_b': (0.0, 0.1)}
    factors = {'L0_gnn_attn_W': 8.0,
     'L0_gnn_attn_b': 8.0,
     'L0_gnn_ev_W': 3.685,
     'L0_gnn_ev_b': 2.673,
     'L1_gnn_Wphi': 8.0,
     'L2_gnn_bn': 2.931}
    for name, (base, spread) in spreads.items():
        noise = np.random.default_rng([zlib.crc32(name.encode()), seed]).standard_normal(out[name].shape)
        drawn = base * np.exp(spread * noise) if base else spread * noise
        out[name] = jnp.asarray(drawn.astype(out[name].dtype))
    for name, factor in factors.items():
        out[name] = (out[name] * factor).astype(out[name].dtype)
    return out
```

```python
from contextlib import ExitStack, contextmanager

import concourse.bass as bass
from concourse import mybir

ALU = mybir.AluOpType
ACT = mybir.ActivationFunctionType
F32 = mybir.dt.float32
BF16 = mybir.dt.bfloat16
I32 = mybir.dt.int32
AX = mybir.AxisListType.X
RMAX = bass.bass_isa.ReduceOp.max
ds = bass.ds

P = 128
N = 3125
E = 100000
D = 128
DE = 64
NB = -(-N // P)
LAST = N - (NB - 1) * P
EP, EC = 125, 800
G = 4
STEP = 2 * G
J = -(-((E + NB * (P - 1)) // P) // STEP) * STEP
LOOPS = J // STEP
RW = DE + 2
BIG = 2.0 ** 100
NCH = 5


class Core:

    def __init__(self, nc, ctx):
        self.nc, self.ctx, self.stage_sems = nc, ctx, []

    def sb(self, name, shape, dt=F32, ctx=None):
        return (ctx or self.ctx).enter_context(self.nc.sbuf_tensor(name, shape, dt))

    def ps(self, name, shape, ctx, dt=F32):
        return ctx.enter_context(self.nc.psum_tensor(name, shape, dt))

    def sem(self, name):
        self.stage_sems.append(self.nc.alloc_semaphore(name))
        return self.stage_sems[-1]

    @contextmanager
    def block(self):
        with self.nc.Block() as block:
            yield block
        self.nc.clear_and_free_semaphores(self.stage_sems)
        self.nc.all_engine_barrier()
        self.stage_sems = []


def wide(ap, n, shape):
    return ap.unsqueeze(2).to_broadcast(shape)


def over_blocks(ap, shape):
    return ap.unsqueeze(1).to_broadcast(shape)


def steps(eng, count, body):
    body(0, True)
    with eng.Fori(1, count) as i:
        body(i, False)



def load_stage(k, a):
    nc = k.nc
    k.iota_row = k.sb("iota_row", [P, P])
    k.iota_tile = k.sb("iota_tile", [P, J])
    k.iota_col = k.sb("iota_col", [P, 1])
    k.ident = k.sb("ident", [P, P])
    k.ident_h = k.sb("ident_h", [P, P], BF16)
    k.ones = k.sb("ones", [P, P])
    k.ones_h = k.sb("ones_h", [P, P], BF16)
    k.before = k.sb("before", [P, P])
    k.before_h = k.sb("before_h", [P, P], BF16)
    k.last_rows = k.sb("last_rows", [P, 1])
    k.X = k.sb("X", [P, NB, D])
    k.att = k.sb("att", [P, D + DE, 4])
    k.att_b = k.sb("att_b", [P, 4])
    k.att_m = k.sb("att_m", [P, D + DE])
    k.att_bm = k.sb("att_bm", [P, 1])
    w = {}

    def weight(name, rows, cols):
        w[name] = k.sb("w_" + name, [rows, cols])
        return w[name]

    loads = []
    weight("ev", DE + 1, D)
    loads += [(w["ev"][0:DE, :], a["L0_gnn_ev_W"]), (w["ev"][DE:DE + 1, :], a["L0_gnn_ev_b"].unsqueeze(0))]
    weight("We", DE + 1, D)
    loads += [(w["We"][0:DE, :], a["L1_gnn_We_w"]), (w["We"][DE:DE + 1, :], a["L1_gnn_We_b"].unsqueeze(0))]
    for n, s in (("out1", "L0_gnn_out1_W"), ("out2", "L0_gnn_out2_W"), ("Wg", "L1_gnn_Wg_in_w"),
                 ("msg", "L1_gnn_msg_w"), ("lin", "L1_gnn_lin_w"), ("W2", "L2_gnn_W2"), ("Wn", "L2_gnn_Wn"),
                 ("s1", "L3_gnn_w1_self"), ("n1", "L3_gnn_w1_neigh"), ("s2", "L3_gnn_w2_self"),
                 ("n2", "L3_gnn_w2_neigh"), ("s3", "L3_gnn_w3_self"), ("n3", "L3_gnn_w3_neigh")):
        loads.append((weight(n, P, D)[:], a[s]))
    weight("qky", P, 2 * D)
    loads += [(w["qky"][:, 0:64], a["L1_gnn_Wq"]), (w["qky"][:, 64:128], a["L1_gnn_Wk"]),
              (w["qky"][:, 128:256], a["L1_gnn_Wy_w"])]
    loads.append((weight("ffn1", P, 2 * D)[:], a["L1_gnn_ffn_w1"]))
    weight("ffn2", P, 2 * D)
    loads += [(w["ffn2"][:, 0:D], a["L1_gnn_ffn_w2"][0:P, :]), (w["ffn2"][:, D:2 * D], a["L1_gnn_ffn_w2"][P:2 * P, :])]
    weight("W1ab", P, 2 * D)
    loads += [(w["W1ab"][:, 0:D], a["L2_gnn_W1"][0:P, :]), (w["W1ab"][:, D:2 * D], a["L2_gnn_W1"][P:2 * P, :])]
    loads.append((weight("W1c", DE, D)[:], a["L2_gnn_W1"][2 * P:2 * P + DE, :]))
    k.gtok = k.sb("gtok", [P, 1])
    loads.append((k.gtok[:], a["L1_gnn_g_token"].rearrange("a d -> d a")))
    k.w = w

    rows = {"out1": "L0_gnn_out1_b", "out2": "L0_gnn_out2_b", "Wg": "L1_gnn_Wg_in_b", "ln1g": "L1_gnn_ln1_g",
            "ln1b": "L1_gnn_ln1_b", "msg": "L1_gnn_msg_b", "lin": "L1_gnn_lin_b", "ln2g": "L1_gnn_ln2_g",
            "ln2b": "L1_gnn_ln2_b", "phi": "L1_gnn_Wphi", "ln3g": "L1_gnn_ln3_g", "ln3b": "L1_gnn_ln3_b",
            "ffn1": "L1_gnn_ffn_b1", "ffn2": "L1_gnn_ffn_b2", "b2": "L2_gnn_b2", "bn": "L2_gnn_bn",
            "gamma": "L2_gnn_gamma", "beta": "L2_gnn_beta", "s1": "L3_gnn_b1", "s2": "L3_gnn_b2",
            "s3": "L3_gnn_b3", "bn1g": "L3_gnn_bn1_g", "bn1b": "L3_gnn_bn1_b", "bn2g": "L3_gnn_bn2_g",
            "bn2b": "L3_gnn_bn2_b", "lng": "L3_gnn_ln_g", "lnb": "L3_gnn_ln_b"}
    k.r = {}
    for n, s in rows.items():
        k.r[n] = k.sb("r_" + n, [P, a[s].shape[0]])
        loads.append((k.r[n][:], a[s].partition_broadcast(P)))
    k.r["ab"] = k.sb("r_ab", [P, 2 * D])
    k.r["qky"] = k.sb("r_qky", [P, 2 * D])
    k.r["none"] = k.sb("r_none", [P, D])
    loads.append((k.r["ab"][:, 0:D], a["L2_gnn_b1"].partition_broadcast(P)))
    loads.append((k.r["qky"][:, D:2 * D], a["L1_gnn_Wy_b"].partition_broadcast(P)))
    k.eps = k.sb("eps", [P, 1])
    loads.append((k.eps[:], a["L1_gnn_eps"].partition_broadcast(P)))
    loads.append((k.att[:], a["L0_gnn_attn_W"].partition_broadcast(P)))
    loads.append((k.att_b[:], a["L0_gnn_attn_b"].partition_broadcast(P)))
    loads.append((k.X[:, 0:NB - 1, :], a["x"][0:(NB - 1) * P, :].rearrange("(b p) f -> p b f", p=P)))

    k.tile_max = k.sb("tile_max", [P, J])
    k.tile_deg = k.sb("tile_deg", [P, J])
    cleared, loaded, iotas, made = (k.sem(s) for s in ("cleared", "loaded", "iotas", "made"))
    k.pad_meta = k.sb("pad_meta", [P, 64, 2])
    ic = k.sb("iota_i", [P, P], I32)
    with k.block() as block:
        @block.sync
        def _(sp):
            for dst, src in loads:
                sp.dma_start(dst, src).then_inc(loaded, 16)
            sp.wait_ge(cleared, 1)
            sp.dma_start(k.X[0:LAST, NB - 1, :], a["x"][(NB - 1) * P:N, :]).then_inc(loaded, 16)
            sp.wait_ge(loaded, 16 * (len(loads) + 1))

        @block.gpsimd
        def _(pool):
            nc.gpsimd.iota(k.iota_row[:], [[1, P]], base=0, channel_multiplier=0,
                           allow_small_or_imprecise_dtypes=True).then_inc(iotas, 1)
            nc.gpsimd.iota(k.iota_tile[:], [[1, J]], base=0, channel_multiplier=0,
                           allow_small_or_imprecise_dtypes=True).then_inc(iotas, 1)
            nc.gpsimd.iota(k.iota_col[:], [[1, 1]], base=0, channel_multiplier=1,
                           allow_small_or_imprecise_dtypes=True).then_inc(iotas, 1)

        @block.vector
        def _(dve):
            dve.memset(k.X[:, NB - 1, :], 0.0).then_inc(cleared, 1)
            dve.memset(k.ones[:], 1.0)
            dve.memset(k.ones_h[:], 1.0)
            dve.memset(k.r["ab"][:, D:2 * D], 0.0)
            dve.memset(k.r["qky"][:, 0:D], 0.0)
            dve.memset(k.r["none"][:], 0.0)
            dve.memset(k.pad_meta[:, :, 0:1], -1.0)
            dve.memset(k.pad_meta[:, :, 1:2], 0.0)
            dve.wait_ge(iotas, 3)
            dve.tensor_scalar(k.ident[:], k.iota_row[:], k.iota_col[:], None, ALU.is_equal)
            dve.tensor_scalar(k.ident_h[:], k.iota_row[:], k.iota_col[:], None, ALU.is_equal)
            dve.tensor_scalar(k.before[:], k.iota_row[:], k.iota_col[:], None, ALU.is_gt)
            dve.tensor_scalar(k.before_h[:], k.iota_row[:], k.iota_col[:], None, ALU.is_gt)
            dve.tensor_scalar(k.last_rows[:], k.iota_col[:], float(LAST), None, ALU.is_lt)
            dve.wait_ge(loaded, 16 * (len(loads) + 1))
            dve.tensor_reduce(k.att_m[:], k.att[:], AX, ALU.add).then_inc(made, 1)
            dve.tensor_reduce(k.att_bm[:], k.att_b[:], AX, ALU.add).then_inc(made, 1)
            dve.wait_ge(made, 2)
            dve.tensor_scalar(k.att_m[:], k.att_m[:], 0.25, None, ALU.mult)
            dve.tensor_scalar(k.att_bm[:], k.att_bm[:], 0.25, None, ALU.mult)



def order_stage(k, o, key_i, other_i):
    nc, n = k.nc, o.name
    keys_in, blocks, mask1, tot, mask2, placed, step, tot_free, masks_used, sums_used, base = (
        k.sem(f"{n}_{s}") for s in ("keys_in", "blocks", "mask1", "totals", "mask2", "placed", "step",
                                    "tot_free", "masks_used", "sums_used", "base"))
    H = EC // 2
    JH = J // 2
    with ExitStack() as c:
        ki = k.sb(n + "_ki", [EP, EC], I32, c)
        oi = k.sb(n + "_oi", [EP, EC], I32, c)
        bi = k.sb(n + "_bi", [EP, EC], I32, c)
        bf = k.sb(n + "_bf", [EP, EC], F32, c)
        mask = k.sb(n + "_mask", [EP, 2, EC], BF16, c)
        pick = k.sb(n + "_pick", [EP, 2 * NB - 1], BF16, c)
        totals = k.sb(n + "_totals", [NB, EC], F32, c)
        upto = k.sb(n + "_upto", [NB, EC], F32, c)
        first = k.sb(n + "_first", [NB, EC], F32, c)
        onesr = k.sb(n + "_onesr", [NB, EC], F32, c)
        tiles_i = k.sb(n + "_tiles_i", [NB, 1], I32, c)
        tiles = k.sb(n + "_tiles", [NB, 1], F32, c)
        start = k.sb(n + "_start", [NB, 2], F32, c)
        past = k.sb(n + "_past", [NB, J], BF16, c)
        rank = k.sb(n + "_rank", [EP, EC], F32, c)
        part = k.sb(n + "_part", [EP, EC], F32, c)
        low = k.sb(n + "_low", [EP, EC], I32, c)
        pt = k.ps(n + "_pt", [P, 2, 512], c)
        pr = k.ps(n + "_pr", [P, 2, 2, 512], c)
        pb = k.ps(n + "_pb", [P, 2, 512], c)
        with k.block() as block:
            @block.sync
            def _(sp):
                sp.dma_start(ki[:], key_i.rearrange("(p c) -> p c", p=EP)).then_inc(keys_in, 16)
                sp.dma_start(oi[:], other_i.rearrange("(p c) -> p c", p=EP)).then_inc(keys_in, 16)
                sp.wait_ge(keys_in, 32)

            @block.tensor
            def _(pe):
                for b in range(NB):
                    pe.wait_ge(mask1, b + 1)
                    for h in range(2):
                        mm = pe.matmul(pt[0:NB, h, 0:H], pick[:, NB - 1 - b:2 * NB - 1 - b],
                                       mask[:, b % 2, h * H:(h + 1) * H], start=(b == 0), stop=(b == NB - 1))
                    mm.then_inc(masks_used, 1)
                pe.wait_ge(blocks, 1)
                pe.matmul(pb[0:NB, 0, 0:1], k.before[0:NB, 0:NB], tiles[:], start=True, stop=True).then_inc(base, 1)
                pe.wait_ge(blocks, 2)
                for h in range(2):
                    mm = pe.matmul(pb[:, h, 0:JH], k.ones_h[0:NB, :], past[:, h * JH:(h + 1) * JH],
                                   start=True, stop=True)
                mm.then_inc(base, 1)
                for b in range(NB):
                    pe.wait_ge(mask2, b + 1)
                    if b >= 2:
                        pe.wait_ge(sums_used, b - 1)
                    for h in range(2):
                        pe.matmul(pr[0:EP, b % 2, h, 0:H], k.before_h[0:EP, 0:EP],
                                  mask[:, b % 2, h * H:(h + 1) * H], start=True, stop=False)
                        mm = pe.matmul(pr[0:EP, b % 2, h, 0:H], k.ident[0:NB, b:b + 1].to_broadcast([NB, EP]),
                                       first[:, h * H:(h + 1) * H], start=False, stop=True)
                    mm.then_inc(placed, 1)

            @block.vector
            def _(dve):
                done = [0]

                def link(ins):
                    done[0] += 1
                    ins.then_inc(step, 1)
                    dve.wait_ge(step, done[0])

                dve.memset(pick[:], 0.0)
                dve.memset(rank[:], 0.0)
                link(dve.memset(onesr[:], 1.0))
                link(dve.memset(pick[:, NB - 1:NB], 1.0))
                dve.wait_ge(keys_in, 32)
                link(dve.tensor_scalar(bi[:], ki[:], 7, None, ALU.arith_shift_right))
                link(dve.tensor_scalar(low[:], ki[:], P - 1, None, ALU.bitwise_and))
                link(dve.tensor_copy(bf[:], bi[:]))
                dve.tensor_copy(o.meta[:, :, 0], low[:])
                dve.tensor_copy(o.meta[:, :, 1], oi[:])
                for b in range(NB):
                    if b >= 2:
                        dve.wait_ge(masks_used, b - 1)
                    dve.tensor_scalar(mask[:, b % 2, :], bf[:], float(b), None, ALU.is_equal).then_inc(mask1, 1)
                dve.wait_ge(masks_used, NB)
                link(dve.tensor_copy(totals[:].rearrange("b (h c) -> b h c", h=2), pt[0:NB, :, 0:H]))
                link(dve.tensor_tensor_scan(upto[:], onesr[:], totals[:], 0.0, ALU.mult, ALU.add))
                link(dve.tensor_tensor(first[:], upto[:], totals[:], ALU.subtract))
                link(dve.tensor_scalar(tiles[:], upto[:, EC - 1:EC], float(P - 1), None, ALU.add))
                link(dve.tensor_copy(tiles_i[:], tiles[:]))
                link(dve.tensor_scalar(tiles_i[:], tiles_i[:], 7, None, ALU.arith_shift_right))
                dve.tensor_copy(tiles[:], tiles_i[:]).then_inc(blocks, 1)
                dve.wait_ge(base, 1)
                link(dve.tensor_copy(start[:, 0:1], pb[0:NB, 0, 0:1]))
                link(dve.tensor_tensor(start[:, 1:2], start[:, 0:1], tiles[:], ALU.add))
                dve.tensor_scalar(past[:], k.iota_tile[0:NB, :], start[:, 1:2], None, ALU.is_ge).then_inc(blocks, 1)
                link(dve.tensor_scalar(start[:, 0:1], start[:, 0:1], float(P), None, ALU.mult))
                link(dve.tensor_scalar(first[:], first[:], start[:, 0:1], None, ALU.add))
                dve.wait_ge(base, 2)
                link(dve.tensor_scalar(o.block_f[:].rearrange("p (h j) -> p h j", h=2), pb[:, :, 0:JH],
                                       float(NB - 1), None, ALU.min))
                dve.tensor_copy(o.block_i[:], o.block_f[:])

                def make_mask(b):
                    if b >= 2:
                        dve.wait_ge(placed, b - 1)
                    dve.tensor_scalar(mask[:, b % 2, :], bf[:], float(b), None, ALU.is_equal).then_inc(mask2, 1)

                make_mask(0)
                for b in range(NB):
                    if b + 1 < NB:
                        make_mask(b + 1)
                    dve.wait_ge(placed, b + 1)
                    dve.wait_ge(mask2, b + 1)
                    ins = dve.tensor_tensor(part[:].rearrange("p (h c) -> p h c", h=2), pr[0:EP, b % 2, :, 0:H],
                                            mask[:, b % 2, :].rearrange("p (h c) -> p h c", h=2), ALU.mult)
                    ins.then_inc(sums_used, 1)
                    dve.wait_ge(sums_used, b + 1)
                    link(dve.tensor_tensor(rank[:], rank[:], part[:], ALU.add))
                link(dve.tensor_copy(bi[:], rank[:]))
                link(dve.tensor_scalar(low[:], bi[:], P - 1, None, ALU.bitwise_and))
                link(dve.tensor_scalar(bi[:], bi[:], 7, None, ALU.arith_shift_right))
                link(dve.tensor_scalar(low[:], low[:], J, None, ALU.mult))
                dve.tensor_tensor(o.row[:], low[:], bi[:], ALU.add)


def scatter_features_stage(k, o, edge_attr):
    nc = k.nc
    CW = 8
    FB = 8
    attr = edge_attr.rearrange("(p c) f -> p c f", p=EP)
    blank_made, blanked, staged, begun = (k.sem(s) for s in ("f_blank_made", "f_blanked", "f_staged", "f_begun"))
    features_in = [k.sem(f"f_features_in{p}") for p in range(2)]
    sent = [k.sem(f"f_sent{p}") for p in range(2)]
    with ExitStack() as c:
        blank = k.sb("f_blank", [P, FB, RW], F32, c)
        rows = k.sb("f_rows", [EP, 2, CW, RW], F32, c)
        at = k.sb("f_at", [EP, 2, CW], I32, c)
        with k.block() as block:
            @block.sync
            def _(sp):
                sp.wait_ge(blank_made, 3)
                sp.dma_start(o.rows_dram.rearrange("(p r j) w -> p r (j w)", p=P, j=FB),
                             blank[:].rearrange("p j w -> p (j w)").unsqueeze(1).to_broadcast([P, J // FB, FB * RW])
                             ).then_inc(blanked, 16)

                def body(i, first):
                    for p in range(2):
                        if not first:
                            sp.wait_ge(sent[p], 16 * CW * i)
                        sp.dma_start(rows[:, p, :, 0:DE], attr[:, ds(i * 2 * CW + p * CW, CW), :]
                                     ).then_inc(features_in[p], 16)
                steps(sp, EC // (2 * CW), body)

            @block.scalar
            def _(act):
                def body(i, first):
                    for p in range(2):
                        if not first:
                            act.wait_ge(sent[p], 16 * CW * i)
                        c0 = i * 2 * CW + p * CW
                        nc.scalar.copy(at[:, p, :], o.row[:, ds(c0, CW)]).then_inc(staged, 1)
                        nc.scalar.copy(rows[:, p, :, DE:RW], o.meta[:, ds(c0, CW), :]).then_inc(staged, 1)
                steps(act, EC // (2 * CW), body)

            @block.vector
            def _(dve):
                dve.memset(blank[:, :, 0:DE], 0.0).then_inc(blank_made, 1)
                dve.memset(blank[:, :, DE:DE + 1], -1.0).then_inc(blank_made, 1)
                dve.memset(blank[:, :, DE + 1:RW], 0.0).then_inc(blank_made, 1)

            @block.gpsimd
            def _(pool):
                pool.wait_ge(blanked, 16)

                def body(i, first):
                    for p in range(2):
                        pool.wait_ge(features_in[p], 16 * (i + 1))
                        pool.wait_ge(staged, 4 * i + 2 * p + 2)
                        pool.sem_inc(begun, 1)
                        for q in range(CW):
                            pool.indirect_dma_start(
                                o.rows_dram, bass.IndirectOffsetOnAxis(ap=at[:, p, q:q + 1], axis=0),
                                rows[:, p, q, :], None).then_inc(sent[p], 16)
                steps(pool, EC // (2 * CW), body)
                for p in range(2):
                    pool.wait_ge(sent[p], 16 * EC // 2)



def score_stage(k, o, so):
    nc = k.nc
    CW = 8
    (blanked, index_staged, copied, features_in0, features_in1, scored, spread, penalties, sums, meta_kept,
     rows_done, maxima) = (k.sem("sc_" + s) for s in (
         "blanked", "index_staged", "copied", "features_in0", "features_in1", "scored", "spread", "penalties",
         "sums", "meta_kept", "rows_done", "maxima"))
    sent = [k.sem(f"sc_sent{p}") for p in range(2)]
    features_in = [features_in0, features_in1]
    rows_dram = o.rows_dram.rearrange("(e j) w -> e j w", e=P)
    with ExitStack() as c:
        at = k.sb("sc_at", [EP, 2, CW], I32, c)
        ids = k.sb("sc_ids", [EP, 2, CW, 2], F32, c)
        rows = k.sb("sc_rows", [P, 2, G, RW], F32, c)
        prod = k.sb("sc_prod", [P, 2, G, DE], F32, c)
        sg = k.sb("sc_sg", [P, 2, G], F32, c)
        lo = k.sb("sc_lo", [P, 2, G], BF16, c)
        pen = k.sb("sc_pen", [P, 2, G, P], F32, c)
        tmp = k.sb("sc_tmp", [P, 2, G, P], F32, c)
        node_bc = k.ps("sc_node", [P, 2, 512], c)
        score_bc = k.ps("sc_score", [P, 2, 512], c)
        with k.block() as block:
            @block.sync
            def _(sp):
                sp.dma_start(so.ids_dram.rearrange("(p r j) w -> p r (j w)", p=P, j=8),
                             k.pad_meta[:, 0:8, :].rearrange("p j w -> p (j w)").unsqueeze(1)
                             .to_broadcast([P, J // 8, 16])).then_inc(blanked, 16)

                def body(i, first):
                    for p in range(2):
                        if not first:
                            sp.wait_ge(scored, 4 * i + 2 * p - 2)
                            sp.wait_ge(meta_kept, 4 * i + 2 * p - 2)
                        sp.dma_start(rows[:, p], rows_dram[:, ds(i * STEP + p * G, G), :]).then_inc(features_in[p], 16)
                steps(sp, LOOPS, body)

            @block.gpsimd
            def _(pool):
                pool.wait_ge(blanked, 16)

                def body(i, first):
                    for p in range(2):
                        if not first:
                            pool.wait_ge(sent[p], 16 * CW * i)
                        c0 = i * 2 * CW + p * CW
                        nc.gpsimd.tensor_copy(at[:, p, :], so.row[:, ds(c0, CW)]).then_inc(index_staged, 1)
                        nc.gpsimd.tensor_copy(ids[:, p], so.meta[:, ds(c0, CW), :]).then_inc(index_staged, 1)
                        pool.wait_ge(index_staged, 4 * i + 2 * p + 2)
                        pool.sem_inc(copied, 1)
                        for q in range(CW):
                            pool.indirect_dma_start(
                                so.ids_dram, bass.IndirectOffsetOnAxis(ap=at[:, p, q:q + 1], axis=0),
                                ids[:, p, q, :], None).then_inc(sent[p], 16)
                steps(pool, EC // (2 * CW), body)
                for p in range(2):
                    pool.wait_ge(sent[p], 16 * EC // 2)

            @block.tensor
            def _(pe):
                def body(i, first):
                    for p in range(2):
                        pe.wait_ge(scored, 4 * i + 2 * p + 2)
                        if not first:
                            pe.wait_ge(sums, 2 * i + p - 1)
                            pe.wait_ge(penalties, 2 * i + p - 1)
                        for g in range(G):
                            pe.matmul(node_bc[:, p, g * P:(g + 1) * P], lo[:, p, g:g + 1].to_broadcast([P, P]),
                                      k.ident_h[:], start=True, stop=True)
                            mm = pe.matmul(score_bc[:, p, g * P:(g + 1) * P], sg[:, p, g:g + 1].to_broadcast([P, P]),
                                           k.ident[:], start=True, stop=True)
                        mm.then_inc(spread, 1)
                steps(pe, LOOPS, body)

            @block.scalar
            def _(act):
                def body(i, first):
                    for p in range(2):
                        act.wait_ge(features_in[p], 16 * (i + 1))
                        nc.scalar.copy(o.slot[:, ds(i * STEP + p * G, G), :], rows[:, p, :, DE:RW]).then_inc(meta_kept, 1)
                        act.wait_ge(scored, 4 * i + 2 * p + 2)
                        nc.scalar.copy(k.scores[:, ds(i * STEP + p * G, G)], sg[:, p, :]).then_inc(meta_kept, 1)
                steps(act, LOOPS, body)

            @block.vector
            def _(dve):
                w2 = k.att_m[:, D:D + DE].unsqueeze(1).to_broadcast([P, G, DE])

                def body(i, first):
                    for p in range(2):
                        dve.wait_ge(features_in[p], 16 * (i + 1))
                        dve.tensor_tensor(prod[:, p], rows[:, p, :, 0:DE], w2, ALU.mult).then_inc(rows_done, 1)
                        if not first:
                            dve.wait_ge(spread, 2 * i + p - 1)
                            dve.wait_ge(meta_kept, 4 * i + 2 * p - 2)
                        dve.tensor_copy(lo[:, p], rows[:, p, :, DE]).then_inc(scored, 1)
                        dve.wait_ge(rows_done, 2 * i + p + 1)
                        dve.tensor_reduce(sg[:, p], prod[:, p], AX, ALU.add).then_inc(scored, 1)
                    for p in range(2):
                        dve.wait_ge(spread, 2 * i + p + 1)
                        dve.tensor_scalar(pen[:, p], node_bc[:, p].rearrange("p (g e) -> p g e", g=G), k.iota_col[:], -BIG,
                                          ALU.not_equal, ALU.mult).then_inc(penalties, 1)
                        dve.wait_ge(penalties, 2 * i + p + 1)
                        dve.tensor_tensor(tmp[:, p], score_bc[:, p].rearrange("p (g e) -> p g e", g=G), pen[:, p], ALU.add).then_inc(sums, 1)
                        dve.tensor_reduce(k.tile_deg[:, ds(i * STEP + p * G, G)], pen[:, p], AX, ALU.add).then_inc(maxima, 1)
                        dve.wait_ge(sums, 2 * i + p + 1)
                        dve.tensor_reduce(k.tile_max[:, ds(i * STEP + p * G, G)], tmp[:, p], AX, ALU.max).then_inc(maxima, 1)
                steps(dve, LOOPS, body)


def node_maximum_stage(k, o, so):
    nc = k.nc
    slots_in, sel, part, step, node = (k.sem("nm_" + s) for s in ("slots_in", "sel", "part", "step", "node"))
    with ExitStack() as c:
        one = k.sb("nm_one", [P, J], F32, c)
        two = k.sb("nm_two", [P, J], F32, c)
        prod = k.sb("nm_prod", [P, NB, D], F32, c)
        mt = k.sb("nm_mt", [P, NB], F32, c)
        with k.block() as block:
            @block.sync
            def _(sp):
                sp.dma_start(so.slot[:], so.ids_dram.rearrange("(e j) w -> e j w", e=P)).then_inc(slots_in, 16)
                sp.wait_ge(slots_in, 16)

            @block.vector
            def _(dve):
                n = [0]

                def link(ins):
                    n[0] += 1
                    ins.then_inc(step, 1)
                    dve.wait_ge(step, n[0])

                link(dve.tensor_scalar(k.tile_deg[:], k.tile_deg[:], 1.0 / BIG, float(P), ALU.mult, ALU.add))
                link(dve.tensor_tensor(prod[:], k.X[:], over_blocks(k.att_m[:, 0:D], [P, NB, D]), ALU.mult))
                link(dve.tensor_reduce(mt[:], prod[:], AX, ALU.add))
                link(dve.tensor_scalar(k.mx[:, :, 1], mt[:], k.att_bm[:], None, ALU.add))
                with dve.Fori(0, NB) as b:
                    dve.tensor_scalar(one[:], o.block_f[:], k.iota_row[:, ds(b, 1)], -BIG, ALU.not_equal, ALU.mult
                                      ).then_inc(sel, 1)
                    dve.wait_ge(sel, 4 * b + 1)
                    dve.tensor_tensor(two[:], one[:], k.tile_max[:], ALU.add).then_inc(sel, 1)
                    dve.wait_ge(sel, 4 * b + 2)
                    dve.tensor_reduce(mt[:, ds(b, 1)], two[:], AX, ALU.max).then_inc(part, 1)
                    dve.scalar_tensor_tensor(one[:], o.block_f[:], k.iota_row[:, ds(b, 1)], k.tile_deg[:],
                                             ALU.is_equal, ALU.mult).then_inc(sel, 1)
                    dve.wait_ge(sel, 4 * b + 3)
                    dve.tensor_reduce(k.deg[:, ds(b, 1)], one[:], AX, ALU.add).then_inc(sel, 1)
                    dve.wait_ge(sel, 4 * b + 4)
                dve.wait_ge(part, NB)
                link(dve.tensor_tensor(k.mx[:, :, 0], mt[:], k.mx[:, :, 1], ALU.add))
                link(dve.tensor_scalar(k.deg[:], k.deg[:], 1.0, None, ALU.max))
                dve.reciprocal(k.deg[:], k.deg[:]).then_inc(node, 1)
                dve.wait_ge(node, 1)


def attention_sum_stage(k, o, acc):
    nc = k.nc
    (cleared, nodes_taken, spread, onehots, looked_up, exponents, weights, weighted, summed, added, ones_put,
     diff) = (k.sem("as_" + s) for s in ("cleared", "nodes_taken", "spread", "onehots", "looked_up", "exponents",
                                         "weights", "weighted", "summed", "added", "ones_put", "diff"))
    features_in = [k.sem(f"as_features_in{p}") for p in range(2)]
    rows_dram = o.rows_dram.rearrange("(e j) w -> e j w", e=P)
    with ExitStack() as c:
        rows = k.sb("as_rows", [P, 2, G, RW], F32, c)
        lo = k.sb("as_lo", [P, 2, G], BF16, c)
        sg = k.sb("as_sg", [P, 2, G], F32, c)
        oht = k.sb("as_oht", [P, 2, G, P], F32, c)
        ohw = k.sb("as_ohw", [P, 2, G, P], F32, c)
        d1 = k.sb("as_d1", [P, 2, G], F32, c)
        d2 = k.sb("as_d2", [P, 2, G], F32, c)
        wt = k.sb("as_wt", [P, 2, G], F32, c)
        node_bc = k.ps("as_node", [P, 2, 512], c)
        found = k.ps("as_found", [P, 2, 512], c)
        sums = k.ps("as_sums", [P, 2, 512], c)
        with k.block() as block:
            @block.sync
            def _(sp):
                def body(i, first):
                    for p in range(2):
                        if not first:
                            sp.wait_ge(summed, 2 * i + p - 1)
                            sp.wait_ge(weighted, 2 * i + p - 1)
                        sp.dma_start(rows[:, p], rows_dram[:, ds(i * STEP + p * G, G), :]).then_inc(features_in[p], 16)
                steps(sp, LOOPS, body)

            @block.tensor
            def _(pe):
                def body(i, first):
                    for p in range(2):
                        pe.wait_ge(nodes_taken, 4 * i + 2 * p + 2)
                        if not first:
                            pe.wait_ge(onehots, 2 * i + p - 1)
                        for g in range(G):
                            mm = pe.matmul(node_bc[:, p, g * P:(g + 1) * P], lo[:, p, g:g + 1].to_broadcast([P, P]),
                                           k.ident_h[:], start=True, stop=True)
                        mm.then_inc(spread, 1)
                    for p in range(2):
                        pe.wait_ge(onehots, 2 * i + p + 1)
                        if not first:
                            pe.wait_ge(exponents, 2 * i + p - 1)
                        for g in range(G):
                            b = pe.value_load(o.block_i[0:1, ds(i * STEP + p * G + g, 1)], min_val=0, max_val=NB - 1)
                            mm = pe.matmul(found[:, p, 2 * g:2 * g + 2], oht[:, p, g, :], k.mx[:, ds(b, 1), :],
                                           start=True, stop=True)
                        mm.then_inc(looked_up, 1)
                    for p in range(2):
                        pe.wait_ge(weighted, 2 * i + p + 1)
                        pe.wait_ge(ones_put, 2 * i + p + 1)
                        if not first:
                            pe.wait_ge(added, (2 * i + p - 1) * G)
                        for g in range(G):
                            mm = pe.matmul(sums[:, p, g * RW:(g + 1) * RW], ohw[:, p, g, :], rows[:, p, g, :],
                                           start=True, stop=True)
                        mm.then_inc(summed, 1)
                steps(pe, LOOPS, body)

            @block.scalar
            def _(act):
                def body(i, first):
                    for p in range(2):
                        act.wait_ge(features_in[p], 16 * (i + 1))
                        if not first:
                            act.wait_ge(spread, 2 * i + p - 1)
                            act.wait_ge(diff, 2 * i + p - 1)
                        nc.scalar.copy(lo[:, p], rows[:, p, :, DE]).then_inc(nodes_taken, 1)
                        nc.scalar.copy(sg[:, p], k.scores[:, ds(i * STEP + p * G, G)]).then_inc(nodes_taken, 1)
                    for p in range(2):
                        act.wait_ge(exponents, 2 * i + p + 1)
                        if not first:
                            act.wait_ge(weighted, 2 * i + p - 1)
                        nc.scalar.activation(wt[:, p], d2[:, p], ACT.Exp).then_inc(weights, 1)
                steps(act, LOOPS, body)

            @block.vector
            def _(dve):
                dve.memset(acc[:], 0.0).then_inc(cleared, 1)
                dve.wait_ge(cleared, 1)

                def body(i, first):
                    for p in range(2):
                        dve.wait_ge(spread, 2 * i + p + 1)
                        if not first:
                            dve.wait_ge(looked_up, 2 * i + p - 1)
                        dve.tensor_scalar(oht[:, p], node_bc[:, p].rearrange("p (g e) -> p g e", g=G), k.iota_col[:],
                                          None, ALU.is_equal).then_inc(onehots, 1)
                    for p in range(2):
                        f = found[:, p, 0:2 * G].rearrange("p (g t) -> p g t", t=2)
                        dve.wait_ge(looked_up, 2 * i + p + 1)
                        dve.wait_ge(nodes_taken, 4 * i + 2 * p + 2)
                        dve.tensor_tensor(d1[:, p], sg[:, p], f[:, :, 1], ALU.add).then_inc(diff, 1)
                        dve.wait_ge(diff, 2 * i + p + 1)
                        if not first:
                            dve.wait_ge(weights, 2 * i + p - 1)
                        dve.tensor_tensor(d2[:, p], d1[:, p], f[:, :, 0], ALU.subtract).then_inc(exponents, 1)
                    for p in range(2):
                        dve.wait_ge(weights, 2 * i + p + 1)
                        if not first:
                            dve.wait_ge(summed, 2 * i + p - 1)
                        for g in range(G):
                            ins = dve.tensor_scalar(ohw[:, p, g, :], k.iota_row[:], rows[:, p, g, DE:DE + 1],
                                                    wt[:, p, g:g + 1], ALU.is_equal, ALU.mult)
                        ins.then_inc(weighted, 1)
                        dve.memset(rows[:, p, :, DE + 1:RW], 1.0).then_inc(ones_put, 1)
                    for p in range(2):
                        dve.wait_ge(summed, 2 * i + p + 1)
                        for g in range(G):
                            n = (2 * i + p) * G + g
                            b = dve.value_load(o.block_i[0:1, ds(n, 1)], min_val=0, max_val=NB - 1)
                            if g or not first or p:
                                dve.wait_ge(added, n)
                            dve.tensor_tensor(acc[:, ds(b, 1), :], acc[:, ds(b, 1), :],
                                              sums[:, p, g * RW:(g + 1) * RW].unsqueeze(1), ALU.add).then_inc(added, 1)
                steps(dve, LOOPS, body)



def far_ends_stage(k, orders):
    with k.block() as block:
        @block.vector
        def _(dve):
            for o in orders:
                dve.tensor_copy(o.far_i[:], o.slot[:, :, 1])


def gather_sum_stage(k, name, o, table, acc):
    nc = k.nc
    cleared, staged, onehots, summed, added = (k.sem(f"{name}_{s}") for s in (
        "cleared", "staged", "onehots", "summed", "added"))
    begun = k.sem(f"{name}_begun")
    rows_in = [k.sem(f"{name}_rows_in{p}") for p in range(2)]
    with ExitStack() as c:
        rows = k.sb(name + "_rows", [P, 2, G, D], F32, c)
        far = k.sb(name + "_far", [P, 2, G], I32, c)
        oh = k.sb(name + "_oh", [P, 2, G, P], F32, c)
        sums = k.ps(name + "_sums", [P, 2, 512], c)
        with k.block() as block:
            @block.scalar
            def _(act):
                def body(i, first):
                    for p in range(2):
                        if not first:
                            act.wait_ge(rows_in[p], 16 * G * i)
                        nc.scalar.copy(far[:, p], o.far_i[:, ds(i * STEP + p * G, G)]).then_inc(staged, 1)
                steps(act, LOOPS, body)

            @block.gpsimd
            def _(pool):
                def body(i, first):
                    for p in range(2):
                        pool.wait_ge(staged, 2 * i + p + 1)
                        if not first:
                            pool.wait_ge(summed, 2 * i + p - 1)
                        pool.sem_inc(begun, 1)
                        for g in range(G):
                            pool.indirect_dma_start(rows[:, p, g, :], None, table,
                                                    bass.IndirectOffsetOnAxis(ap=far[:, p, g:g + 1], axis=0)
                                                    ).then_inc(rows_in[p], 16)
                steps(pool, LOOPS, body)

            @block.tensor
            def _(pe):
                def body(i, first):
                    for p in range(2):
                        pe.wait_ge(onehots, 2 * i + p + 1)
                        pe.wait_ge(rows_in[p], 16 * G * (i + 1))
                        if not first:
                            pe.wait_ge(added, (2 * i + p - 1) * G)
                        for g in range(G):
                            mm = pe.matmul(sums[:, p, g * P:(g + 1) * P], oh[:, p, g, :], rows[:, p, g, :],
                                           start=True, stop=True)
                        mm.then_inc(summed, 1)
                steps(pe, LOOPS, body)

            @block.vector
            def _(dve):
                dve.memset(acc[:], 0.0).then_inc(cleared, 1)
                dve.wait_ge(cleared, 1)

                def body(i, first):
                    for p in range(2):
                        if not first:
                            dve.wait_ge(summed, 2 * i + p - 1)
                        dve.tensor_tensor(oh[:, p], over_blocks(k.iota_row[:], [P, G, P]),
                                          wide(o.slot[:, ds(i * STEP + p * G, G), 0], G, [P, G, P]), ALU.is_equal
                                          ).then_inc(onehots, 1)
                    for p in range(2):
                        dve.wait_ge(summed, 2 * i + p + 1)
                        for g in range(G):
                            n = (2 * i + p) * G + g
                            b = dve.value_load(o.block_i[0:1, ds(n, 1)], min_val=0, max_val=NB - 1)
                            if g or not first or p:
                                dve.wait_ge(added, n)
                            dve.tensor_tensor(acc[:, ds(b, 1), :], acc[:, ds(b, 1), :],
                                              sums[:, p, g * P:(g + 1) * P].unsqueeze(1), ALU.add).then_inc(added, 1)
                steps(dve, LOOPS, body)



VW = 3 * DE


def tanh_stage(k, o, table, qky, edges_dram):
    nc = k.nc
    (staged, spread, onehots, looked_up, pre, tanhs, prods, scored, kept) = (k.sem("th_" + s) for s in (
        "staged", "spread", "onehots", "looked_up", "pre", "tanhs", "prods", "scored", "kept"))
    begun = k.sem("th_begun")
    rows_in = [k.sem(f"th_rows_in{p}") for p in range(2)]
    stored = [k.sem(f"th_stored{p}") for p in range(2)]
    out_rows = edges_dram.rearrange("(e j) w -> e j w", e=P)
    with ExitStack() as c:
        rows = k.sb("th_rows", [P, 2, G, VW], F32, c)
        far = k.sb("th_far", [P, 2, G], I32, c)
        lo = k.sb("th_lo", [P, 2, G], BF16, c)
        oht = k.sb("th_oht", [P, 2, G, P], F32, c)
        sumqk = k.sb("th_sum", [P, 2, G, DE], F32, c)
        prod = k.sb("th_prod", [P, 2, G, DE], F32, c)
        node_bc = k.ps("th_node", [P, 2, 512], c)
        query = k.ps("th_query", [P, 2, 512], c)
        with k.block() as block:
            @block.scalar
            def _(act):
                def body(i, first):
                    for p in range(2):
                        if not first:
                            act.wait_ge(rows_in[p], 16 * G * i)
                            act.wait_ge(spread, 2 * i + p - 1)
                        nc.scalar.copy(far[:, p], o.far_i[:, ds(i * STEP + p * G, G)]).then_inc(staged, 1)
                        nc.scalar.copy(lo[:, p], o.slot[:, ds(i * STEP + p * G, G), 0]).then_inc(staged, 1)
                    for p in range(2):
                        act.wait_ge(pre, 2 * i + p + 1)
                        nc.scalar.activation(rows[:, p, :, 0:DE], sumqk[:, p], ACT.Tanh).then_inc(tanhs, 1)
                steps(act, LOOPS, body)

            @block.sync
            def _(sp):
                def body(i, first):
                    for p in range(2):
                        sp.wait_ge(tanhs, 2 * i + p + 1)
                        sp.dma_start(out_rows[:, ds(i * STEP + p * G, G), :], rows[:, p]).then_inc(stored[p], 16)
                steps(sp, LOOPS, body)
                for p in range(2):
                    sp.wait_ge(stored[p], 16 * LOOPS)

            @block.gpsimd
            def _(pool):
                def body(i, first):
                    for p in range(2):
                        pool.wait_ge(staged, 4 * i + 2 * p + 1)
                        if not first:
                            pool.wait_ge(stored[p], 16 * i)
                            pool.wait_ge(prods, 2 * i + p - 1)
                        pool.sem_inc(begun, 1)
                        for g in range(G):
                            pool.indirect_dma_start(rows[:, p, g, :], None, table,
                                                    bass.IndirectOffsetOnAxis(ap=far[:, p, g:g + 1], axis=0)
                                                    ).then_inc(rows_in[p], 16)
                steps(pool, LOOPS, body)

            @block.tensor
            def _(pe):
                def body(i, first):
                    for p in range(2):
                        pe.wait_ge(staged, 4 * i + 2 * p + 2)
                        if not first:
                            pe.wait_ge(onehots, 2 * i + p - 1)
                        for g in range(G):
                            mm = pe.matmul(node_bc[:, p, g * P:(g + 1) * P], lo[:, p, g:g + 1].to_broadcast([P, P]),
                                           k.ident_h[:], start=True, stop=True)
                        mm.then_inc(spread, 1)
                    for p in range(2):
                        pe.wait_ge(onehots, 2 * i + p + 1)
                        if not first:
                            pe.wait_ge(pre, 2 * i + p - 1)
                        for g in range(G):
                            b = pe.value_load(o.block_i[0:1, ds(i * STEP + p * G + g, 1)], min_val=0, max_val=NB - 1)
                            mm = pe.matmul(query[:, p, g * DE:(g + 1) * DE], oht[:, p, g, :], qky[:, ds(b, 1), 0:DE],
                                           start=True, stop=True)
                        mm.then_inc(looked_up, 1)
                steps(pe, LOOPS, body)

            @block.vector
            def _(dve):
                phi = k.r["phi"][:].unsqueeze(1).to_broadcast([P, G, DE])

                def body(i, first):
                    for p in range(2):
                        dve.wait_ge(spread, 2 * i + p + 1)
                        if not first:
                            dve.wait_ge(looked_up, 2 * i + p - 1)
                        dve.tensor_scalar(oht[:, p], node_bc[:, p].rearrange("p (g e) -> p g e", g=G), k.iota_col[:],
                                          None, ALU.is_equal).then_inc(onehots, 1)
                    for p in range(2):
                        dve.wait_ge(looked_up, 2 * i + p + 1)
                        dve.wait_ge(rows_in[p], 16 * G * (i + 1))
                        if not first:
                            dve.wait_ge(tanhs, 2 * i + p - 1)
                        dve.tensor_tensor(sumqk[:, p], query[:, p, 0:G * DE].rearrange("p (g f) -> p g f", g=G),
                                          rows[:, p, :, 0:DE], ALU.add).then_inc(pre, 1)
                    for p in range(2):
                        dve.wait_ge(tanhs, 2 * i + p + 1)
                        if not first:
                            dve.wait_ge(scored, 2 * i + p - 1)
                        dve.tensor_tensor(prod[:, p], rows[:, p, :, 0:DE], phi, ALU.mult).then_inc(prods, 1)
                        dve.wait_ge(prods, 2 * i + p + 1)
                        dve.tensor_reduce(k.scores[:, ds(i * STEP + p * G, G)], prod[:, p], AX, ALU.add).then_inc(scored, 1)
                steps(dve, LOOPS, body)


def softmax_weights_stage(k, o):
    nc = k.nc
    step, largest, spread, shifted, done = (k.sem("sw_" + s) for s in ("step", "largest", "spread", "shifted", "done"))
    with ExitStack() as c:
        none = k.sb("sw_none", [P, J], F32, c)
        col = k.sb("sw_col", [P, 1], F32, c)
        top = k.sb("sw_top", [P, 1], F32, c)
        neg = k.sb("sw_neg", [P, 1], F32, c)
        with k.block() as block:
            @block.vector
            def _(dve):
                dve.tensor_scalar(none[:], o.slot[:, :, 0], 0.0, -BIG, ALU.is_lt, ALU.mult).then_inc(step, 1)
                dve.wait_ge(step, 1)
                dve.tensor_tensor(k.scores[:], k.scores[:], none[:], ALU.add).then_inc(step, 1)
                dve.wait_ge(step, 2)
                dve.tensor_reduce(col[:], k.scores[:], AX, ALU.max).then_inc(largest, 1)
                dve.wait_ge(spread, 1)
                dve.tensor_scalar(neg[:], top[:], -1.0, None, ALU.mult).then_inc(shifted, 1)

            @block.gpsimd
            def _(pool):
                pool.wait_ge(largest, 1)
                nc.gpsimd.partition_all_reduce(top[:], col[:], P, RMAX).then_inc(spread, 1)

            @block.scalar
            def _(act):
                act.wait_ge(shifted, 1)
                nc.scalar.activation(k.scores[:], k.scores[:], ACT.Exp, bias=neg[:]).then_inc(done, 1)


def weighted_sum_stage(k, o, edges_dram, acc):
    nc = k.nc
    W = VW + 1
    (cleared, staged, weighted, summed, added, ones_put) = (k.sem("ws_" + s) for s in (
        "cleared", "staged", "weighted", "summed", "added", "ones_put"))
    rows_in = [k.sem(f"ws_rows_in{p}") for p in range(2)]
    rows_dram = edges_dram.rearrange("(e j) w -> e j w", e=P)
    with ExitStack() as c:
        rows = k.sb("ws_rows", [P, 2, G, W], F32, c)
        ohw = k.sb("ws_ohw", [P, 2, G, P], F32, c)
        wt = k.sb("ws_wt", [P, 2, G], F32, c)
        lo = k.sb("ws_lo", [P, 2, G], F32, c)
        sums = k.ps("ws_sums", [P, 2, G, 256], c)
        with k.block() as block:
            @block.sync
            def _(sp):
                sp.wait_ge(ones_put, 1)

                def body(i, first):
                    for p in range(2):
                        if not first:
                            sp.wait_ge(summed, 2 * i + p - 1)
                        sp.dma_start(rows[:, p, :, 0:VW], rows_dram[:, ds(i * STEP + p * G, G), :]).then_inc(rows_in[p], 16)
                steps(sp, LOOPS, body)

            @block.scalar
            def _(act):
                def body(i, first):
                    for p in range(2):
                        if not first:
                            act.wait_ge(weighted, 2 * i + p - 1)
                        nc.scalar.copy(wt[:, p], k.scores[:, ds(i * STEP + p * G, G)]).then_inc(staged, 1)
                        nc.scalar.copy(lo[:, p], o.slot[:, ds(i * STEP + p * G, G), 0]).then_inc(staged, 1)
                steps(act, LOOPS, body)

            @block.tensor
            def _(pe):
                def body(i, first):
                    for p in range(2):
                        pe.wait_ge(weighted, 2 * i + p + 1)
                        pe.wait_ge(rows_in[p], 16 * (i + 1))
                        if not first:
                            pe.wait_ge(added, (2 * i + p - 1) * G)
                        for g in range(G):
                            mm = pe.matmul(sums[:, p, g, 0:W], ohw[:, p, g, :], rows[:, p, g, :], start=True, stop=True)
                        mm.then_inc(summed, 1)
                steps(pe, LOOPS, body)

            @block.vector
            def _(dve):
                dve.memset(rows[:, :, :, VW:W], 1.0).then_inc(ones_put, 1)
                dve.memset(acc[:], 0.0).then_inc(cleared, 1)
                dve.wait_ge(cleared, 1)

                def body(i, first):
                    for p in range(2):
                        dve.wait_ge(staged, 4 * i + 2 * p + 2)
                        if not first:
                            dve.wait_ge(summed, 2 * i + p - 1)
                        for g in range(G):
                            ins = dve.tensor_scalar(ohw[:, p, g, :], k.iota_row[:], lo[:, p, g:g + 1],
                                                    wt[:, p, g:g + 1], ALU.is_equal, ALU.mult)
                        ins.then_inc(weighted, 1)
                    for p in range(2):
                        dve.wait_ge(summed, 2 * i + p + 1)
                        for g in range(G):
                            n = (2 * i + p) * G + g
                            b = dve.value_load(o.block_i[0:1, ds(n, 1)], min_val=0, max_val=NB - 1)
                            if g or not first or p:
                                dve.wait_ge(added, n)
                            dve.tensor_tensor(acc[:, ds(b, 1), :], acc[:, ds(b, 1), :],
                                              sums[:, p, g, 0:W].unsqueeze(1), ALU.add).then_inc(added, 1)
                steps(dve, LOOPS, body)



def message_stage(k, o, table, ab, acc):
    nc = k.nc
    (cleared, staged, spread, turned, onehots, features_t, first_part, hidden, hidden_turned, hidden_t, second,
     biased, messages, endhots, summed, added) = (k.sem("ms_" + s) for s in (
         "cleared", "staged", "spread", "turned", "onehots", "features_t", "first_part", "hidden", "hidden_turned",
         "hidden_t", "second", "biased", "messages", "endhots", "summed", "added"))
    begun = k.sem("ms_begun")
    rows_in = [k.sem(f"ms_rows_in{p}") for p in range(2)]
    features_in = [k.sem(f"ms_features_in{p}") for p in range(2)]
    rows_dram = o.rows_dram.rearrange("(e j) w -> e j w", e=P)

    def four(ap):
        return ap.rearrange("p (g f) -> p g f", g=G)

    with ExitStack() as c:
        feat = k.sb("ms_feat", [P, 2, G, RW], F32, c)
        rows = k.sb("ms_rows", [P, 2, G, D], F32, c)
        far = k.sb("ms_far", [P, 2, G], I32, c)
        lo = k.sb("ms_lo", [P, 2, G], BF16, c)
        oht = k.sb("ms_oht", [P, 2, G, P], F32, c)
        oh = k.sb("ms_oh", [P, 2, G, P], F32, c)
        ft = k.sb("ms_ft", [DE, 2, G * P], F32, c)
        h = k.sb("ms_h", [P, 2, G, D], F32, c)
        ht = k.sb("ms_ht", [P, 2, G * P], F32, c)
        m = k.sb("ms_m", [P, 2, G, D], F32, c)
        pa = k.ps("ms_pa", [P, 2, 512], c)
        pb = k.ps("ms_pb", [P, 2, 512], c)
        pc = k.ps("ms_pc", [P, 2, 512], c)
        pd = k.ps("ms_pd", [P, 2, 512], c)
        with k.block() as block:
            @block.sync
            def _(sp):
                def body(i, first):
                    for p in range(2):
                        if not first:
                            sp.wait_ge(turned, 2 * i + p - 1)
                        sp.dma_start(feat[:, p], rows_dram[:, ds(i * STEP + p * G, G), :]).then_inc(features_in[p], 16)
                steps(sp, LOOPS, body)

            @block.gpsimd
            def _(pool):
                def body(i, first):
                    for p in range(2):
                        pool.wait_ge(staged, 4 * i + 2 * p + 1)
                        if not first:
                            pool.wait_ge(first_part, 2 * i + p - 1)
                        pool.sem_inc(begun, 1)
                        for g in range(G):
                            pool.indirect_dma_start(rows[:, p, g, :], None, table,
                                                    bass.IndirectOffsetOnAxis(ap=far[:, p, g:g + 1], axis=0)
                                                    ).then_inc(rows_in[p], 16)
                steps(pool, LOOPS, body)

            @block.tensor
            def _(pe):
                def body(i, first):
                    for p in range(2):
                        pe.wait_ge(staged, 4 * i + 2 * p + 2)
                        pe.wait_ge(features_in[p], 16 * (i + 1))
                        if not first:
                            pe.wait_ge(hidden_t, 2 * i + p - 1)
                            pe.wait_ge(biased, 2 * i + p - 1)
                        for g in range(G):
                            mm = pe.matmul(pa[:, p, g * P:(g + 1) * P], lo[:, p, g:g + 1].to_broadcast([P, P]),
                                           k.ident_h[:], start=True, stop=True)
                        mm.then_inc(spread, 1)
                        for g in range(G):
                            mm = pe.transpose(pb[0:DE, p, g * P:(g + 1) * P], feat[:, p, g, 0:DE], k.ident[:])
                        mm.then_inc(turned, 1)
                    for p in range(2):
                        pe.wait_ge(onehots, 2 * i + p + 1)
                        pe.wait_ge(features_t, 2 * i + p + 1)
                        if not first:
                            pe.wait_ge(first_part, 2 * i + p - 1)
                        for g in range(G):
                            b = pe.value_load(o.block_i[0:1, ds(i * STEP + p * G + g, 1)], min_val=0, max_val=NB - 1)
                            pe.matmul(pc[:, p, g * P:(g + 1) * P], oht[:, p, g, :], ab[:, ds(b, 1), D:2 * D],
                                      start=True, stop=False)
                            mm = pe.matmul(pc[:, p, g * P:(g + 1) * P], ft[:, p, g * P:(g + 1) * P], k.w["W1c"][:],
                                           start=False, stop=True)
                        mm.then_inc(hidden, 1)
                    for p in range(2):
                        pe.wait_ge(first_part, 2 * i + p + 1)
                        for g in range(G):
                            mm = pe.transpose(pa[:, p, g * P:(g + 1) * P], h[:, p, g, :], k.ident[:])
                        mm.then_inc(hidden_turned, 1)
                    for p in range(2):
                        pe.wait_ge(hidden_t, 2 * i + p + 1)
                        for g in range(G):
                            mm = pe.matmul(pb[:, p, g * P:(g + 1) * P], ht[:, p, g * P:(g + 1) * P], k.w["W2"][:],
                                           start=True, stop=True)
                        mm.then_inc(second, 1)
                    for p in range(2):
                        pe.wait_ge(messages, 2 * i + p + 1)
                        pe.wait_ge(endhots, 2 * i + p + 1)
                        if not first:
                            pe.wait_ge(added, (2 * i + p - 1) * G)
                        for g in range(G):
                            mm = pe.matmul(pd[:, p, g * P:(g + 1) * P], oh[:, p, g, :], m[:, p, g, :], start=True, stop=True)
                        mm.then_inc(summed, 1)
                steps(pe, LOOPS, body)

            @block.scalar
            def _(act):
                def body(i, first):
                    for p in range(2):
                        if not first:
                            act.wait_ge(rows_in[p], 16 * G * i)
                            act.wait_ge(spread, 2 * i + p - 1)
                        nc.scalar.copy(far[:, p], o.far_i[:, ds(i * STEP + p * G, G)]).then_inc(staged, 1)
                        nc.scalar.copy(lo[:, p], o.slot[:, ds(i * STEP + p * G, G), 0]).then_inc(staged, 1)
                    for p in range(2):
                        act.wait_ge(turned, 2 * i + p + 1)
                        if not first:
                            act.wait_ge(hidden, 2 * i + p - 1)
                        nc.scalar.copy(ft[:, p], pb[0:DE, p]).then_inc(features_t, 1)
                    for p in range(2):
                        act.wait_ge(hidden_turned, 2 * i + p + 1)
                        if not first:
                            act.wait_ge(second, 2 * i + p - 1)
                        nc.scalar.activation(ht[:, p], pa[:, p], ACT.Relu).then_inc(hidden_t, 1)
                    for p in range(2):
                        act.wait_ge(biased, 2 * i + p + 1)
                        nc.scalar.activation(m[:, p], m[:, p], ACT.Relu).then_inc(messages, 1)
                steps(act, LOOPS, body)

            @block.vector
            def _(dve):
                dve.memset(acc[:], 0.0).then_inc(cleared, 1)
                dve.wait_ge(cleared, 1)

                def body(i, first):
                    for p in range(2):
                        dve.wait_ge(spread, 2 * i + p + 1)
                        if not first:
                            dve.wait_ge(hidden, 2 * i + p - 1)
                        dve.tensor_scalar(oht[:, p], four(pa[:, p]), k.iota_col[:], None, ALU.is_equal).then_inc(onehots, 1)
                        if not first:
                            dve.wait_ge(summed, 2 * i + p - 1)
                        dve.tensor_tensor(oh[:, p], over_blocks(k.iota_row[:], [P, G, P]),
                                          wide(o.slot[:, ds(i * STEP + p * G, G), 0], G, [P, G, P]), ALU.is_equal
                                          ).then_inc(endhots, 1)
                    for p in range(2):
                        dve.wait_ge(hidden, 2 * i + p + 1)
                        dve.wait_ge(rows_in[p], 16 * G * (i + 1))
                        if not first:
                            dve.wait_ge(hidden_turned, 2 * i + p - 1)
                        dve.tensor_tensor(h[:, p], four(pc[:, p]), rows[:, p], ALU.add).then_inc(first_part, 1)
                    for p in range(2):
                        dve.wait_ge(second, 2 * i + p + 1)
                        if not first:
                            dve.wait_ge(summed, 2 * i + p - 1)
                        dve.tensor_tensor(m[:, p], four(pb[:, p]), over_blocks(k.r["b2"][:], [P, G, D]), ALU.add
                                          ).then_inc(biased, 1)
                    for p in range(2):
                        dve.wait_ge(summed, 2 * i + p + 1)
                        for g in range(G):
                            n = (2 * i + p) * G + g
                            b = dve.value_load(o.block_i[0:1, ds(n, 1)], min_val=0, max_val=NB - 1)
                            if g or not first or p:
                                dve.wait_ge(added, n)
                            dve.tensor_tensor(acc[:, ds(b, 1), :], acc[:, ds(b, 1), :],
                                              pd[:, p, g * P:(g + 1) * P].unsqueeze(1), ALU.add).then_inc(added, 1)
                steps(dve, LOOPS, body)



def product_stage(k, name, terms, out, width, bias):
    nc = k.nc
    T = len(terms)
    stride = P if width <= P else 2 * P
    staged, turned, turned_in, made, written = (k.sem(f"{name}_{s}") for s in (
        "staged", "turned", "turned_in", "made", "written"))
    with ExitStack() as c:
        st = [k.sb(f"{name}_st{t}", [P, NCH, K], F32, c) for t, (_, K, _) in enumerate(terms)]
        xt = [k.sb(f"{name}_xt{t}", [K, NCH * P], F32, c) for t, (_, K, _) in enumerate(terms)]
        pt = [k.ps(f"{name}_pt{t}", [P, 1024], c) for t in range(T)]
        po = k.ps(f"{name}_po", [P, 1024 if stride == P else 1536], c)
        pov = po[:, 0:NCH * stride].rearrange("p (b f) -> p b f", b=NCH)
        with k.block() as block:
            @block.scalar
            def _(act):
                def body(i, first):
                    for t, (x, K, _) in enumerate(terms):
                        if not first:
                            act.wait_ge(turned, T * i)
                        nc.scalar.copy(st[t][:], x[:, ds(i * NCH, NCH), :]).then_inc(staged, 1)
                steps(act, NB // NCH, body)

            @block.tensor
            def _(pe):
                def body(i, first):
                    for t, (_, K, _) in enumerate(terms):
                        pe.wait_ge(staged, T * i + t + 1)
                        if not first:
                            pe.wait_ge(turned_in, T * i)
                        for q in range(NCH):
                            mm = pe.transpose(pt[t][0:K, q * P:(q + 1) * P], st[t][:, q, :], k.ident[:])
                        mm.then_inc(turned, 1)
                    pe.wait_ge(turned_in, T * i + T)
                    if not first:
                        pe.wait_ge(written, i)
                    for q in range(NCH):
                        for t, (_, K, w) in enumerate(terms):
                            mm = pe.matmul(pov[:, q, 0:width], xt[t][:, q * P:(q + 1) * P], w, start=(t == 0), stop=(t == T - 1))
                    mm.then_inc(made, 1)
                steps(pe, NB // NCH, body)

            @block.vector
            def _(dve):
                def body(i, first):
                    for t, (_, K, _) in enumerate(terms):
                        dve.wait_ge(turned, T * i + t + 1)
                        if not first:
                            dve.wait_ge(made, i)
                        dve.tensor_copy(xt[t][:], pt[t][0:K, 0:NCH * P]).then_inc(turned_in, 1)
                    dve.wait_ge(made, i + 1)
                    dve.tensor_tensor(out[:, ds(i * NCH, NCH), 0:width], pov[:, :, 0:width],
                                      over_blocks(bias[:, 0:width], [P, NCH, width]), ALU.add).then_inc(written, 1)
                steps(dve, NB // NCH, body)


class Chain:

    def __init__(self, dve, step, variances=None, roots=None):
        self.dve, self.step, self.n = dve, step, 0
        self.variances, self.roots, self.rooted = variances, roots, 0

    def root(self, ins, place):
        self.rooted += 1
        ins.then_inc(self.variances, 1)
        self.dve.wait_ge(self.roots, self.rooted)
        self(self.dve.reciprocal(place, place))

    def __call__(self, ins):
        self.n += 1
        ins.then_inc(self.step, 1)
        self.dve.wait_ge(self.step, self.n)

    def norm(self, k, out, x, sq, col, gain=None, bias=None, eps=1e-5):
        dve, full = self.dve, [P, NB, D]
        self(dve.tensor_reduce(col[:, 0, :], x[:], AX, ALU.add))
        self(dve.tensor_scalar(col[:, 0, :], col[:, 0, :], 1.0 / D, None, ALU.mult))
        self(dve.tensor_tensor(out[:], x[:], wide(col[:, 0, :], D, full), ALU.subtract))
        self(dve.tensor_tensor(sq[:], out[:], out[:], ALU.mult))
        self(dve.tensor_reduce(col[:, 1, :], sq[:], AX, ALU.add))
        self.root(dve.tensor_scalar(col[:, 1, :], col[:, 1, :], 1.0 / D, eps, ALU.mult, ALU.add), col[:, 1, :])
        self(dve.tensor_tensor(out[:], out[:], wide(col[:, 1, :], D, full), ALU.mult))
        if gain is not None:
            self(dve.tensor_tensor(out[:], out[:], over_blocks(gain[:], full), ALU.mult))
            self(dve.tensor_tensor(out[:], out[:], over_blocks(bias[:], full), ALU.add))


def root_program(act, variances, roots, places):
    for n, ap in enumerate(places):
        act.wait_ge(variances, n + 1)
        act.activation(ap, ap, ACT.Sqrt).then_inc(roots, 1)


def node_stage(k, name, program, norms=0):
    step, variances, roots = (k.sem(f"{name}_{s}") for s in ("step", "variances", "roots"))
    with k.block() as block:
        @block.scalar
        def _(act):
            root_program(act, variances, roots, [k.col[:, 1, :]] * norms)

        @block.vector
        def _(dve):
            program(Chain(dve, step, variances, roots), dve)


def store_stage(k, name, pairs):
    stored = k.sem(name + "_stored")
    with k.block() as block:
        @block.sync
        def _(sp):
            for table, x in pairs:
                sp.dma_start(table.rearrange("(b p) f -> p b f", p=P), x).then_inc(stored, 16)
            sp.wait_ge(stored, 16 * len(pairs))


def global_token_stage(k):
    nc = k.nc
    step, summed, token, spread = (k.sem("gt_" + s) for s in ("step", "summed", "token", "spread"))
    with ExitStack() as c:
        part = k.sb("gt_part", [P, D], F32, c)
        g = k.sb("gt_g", [P, 1], F32, c)
        row = k.sb("gt_row", [P, D], F32, c)
        pg = k.ps("gt_pg", [P, 512], c)
        pr = k.ps("gt_pr", [P, 512], c)
        with k.block() as block:
            @block.tensor
            def _(pe):
                pe.wait_ge(summed, 1)
                pe.matmul(pg[:, 0:1], part[:], k.ones[:, 0:1], start=True, stop=True).then_inc(token, 1)
                pe.wait_ge(summed, 2)
                pe.matmul(pr[:, 0:D], g[:].to_broadcast([P, P]), k.w["Wg"][:], start=True, stop=True).then_inc(spread, 1)

            @block.vector
            def _(dve):
                link = Chain(dve, step)
                link(dve.tensor_scalar(k.X[:, NB - 1, :], k.X[:, NB - 1, :], k.last_rows[:], None, ALU.mult))
                dve.tensor_reduce(part[:], k.X[:].rearrange("p b f -> p f b"), AX, ALU.add).then_inc(summed, 1)
                dve.wait_ge(token, 1)
                dve.tensor_scalar(g[:], pg[:, 0:1], 1.0 / N, k.gtok[:], ALU.mult, ALU.add).then_inc(summed, 1)
                dve.wait_ge(spread, 1)
                link(dve.tensor_tensor(row[:], pr[:, 0:D], k.r["Wg"][:], ALU.add))
                link(dve.tensor_tensor(k.X[:], k.X[:], over_blocks(row[:], [P, NB, D]), ALU.add))


def batch_norm_stage(k, name, x, sq, gain, bias):
    nc, full = k.nc, [P, NB, D]
    step, summed, spread, variances, roots = (k.sem(f"{name}_{s}") for s in (
        "step", "summed", "spread", "variances", "roots"))
    with ExitStack() as c:
        part = k.sb(name + "_part", [P, 2, D], F32, c)
        row = k.sb(name + "_row", [P, 2, D], F32, c)
        pr = k.ps(name + "_pr", [P, 2, 512], c)
        with k.block() as block:
            @block.tensor
            def _(pe):
                for t in range(2):
                    pe.wait_ge(summed, t + 1)
                    pe.matmul(pr[:, t, 0:D], k.ones[:], part[:, t, :], start=True, stop=True).then_inc(spread, 1)

            @block.scalar
            def _(act):
                root_program(act, variances, roots, [row[:, 1]])

            @block.vector
            def _(dve):
                link = Chain(dve, step, variances, roots)
                link(dve.tensor_scalar(x[:, NB - 1, :], x[:, NB - 1, :], k.last_rows[:], None, ALU.mult))
                dve.tensor_reduce(part[:, 0], x[:].rearrange("p b f -> p f b"), AX, ALU.add).then_inc(summed, 1)
                dve.wait_ge(spread, 1)
                link(dve.tensor_scalar(row[:, 0], pr[:, 0, 0:D], 1.0 / N, None, ALU.mult))
                link(dve.tensor_tensor(x[:], x[:], over_blocks(row[:, 0], full), ALU.subtract))
                link(dve.tensor_tensor(sq[:], x[:], x[:], ALU.mult))
                link(dve.tensor_scalar(sq[:, NB - 1, :], sq[:, NB - 1, :], k.last_rows[:], None, ALU.mult))
                dve.tensor_reduce(part[:, 1], sq[:].rearrange("p b f -> p f b"), AX, ALU.add).then_inc(summed, 1)
                dve.wait_ge(spread, 2)
                link.root(dve.tensor_scalar(row[:, 1], pr[:, 1, 0:D], 1.0 / N, 1e-5, ALU.mult, ALU.add), row[:, 1])
                link(dve.tensor_tensor(row[:, 1], row[:, 1], gain[:], ALU.mult))
                link(dve.tensor_tensor(x[:], x[:], over_blocks(row[:, 1], full), ALU.mult))
                link(dve.tensor_tensor(x[:], x[:], over_blocks(bias[:], full), ALU.add))



class Order:

    def __init__(self, k, name):
        self.name = name
        self.slot = k.sb(name + "_slot", [P, J, 2])
        self.far_i = k.sb(name + "_far_i", [P, J], I32)
        self.block_f = k.sb(name + "_block_f", [P, J])
        self.block_i = k.sb(name + "_block_i", [P, J], I32)


def build(nc, a, out):
    with ExitStack() as ctx:
        k = Core(nc, ctx)
        load_stage(k, a)
        k.scores = k.sb("scores", [P, J])
        k.deg = k.sb("deg", [P, NB])
        k.mx = k.sb("mx", [P, NB, 2])
        by_dst, by_src = Order(k, "dst"), Order(k, "src")
        early = ExitStack()
        for o in (by_dst, by_src):
            o.row = k.sb(o.name + "_row", [EP, EC], I32, early)
            o.meta = k.sb(o.name + "_meta", [EP, EC, 2], F32, early)
        by_dst.rows_dram = nc.dram_tensor("rows_by_dst", (P * J, RW), F32).ap()
        by_src.ids_dram = nc.dram_tensor("ids_by_src", (P * J, 2), F32).ap()
        edges_dram = nc.dram_tensor("edges_by_src", (P * J, VW), F32).ap()
        tables = [nc.dram_tensor(f"table{n}", (P * NB, D), F32).ap() for n in range(5)]
        table_kv = nc.dram_tensor("table_kv", (P * NB, VW), F32).ap()
        order_stage(k, by_dst, a["dst"], a["src"])
        order_stage(k, by_src, a["src"], a["dst"])
        scatter_features_stage(k, by_dst, a["edge_attr_64"])
        score_stage(k, by_dst, by_src)
        node_maximum_stage(k, by_dst, by_src)
        early.close()
        far_ends_stage(k, [by_dst, by_src])

        X, full = k.X, [P, NB, D]
        acc = k.sb("acc", [P, NB, VW + 1])
        A = k.sb("A", full)
        B = k.sb("B", full)
        wide2 = k.sb("wide2", [P, NB, 2 * D])
        col = k.col = k.sb("col", [P, 2, NB])
        relu_tmp = ALU.max

        sum0 = acc[:].rearrange("p b w -> p (b w)")[:, 0:NB * RW].rearrange("p (b w) -> p b w", b=NB)
        attention_sum_stage(k, by_dst, sum0)

        def shares0(link, dve):
            link(dve.tensor_scalar(col[:, 0, :], sum0[:, :, DE + 1], 1e-6, None, ALU.add))
            link(dve.reciprocal(col[:, 0, :], col[:, 0, :]))
            link(dve.tensor_copy(sum0[:, :, DE], sum0[:, :, DE + 1]))
            link(dve.tensor_tensor(sum0[:, :, 0:DE + 1], sum0[:, :, 0:DE + 1], wide(col[:, 0, :], DE + 1, [P, NB, DE + 1]), ALU.mult))
        node_stage(k, "shares0", shares0)
        product_stage(k, "ev", [(sum0[:, :, 0:DE + 1], DE + 1, k.w["ev"][:])], A, D, k.r["none"])
        product_stage(k, "out1", [(A, D, k.w["out1"][:])], B, D, k.r["out1"])
        node_stage(k, "relu0", lambda link, dve: link(dve.tensor_scalar(B[:], B[:], 0.0, None, relu_tmp)))
        product_stage(k, "out2", [(B, D, k.w["out2"][:])], A, D, k.r["out2"])

        def end0(link, dve):
            link(dve.tensor_tensor(A[:], A[:], X[:], ALU.add))
            link(dve.tensor_tensor(A[:], A[:], X[:], ALU.add))
            link.norm(k, X, A, B, col)
        node_stage(k, "end0", end0, norms=1)

        node_stage(k, "keep1", lambda link, dve: link(dve.tensor_copy(A[:], X[:])))
        global_token_stage(k)
        node_stage(k, "ln1", lambda link, dve: link.norm(k, B, X, wide2[:, :, 0:D], col, k.r["ln1g"], k.r["ln1b"]), norms=1)
        product_stage(k, "msg", [(B, D, k.w["msg"][:])], wide2, D, k.r["msg"])
        store_stage(k, "msg_table", [(tables[0], wide2[:, :, 0:D])])
        gather_sum_stage(k, "gs1", by_src, tables[0], acc[:, :, 0:D])

        def mix1(link, dve):
            link(dve.tensor_scalar(k.eps[:], k.eps[:], 1.0, None, ALU.add))
            link(dve.scalar_tensor_tensor(B[:], B[:], k.eps[:], acc[:, :, 0:D], ALU.mult, ALU.add))
        node_stage(k, "mix1", mix1)
        product_stage(k, "lin", [(B, D, k.w["lin"][:])], wide2, D, k.r["lin"])

        def ln2(link, dve):
            link(dve.tensor_scalar(wide2[:, :, 0:D], wide2[:, :, 0:D], 0.0, None, ALU.max))
            link(dve.tensor_tensor(X[:], X[:], wide2[:, :, 0:D], ALU.add))
            link.norm(k, B, X, wide2[:, :, 0:D], col, k.r["ln2g"], k.r["ln2b"])
        node_stage(k, "ln2", ln2, norms=1)
        product_stage(k, "qky", [(B, D, k.w["qky"][:])], wide2, 2 * D, k.r["qky"])
        store_stage(k, "kv_table", [(table_kv, wide2[:, :, DE:2 * D])])
        tanh_stage(k, by_src, table_kv, wide2, edges_dram)
        softmax_weights_stage(k, by_src)
        weighted_sum_stage(k, by_src, edges_dram, acc)

        def shares1(link, dve):
            link(dve.tensor_scalar(col[:, 0, :], acc[:, :, VW], 1e-9, None, ALU.add))
            link(dve.reciprocal(col[:, 0, :], col[:, 0, :]))
            link(dve.tensor_tensor(acc[:], acc[:], wide(col[:, 0, :], VW + 1, [P, NB, VW + 1]), ALU.mult))
            link(dve.tensor_tensor(X[:], X[:], acc[:, :, DE:VW], ALU.add))
            link(dve.tensor_copy(acc[:, :, DE], acc[:, :, VW]))
        node_stage(k, "shares1", shares1)
        product_stage(k, "We", [(acc[:, :, 0:DE + 1], DE + 1, k.w["We"][:])], wide2, D, k.r["none"])

        def ln3(link, dve):
            link(dve.tensor_tensor(X[:], X[:], wide2[:, :, 0:D], ALU.add))
            link.norm(k, B, X, wide2[:, :, 0:D], col, k.r["ln3g"], k.r["ln3b"])
        node_stage(k, "ln3", ln3, norms=1)
        product_stage(k, "ffn1", [(B, D, k.w["ffn1"][:])], wide2, 2 * D, k.r["ffn1"])
        node_stage(k, "relu1", lambda link, dve: link(dve.tensor_scalar(wide2[:], wide2[:], 0.0, None, ALU.max)))
        product_stage(k, "ffn2", [(wide2[:, :, 0:D], D, k.w["ffn2"][:, 0:D]), (wide2[:, :, D:2 * D], D, k.w["ffn2"][:, D:2 * D])],
                      B, D, k.r["ffn2"])

        def end1(link, dve):
            link(dve.tensor_tensor(B[:], B[:], X[:], ALU.add))
            link(dve.tensor_tensor(A[:], A[:], B[:], ALU.add))
            link.norm(k, X, A, B, col)
        node_stage(k, "end1", end1, norms=1)

        product_stage(k, "ab", [(X, D, k.w["W1ab"][:])], wide2, 2 * D, k.r["ab"])
        store_stage(k, "a_table", [(tables[1], wide2[:, :, 0:D])])
        message_stage(k, by_dst, tables[1], wide2, acc[:, :, 0:D])
        node_stage(k, "copy2", lambda link, dve: link(dve.tensor_copy(A[:], acc[:, :, 0:D])))
        product_stage(k, "bn", [(A, D, k.w["Wn"][:])], B, D, k.r["bn"])

        def end2(link, dve):
            link(dve.tensor_scalar(B[:], B[:], 0.0, None, ALU.max))
            link(dve.tensor_tensor(B[:], B[:], X[:], ALU.add))
            link.norm(k, A, B, wide2[:, :, 0:D], col, k.r["gamma"], k.r["beta"])
            link(dve.tensor_tensor(B[:], A[:], X[:], ALU.add))
            link.norm(k, X, B, wide2[:, :, 0:D], col)
        node_stage(k, "end2", end2, norms=2)

        H = wide2[:, :, 0:D]
        T = wide2[:, :, D:2 * D]

        def sage(name, x, table, w_self, w_neigh, bias, dst):
            store_stage(k, name + "_table", [(table, x[:])])
            gather_sum_stage(k, name + "_gs", by_dst, table, acc[:, :, 0:D])
            node_stage(k, name + "_mean", lambda link, dve: link(dve.tensor_tensor(
                acc[:, :, 0:D], acc[:, :, 0:D], wide(k.deg[:], D, full), ALU.mult)))
            product_stage(k, name + "_pr", [(x, D, w_self[:]), (acc[:, :, 0:D], D, w_neigh[:])], dst, D, bias)

        sage("sg1", X, tables[2], k.w["s1"], k.w["n1"], k.r["s1"], A)
        node_stage(k, "relu3", lambda link, dve: link(dve.tensor_scalar(A[:], A[:], 0.0, None, ALU.max)))
        batch_norm_stage(k, "bn1", A, B, k.r["bn1g"], k.r["bn1b"])
        sage("sg2", A, tables[3], k.w["s2"], k.w["n2"], k.r["s2"], B)

        def res3(link, dve):
            link(dve.tensor_scalar(B[:], B[:], 0.0, None, ALU.max))
            link(dve.tensor_tensor(A[:], A[:], B[:], ALU.add))
        node_stage(k, "res3", res3)
        batch_norm_stage(k, "bn2", A, B, k.r["bn2g"], k.r["bn2b"])
        sage("sg3", A, tables[4], k.w["s3"], k.w["n3"], k.r["s3"], B)

        def end3(link, dve):
            link.norm(k, A, B, H, col, k.r["lng"], k.r["lnb"])
            link(dve.tensor_tensor(A[:], A[:], X[:], ALU.add))
            link.norm(k, B, A, H, col)
        node_stage(k, "end3", end3, norms=2)

        written = k.sem("written")
        with k.block() as block:
            @block.sync
            def _(sp):
                sp.dma_start(out[0:(NB - 1) * P, :].rearrange("(b p) f -> p b f", p=P), B[:, 0:NB - 1, :]).then_inc(written, 16)
                sp.dma_start(out[(NB - 1) * P:N, :], B[0:LAST, NB - 1, :]).then_inc(written, 16)
                sp.wait_ge(written, 32)


def kernel(**inputs):
    import numpy as np
    import concourse.bacc as bacc
    from concourse.bass_utils import run_bass_kernel_spmd

    nc = bacc.Bacc("TRN2", target_bir_lowering=False, num_devices=1)
    arrays, a = {}, {}
    for name in inputs:
        v = np.ascontiguousarray(inputs[name])
        if v.ndim == 0:
            v = v.reshape(1)
        arrays["in_" + name] = v
        a[name] = nc.dram_tensor("in_" + name, v.shape, mybir.dt.from_np(v.dtype), kind="ExternalInput").ap()
    out = nc.dram_tensor("out", (N, D), F32, kind="ExternalOutput").ap()
    build(nc, a, out)
    return run_bass_kernel_spmd(nc, [arrays], core_ids=[0]).results[0]["out"]
```

```python
from contextlib import ExitStack, contextmanager

import concourse.bass as bass
from concourse import mybir

ALU = mybir.AluOpType
ACT = mybir.ActivationFunctionType
F32 = mybir.dt.float32
BF16 = mybir.dt.bfloat16
I32 = mybir.dt.int32
AX = mybir.AxisListType.X
RMAX = bass.bass_isa.ReduceOp.max
ds = bass.ds

P = 128
N = 3125
E = 100000
D = 128
DE = 64
NB = -(-N // P)
LAST = N - (NB - 1) * P
EP, EC = 125, 800
G = 4
Q = 4
STEP = Q * G
J = -(-2 * ((E + NB * (2 * P - 1)) // (2 * P)) // STEP) * STEP
LOOPS = J // STEP
RW = DE + 2
BIG = 2.0 ** 100
NCH = 5


class Core:

    def __init__(self, nc, ctx):
        self.nc, self.ctx, self.stage_sems, self.registers, self.taken = nc, ctx, [], [], 0

    def sb(self, name, shape, dt=F32, ctx=None):
        return (ctx or self.ctx).enter_context(self.nc.sbuf_tensor(name, shape, dt))

    def ps(self, name, shape, ctx, dt=F32):
        return ctx.enter_context(self.nc.psum_tensor(name, shape, dt))

    def sem(self, name):
        self.stage_sems.append(self.nc.alloc_semaphore(name))
        return self.stage_sems[-1]

    @contextmanager
    def block(self):
        with self.nc.Block() as block:
            yield block
        self.nc.clear_and_free_semaphores(self.stage_sems)
        self.nc.all_engine_barrier()
        for eng, reg in self.registers:
            eng.free_register(reg)
        self.stage_sems, self.registers = [], []


def wide(ap, n, shape):
    return ap.unsqueeze(2).to_broadcast(shape)


def over_blocks(ap, shape):
    return ap.unsqueeze(1).to_broadcast(shape)


def steps(eng, count, body):
    body(0, True)
    with eng.Fori(1, count) as i:
        body(i, False)


def after(eng, sem, i, p, depth, first, each=1):
    if not first or p >= depth:
        eng.wait_ge(sem, (Q * i + p - depth + 1) * each)



def load_stage(k, a):
    nc = k.nc
    k.iota_row = k.sb("iota_row", [P, P])
    k.iota_col = k.sb("iota_col", [P, 1])
    k.ident = k.sb("ident", [P, P])
    k.ident_h = k.sb("ident_h", [P, P], BF16)
    k.ones = k.sb("ones", [P, P])
    k.ones_h = k.sb("ones_h", [P, P], BF16)
    k.before = k.sb("before", [P, P])
    k.before_h = k.sb("before_h", [P, P], BF16)
    k.last_rows = k.sb("last_rows", [P, 1])
    k.X = k.sb("X", [P, NB, D])
    k.att_b = k.sb("att_b", [P, 4])
    k.att_m = k.sb("att_m", [P, D + DE])
    k.att_bm = k.sb("att_bm", [P, 1])
    w = {}

    def weight(name, rows, cols):
        w[name] = k.sb("w_" + name, [rows, cols])
        return w[name]

    loads = []
    weight("ev", DE + 1, D)
    loads += [(w["ev"][0:DE, :], a["L0_gnn_ev_W"]), (w["ev"][DE:DE + 1, :], a["L0_gnn_ev_b"].unsqueeze(0))]
    weight("We", DE + 1, D)
    loads += [(w["We"][0:DE, :], a["L1_gnn_We_w"]), (w["We"][DE:DE + 1, :], a["L1_gnn_We_b"].unsqueeze(0))]
    for n, s in (("out1", "L0_gnn_out1_W"), ("out2", "L0_gnn_out2_W"), ("Wg", "L1_gnn_Wg_in_w"),
                 ("msg", "L1_gnn_msg_w"), ("lin", "L1_gnn_lin_w"), ("W2", "L2_gnn_W2"), ("Wn", "L2_gnn_Wn"),
                 ("s1", "L3_gnn_w1_self"), ("n1", "L3_gnn_w1_neigh"), ("s2", "L3_gnn_w2_self"),
                 ("n2", "L3_gnn_w2_neigh"), ("s3", "L3_gnn_w3_self"), ("n3", "L3_gnn_w3_neigh")):
        loads.append((weight(n, P, D)[:], a[s]))
    weight("qky", P, 2 * D)
    loads += [(w["qky"][:, 0:64], a["L1_gnn_Wq"]), (w["qky"][:, 64:128], a["L1_gnn_Wk"]),
              (w["qky"][:, 128:256], a["L1_gnn_Wy_w"])]
    loads.append((weight("ffn1", P, 2 * D)[:], a["L1_gnn_ffn_w1"]))
    weight("ffn2", P, 2 * D)
    loads += [(w["ffn2"][:, 0:D], a["L1_gnn_ffn_w2"][0:P, :]), (w["ffn2"][:, D:2 * D], a["L1_gnn_ffn_w2"][P:2 * P, :])]
    weight("W1ab", P, 2 * D)
    loads += [(w["W1ab"][:, 0:D], a["L2_gnn_W1"][0:P, :]), (w["W1ab"][:, D:2 * D], a["L2_gnn_W1"][P:2 * P, :])]
    loads.append((weight("W1c", DE, D)[:], a["L2_gnn_W1"][2 * P:2 * P + DE, :]))
    k.gtok = k.sb("gtok", [P, 1])
    loads.append((k.gtok[:], a["L1_gnn_g_token"].rearrange("a d -> d a")))
    k.w = w

    rows = {"out1": "L0_gnn_out1_b", "out2": "L0_gnn_out2_b", "Wg": "L1_gnn_Wg_in_b", "ln1g": "L1_gnn_ln1_g",
            "ln1b": "L1_gnn_ln1_b", "msg": "L1_gnn_msg_b", "lin": "L1_gnn_lin_b", "ln2g": "L1_gnn_ln2_g",
            "ln2b": "L1_gnn_ln2_b", "phi": "L1_gnn_Wphi", "ln3g": "L1_gnn_ln3_g", "ln3b": "L1_gnn_ln3_b",
            "ffn1": "L1_gnn_ffn_b1", "ffn2": "L1_gnn_ffn_b2", "b2": "L2_gnn_b2", "bn": "L2_gnn_bn",
            "gamma": "L2_gnn_gamma", "beta": "L2_gnn_beta", "s1": "L3_gnn_b1", "s2": "L3_gnn_b2",
            "s3": "L3_gnn_b3", "bn1g": "L3_gnn_bn1_g", "bn1b": "L3_gnn_bn1_b", "bn2g": "L3_gnn_bn2_g",
            "bn2b": "L3_gnn_bn2_b", "lng": "L3_gnn_ln_g", "lnb": "L3_gnn_ln_b"}
    k.r = {}
    for n, s in rows.items():
        k.r[n] = k.sb("r_" + n, [P, a[s].shape[0]])
        loads.append((k.r[n][:], a[s].partition_broadcast(P)))
    k.r["ab"] = k.sb("r_ab", [P, 2 * D])
    k.r["qky"] = k.sb("r_qky", [P, 2 * D])
    k.r["none"] = k.sb("r_none", [P, D])
    loads.append((k.r["ab"][:, 0:D], a["L2_gnn_b1"].partition_broadcast(P)))
    loads.append((k.r["qky"][:, D:2 * D], a["L1_gnn_Wy_b"].partition_broadcast(P)))
    k.eps = k.sb("eps", [P, 1])
    loads.append((k.eps[:], a["L1_gnn_eps"].partition_broadcast(P)))
    k.pad_meta = k.sb("pad_meta", [P, 8, 2])
    k.iota_tile = k.sb("iota_tile", [P, J], F32, k.early)
    k.tile_max = k.sb("tile_max", [P, J], F32, k.early)
    k.tile_deg = k.sb("tile_deg", [P, J], F32, k.early)
    k.att = k.sb("att", [P, D + DE, 4], F32, k.early)
    loads.append((k.att[:], a["L0_gnn_attn_W"].partition_broadcast(P)))
    loads.append((k.att_b[:], a["L0_gnn_attn_b"].partition_broadcast(P)))
    loads.append((k.X[:, 0:NB - 1, :], a["x"][0:(NB - 1) * P, :].rearrange("(b p) f -> p b f", p=P)))

    cleared, loaded, iotas, made = (k.sem(s) for s in ("cleared", "loaded", "iotas", "made"))
    with k.block() as block:
        @block.sync
        def _(sp):
            for dst, src in loads:
                sp.dma_start(dst, src).then_inc(loaded, 16)
            sp.wait_ge(cleared, 1)
            sp.dma_start(k.X[0:LAST, NB - 1, :], a["x"][(NB - 1) * P:N, :]).then_inc(loaded, 16)
            sp.wait_ge(loaded, 16 * (len(loads) + 1))

        @block.gpsimd
        def _(pool):
            nc.gpsimd.iota(k.iota_row[:], [[1, P]], base=0, channel_multiplier=0,
                           allow_small_or_imprecise_dtypes=True).then_inc(iotas, 1)
            nc.gpsimd.iota(k.iota_tile[:], [[1, J]], base=0, channel_multiplier=0,
                           allow_small_or_imprecise_dtypes=True).then_inc(iotas, 1)
            nc.gpsimd.iota(k.iota_col[:], [[1, 1]], base=0, channel_multiplier=1,
                           allow_small_or_imprecise_dtypes=True).then_inc(iotas, 1)

        @block.vector
        def _(dve):
            dve.memset(k.X[:, NB - 1, :], 0.0).then_inc(cleared, 1)
            dve.memset(k.ones[:], 1.0)
            dve.memset(k.ones_h[:], 1.0)
            dve.memset(k.r["ab"][:, D:2 * D], 0.0)
            dve.memset(k.r["qky"][:, 0:D], 0.0)
            dve.memset(k.r["none"][:], 0.0)
            dve.memset(k.pad_meta[:, :, 0:1], -1.0)
            dve.memset(k.pad_meta[:, :, 1:2], 0.0)
            dve.wait_ge(iotas, 3)
            dve.tensor_scalar(k.ident[:], k.iota_row[:], k.iota_col[:], None, ALU.is_equal)
            dve.tensor_scalar(k.ident_h[:], k.iota_row[:], k.iota_col[:], None, ALU.is_equal)
            dve.tensor_scalar(k.before[:], k.iota_row[:], k.iota_col[:], None, ALU.is_gt)
            dve.tensor_scalar(k.before_h[:], k.iota_row[:], k.iota_col[:], None, ALU.is_gt)
            dve.tensor_scalar(k.last_rows[:], k.iota_col[:], float(LAST), None, ALU.is_lt)
            dve.wait_ge(loaded, 16 * (len(loads) + 1))
            dve.tensor_reduce(k.att_m[:], k.att[:], AX, ALU.add).then_inc(made, 1)
            dve.tensor_reduce(k.att_bm[:], k.att_b[:], AX, ALU.add).then_inc(made, 1)
            dve.wait_ge(made, 2)
            dve.tensor_scalar(k.att_m[:], k.att_m[:], 0.25, None, ALU.mult)
            dve.tensor_scalar(k.att_bm[:], k.att_bm[:], 0.25, None, ALU.mult)



def order_stage(k, o, key_i, other_i, beside=None):
    nc, n = k.nc, o.name
    keys_in, blocks, mask1, tot, mask2, placed, step, tot_free, masks_used, sums_used, base = (
        k.sem(f"{n}_{s}") for s in ("keys_in", "blocks", "mask1", "totals", "mask2", "placed", "step",
                                    "tot_free", "masks_used", "sums_used", "base"))
    H = EC // 2
    JH = J // 2
    with ExitStack() as c:
        ki = k.sb(n + "_ki", [EP, EC], I32, c)
        oi = k.sb(n + "_oi", [EP, EC], I32, c)
        bi = k.sb(n + "_bi", [EP, EC], I32, c)
        bf = k.sb(n + "_bf", [EP, EC], F32, c)
        mask = k.sb(n + "_mask", [EP, 2, EC], BF16, c)
        pick = k.sb(n + "_pick", [EP, 2 * NB - 1], BF16, c)
        totals = k.sb(n + "_totals", [NB, EC], F32, c)
        upto = k.sb(n + "_upto", [NB, EC], F32, c)
        first = k.sb(n + "_first", [NB, EC], F32, c)
        onesr = k.sb(n + "_onesr", [NB, EC], F32, c)
        tiles_i = k.sb(n + "_tiles_i", [NB, 1], I32, c)
        tiles = k.sb(n + "_tiles", [NB, 1], F32, c)
        start = k.sb(n + "_start", [NB, 2], F32, c)
        past = k.sb(n + "_past", [NB, J], BF16, c)
        rank = k.sb(n + "_rank", [EP, EC], F32, c)
        part = k.sb(n + "_part", [EP, EC], F32, c)
        low = k.sb(n + "_low", [EP, EC], I32, c)
        pt = k.ps(n + "_pt", [P, 2, 512], c)
        pr = k.ps(n + "_pr", [P, 2, 2, 512], c)
        pb = k.ps(n + "_pb", [P, 2, 512], c)
        beside = beside and beside(c)
        with k.block() as block:
            @block.sync
            def _(sp):
                sp.dma_start(ki[:], key_i.rearrange("(p c) -> p c", p=EP)).then_inc(keys_in, 16)
                sp.dma_start(oi[:], other_i.rearrange("(p c) -> p c", p=EP)).then_inc(keys_in, 16)
                sp.wait_ge(keys_in, 32)
                if beside:
                    beside.sync(sp)

            if beside:
                @block.gpsimd
                def _(pool):
                    beside.gpsimd(pool)

                @block.scalar
                def _(act):
                    beside.scalar(act)

            @block.tensor
            def _(pe):
                for b in range(NB):
                    pe.wait_ge(mask1, b + 1)
                    for h in range(2):
                        mm = pe.matmul(pt[0:NB, h, 0:H], pick[:, NB - 1 - b:2 * NB - 1 - b],
                                       mask[:, b % 2, h * H:(h + 1) * H], start=(b == 0), stop=(b == NB - 1))
                    mm.then_inc(masks_used, 1)
                pe.wait_ge(blocks, 1)
                pe.matmul(pb[0:NB, 0, 0:1], k.before[0:NB, 0:NB], tiles[:], start=True, stop=True).then_inc(base, 1)
                pe.wait_ge(blocks, 2)
                for h in range(2):
                    mm = pe.matmul(pb[:, h, 0:JH], k.ones_h[0:NB, :], past[:, h * JH:(h + 1) * JH],
                                   start=True, stop=True)
                mm.then_inc(base, 1)
                for b in range(NB):
                    pe.wait_ge(mask2, b + 1)
                    if b >= 2:
                        pe.wait_ge(sums_used, b - 1)
                    for h in range(2):
                        pe.matmul(pr[0:EP, b % 2, h, 0:H], k.before_h[0:EP, 0:EP],
                                  mask[:, b % 2, h * H:(h + 1) * H], start=True, stop=False)
                        mm = pe.matmul(pr[0:EP, b % 2, h, 0:H], k.ident[0:NB, b:b + 1].to_broadcast([NB, EP]),
                                       first[:, h * H:(h + 1) * H], start=False, stop=True)
                    mm.then_inc(placed, 1)

            @block.vector
            def _(dve):
                done = [0]

                def link(ins):
                    done[0] += 1
                    ins.then_inc(step, 1)
                    dve.wait_ge(step, done[0])

                if beside:
                    beside.vector(dve)
                dve.memset(pick[:], 0.0)
                dve.memset(rank[:], 0.0)
                link(dve.memset(onesr[:], 1.0))
                link(dve.memset(pick[:, NB - 1:NB], 1.0))
                dve.wait_ge(keys_in, 32)
                link(dve.tensor_scalar(bi[:], ki[:], 7, None, ALU.arith_shift_right))
                link(dve.tensor_scalar(low[:], ki[:], P - 1, None, ALU.bitwise_and))
                link(dve.tensor_copy(bf[:], bi[:]))
                dve.tensor_copy(o.meta[:, :, 0], low[:])
                dve.tensor_copy(o.meta[:, :, 1], oi[:])
                for b in range(NB):
                    if b >= 2:
                        dve.wait_ge(masks_used, b - 1)
                    dve.tensor_scalar(mask[:, b % 2, :], bf[:], float(b), None, ALU.is_equal).then_inc(mask1, 1)
                dve.wait_ge(masks_used, NB)
                link(dve.tensor_copy(totals[:].rearrange("b (h c) -> b h c", h=2), pt[0:NB, :, 0:H]))
                link(dve.tensor_tensor_scan(upto[:], onesr[:], totals[:], 0.0, ALU.mult, ALU.add))
                link(dve.tensor_tensor(first[:], upto[:], totals[:], ALU.subtract))
                link(dve.tensor_scalar(tiles[:], upto[:, EC - 1:EC], float(2 * P - 1), None, ALU.add))
                link(dve.tensor_copy(tiles_i[:], tiles[:]))
                link(dve.tensor_scalar(tiles_i[:], tiles_i[:], 8, None, ALU.arith_shift_right))
                link(dve.tensor_scalar(tiles_i[:], tiles_i[:], 1, None, ALU.arith_shift_left))
                dve.tensor_copy(tiles[:], tiles_i[:]).then_inc(blocks, 1)
                dve.wait_ge(base, 1)
                link(dve.tensor_copy(start[:, 0:1], pb[0:NB, 0, 0:1]))
                link(dve.tensor_tensor(start[:, 1:2], start[:, 0:1], tiles[:], ALU.add))
                dve.tensor_scalar(past[:], k.iota_tile[0:NB, :], start[:, 1:2], None, ALU.is_ge).then_inc(blocks, 1)
                link(dve.tensor_scalar(start[:, 0:1], start[:, 0:1], float(P), None, ALU.mult))
                link(dve.tensor_scalar(first[:], first[:], start[:, 0:1], None, ALU.add))
                dve.wait_ge(base, 2)
                link(dve.tensor_scalar(o.block_f[:].rearrange("p (h j) -> p h j", h=2), pb[:, :, 0:JH],
                                       float(NB - 1), None, ALU.min))
                dve.tensor_copy(o.block_i[:], o.block_f[:].rearrange("p (n t) -> p n t", t=2)[:, :, 0])

                def make_mask(b):
                    if b >= 2:
                        dve.wait_ge(placed, b - 1)
                    dve.tensor_scalar(mask[:, b % 2, :], bf[:], float(b), None, ALU.is_equal).then_inc(mask2, 1)

                make_mask(0)
                for b in range(NB):
                    if b + 1 < NB:
                        make_mask(b + 1)
                    dve.wait_ge(placed, b + 1)
                    dve.wait_ge(mask2, b + 1)
                    ins = dve.tensor_tensor(part[:].rearrange("p (h c) -> p h c", h=2), pr[0:EP, b % 2, :, 0:H],
                                            mask[:, b % 2, :].rearrange("p (h c) -> p h c", h=2), ALU.mult)
                    ins.then_inc(sums_used, 1)
                    dve.wait_ge(sums_used, b + 1)
                    link(dve.tensor_tensor(rank[:], rank[:], part[:], ALU.add))
                link(dve.tensor_copy(bi[:], rank[:]))
                link(dve.tensor_scalar(low[:], bi[:], P - 1, None, ALU.bitwise_and))
                link(dve.tensor_scalar(bi[:], bi[:], 7, None, ALU.arith_shift_right))
                link(dve.tensor_scalar(low[:], low[:], J, None, ALU.mult))
                dve.tensor_tensor(o.row[:], low[:], bi[:], ALU.add)


CW = 8


class FeatureScatter:

    def __init__(self, k, o, edge_attr, c):
        self.k, self.o = k, o
        self.attr = edge_attr.rearrange("(p c) f -> p c f", p=EP)
        self.blank_made, self.blanked, self.staged, self.begun = (
            k.sem(s) for s in ("f_blank_made", "f_blanked", "f_staged", "f_begun"))
        self.features_in = [k.sem(f"f_features_in{p}") for p in range(2)]
        self.sent = [k.sem(f"f_sent{p}") for p in range(2)]
        self.blank = k.sb("f_blank", [P, 8, RW], F32, c)
        self.rows = k.sb("f_rows", [EP, 2, CW, RW], F32, c)
        self.at = k.sb("f_at", [EP, 2, CW], I32, c)

    def sync(self, sp):
        sp.wait_ge(self.blank_made, 3)
        sp.dma_start(self.o.rows_dram.rearrange("(p r j) w -> p r (j w)", p=P, j=8),
                     self.blank[:].rearrange("p j w -> p (j w)").unsqueeze(1).to_broadcast([P, J // 8, 8 * RW])
                     ).then_inc(self.blanked, 16)

        def body(i, first):
            for p in range(2):
                if not first:
                    sp.wait_ge(self.sent[p], 16 * CW * i)
                sp.dma_start(self.rows[:, p, :, 0:DE], self.attr[:, ds(i * 2 * CW + p * CW, CW), :]
                             ).then_inc(self.features_in[p], 16)
        steps(sp, EC // (2 * CW), body)

    def scalar(self, act):
        def body(i, first):
            for p in range(2):
                if not first:
                    act.wait_ge(self.sent[p], 16 * CW * i)
                c0 = i * 2 * CW + p * CW
                act.copy(self.at[:, p, :], self.o.row[:, ds(c0, CW)]).then_inc(self.staged, 1)
                act.copy(self.rows[:, p, :, DE:RW], self.o.meta[:, ds(c0, CW), :]).then_inc(self.staged, 1)
        steps(act, EC // (2 * CW), body)

    def vector(self, dve):
        dve.memset(self.blank[:, :, 0:DE], 0.0).then_inc(self.blank_made, 1)
        dve.memset(self.blank[:, :, DE:DE + 1], -1.0).then_inc(self.blank_made, 1)
        dve.memset(self.blank[:, :, DE + 1:RW], 0.0).then_inc(self.blank_made, 1)

    def gpsimd(self, pool):
        pool.wait_ge(self.blanked, 16)

        def body(i, first):
            for p in range(2):
                pool.wait_ge(self.features_in[p], 16 * (i + 1))
                pool.wait_ge(self.staged, 4 * i + 2 * p + 2)
                pool.sem_inc(self.begun, 1)
                for q in range(CW):
                    pool.indirect_dma_start(
                        self.o.rows_dram, bass.IndirectOffsetOnAxis(ap=self.at[:, p, q:q + 1], axis=0),
                        self.rows[:, p, q, :], None).then_inc(self.sent[p], 16)
        steps(pool, EC // (2 * CW), body)
        for p in range(2):
            pool.wait_ge(self.sent[p], 16 * EC // 2)


def blank_ids_stage(k, so):
    blanked = k.sem("bi_blanked")
    with k.block() as block:
        @block.sync
        def _(sp):
            sp.dma_start(so.ids_dram.rearrange("(p r j) w -> p r (j w)", p=P, j=8),
                         k.pad_meta[:, 0:8, :].rearrange("p j w -> p (j w)").unsqueeze(1)
                         .to_broadcast([P, J // 8, 16])).then_inc(blanked, 16)
            sp.wait_ge(blanked, 16)


class IdScatter:

    def __init__(self, k, so, c, name, lo, hi):
        self.so, self.lo, self.hi = so, lo, hi
        self.staged, self.begun = k.sem(name + "_staged"), k.sem(name + "_begun")
        self.sent = [k.sem(f"{name}_sent{p}") for p in range(2)]
        self.at = k.sb(name + "_at", [EP, 2, CW], I32, c)
        self.ids = k.sb(name + "_ids", [EP, 2, CW, 2], F32, c)

    def gpsimd(self, pool):
        def body(i, first):
            for p in range(2):
                if not first:
                    pool.wait_ge(self.sent[p], 16 * CW * i)
                c0 = i * 2 * CW + (2 * CW * self.lo + p * CW)
                pool.tensor_copy(self.at[:, p, :], self.so.row[:, ds(c0, CW)]).then_inc(self.staged, 1)
                pool.tensor_copy(self.ids[:, p], self.so.meta[:, ds(c0, CW), :]).then_inc(self.staged, 1)
                pool.wait_ge(self.staged, 4 * i + 2 * p + 2)
                pool.sem_inc(self.begun, 1)
                for q in range(CW):
                    pool.indirect_dma_start(
                        self.so.ids_dram, bass.IndirectOffsetOnAxis(ap=self.at[:, p, q:q + 1], axis=0),
                        self.ids[:, p, q, :], None).then_inc(self.sent[p], 16)
        steps(pool, self.hi - self.lo, body)
        for p in range(2):
            pool.wait_ge(self.sent[p], 16 * CW * (self.hi - self.lo))



def score_stage(k, o, ids):
    nc = k.nc
    taken, scored, spread, penalties, sums, meta_kept, products, maxima = (k.sem("sc_" + s) for s in (
        "taken", "scored", "spread", "penalties", "sums", "meta_kept", "products", "maxima"))
    features_in = [k.sem(f"sc_features_in{p}") for p in range(Q)]
    rows_dram = o.rows_dram.rearrange("(e j) w -> e j w", e=P)
    with ExitStack() as c:
        ids = ids(c)
        rows = k.sb("sc_rows", [P, Q, G, RW], F32, c)
        prod = k.sb("sc_prod", [P, Q, G, DE], F32, c)
        sg = k.sb("sc_sg", [P, Q, G], F32, c)
        lo = k.sb("sc_lo", [P, Q, G], BF16, c)
        pen = k.sb("sc_pen", [P, 2, G, P], F32, c)
        tmp = k.sb("sc_tmp", [P, 2, G, P], F32, c)
        node_bc = k.ps("sc_node", [P, 4, 512], c)
        score_bc = k.ps("sc_score", [P, 4, 512], c)
        with k.block() as block:
            @block.sync
            def _(sp):
                def body(i, first):
                    for p in range(Q):
                        after(sp, taken, i, p, Q, first, each=2)
                        after(sp, products, i, p, Q, first)
                        sp.dma_start(rows[:, p], rows_dram[:, ds(i * STEP + p * G, G), :]).then_inc(features_in[p], 16)
                steps(sp, LOOPS, body)

            @block.gpsimd
            def _(pool):
                ids.gpsimd(pool)

            @block.tensor
            def _(pe):
                def body(i, first):
                    for p in range(Q):
                        pe.wait_ge(taken, (Q * i + p + 1) * 2)
                        pe.wait_ge(scored, Q * i + p + 1)
                        after(pe, penalties, i, p, 4, first)
                        after(pe, sums, i, p, 4, first)
                        for g in range(G):
                            pe.matmul(node_bc[:, p, g * P:(g + 1) * P], lo[:, p, g:g + 1].to_broadcast([P, P]),
                                      k.ident_h[:], start=True, stop=True)
                            mm = pe.matmul(score_bc[:, p, g * P:(g + 1) * P], sg[:, p, g:g + 1].to_broadcast([P, P]),
                                           k.ident[:], start=True, stop=True)
                        mm.then_inc(spread, 1)
                steps(pe, LOOPS, body)

            @block.scalar
            def _(act):
                def body(i, first):
                    for p in range(Q):
                        act.wait_ge(features_in[p], 16 * (i + 1))
                        nc.scalar.copy(o.slot[:, ds(i * STEP + p * G, G), :], rows[:, p, :, DE:RW]).then_inc(taken, 1)
                        after(act, spread, i, p, Q, first)
                        nc.scalar.copy(lo[:, p], rows[:, p, :, DE]).then_inc(taken, 1)
                    for p in range(Q):
                        act.wait_ge(scored, Q * i + p + 1)
                        nc.scalar.copy(k.scores[:, ds(i * STEP + p * G, G)], sg[:, p, :]).then_inc(meta_kept, 1)
                steps(act, LOOPS, body)

            @block.vector
            def _(dve):
                w2 = k.att_m[:, D:D + DE].unsqueeze(1).to_broadcast([P, G, DE])

                def body(i, first):
                    for p in range(Q):
                        dve.wait_ge(features_in[p], 16 * (i + 1))
                        dve.tensor_tensor(prod[:, p], rows[:, p, :, 0:DE], w2, ALU.mult).then_inc(products, 1)
                    for p in range(Q):
                        after(dve, meta_kept, i, p, Q, first)
                        after(dve, spread, i, p, Q, first)
                        dve.wait_ge(products, Q * i + p + 1)
                        dve.tensor_reduce(sg[:, p], prod[:, p], AX, ALU.add).then_inc(scored, 1)
                    for p in range(Q):
                        dve.wait_ge(spread, Q * i + p + 1)
                        dve.tensor_scalar(pen[:, p % 2], node_bc[:, p].rearrange("p (g e) -> p g e", g=G), k.iota_col[:],
                                          -BIG, ALU.not_equal, ALU.mult).then_inc(penalties, 1)
                        dve.wait_ge(penalties, Q * i + p + 1)
                        dve.tensor_tensor(tmp[:, p % 2], score_bc[:, p].rearrange("p (g e) -> p g e", g=G),
                                          pen[:, p % 2], ALU.add).then_inc(sums, 1)
                        dve.tensor_reduce(k.tile_deg[:, ds(i * STEP + p * G, G)], pen[:, p % 2], AX, ALU.add
                                          ).then_inc(maxima, 1)
                        dve.wait_ge(sums, Q * i + p + 1)
                        dve.tensor_reduce(k.tile_max[:, ds(i * STEP + p * G, G)], tmp[:, p % 2], AX, ALU.max
                                          ).then_inc(maxima, 1)
                steps(dve, LOOPS, body)


def node_maximum_stage(k, o):
    nc = k.nc
    sel, part, step, node = (k.sem("nm_" + s) for s in ("sel", "part", "step", "node"))
    with ExitStack() as c:
        one = k.sb("nm_one", [P, J], F32, c)
        two = k.sb("nm_two", [P, J], F32, c)
        prod = k.sb("nm_prod", [P, NB, D], F32, c)
        mt = k.sb("nm_mt", [P, NB], F32, c)
        with k.block() as block:
            @block.vector
            def _(dve):
                n = [0]

                def link(ins):
                    n[0] += 1
                    ins.then_inc(step, 1)
                    dve.wait_ge(step, n[0])

                link(dve.tensor_scalar(k.tile_deg[:], k.tile_deg[:], 1.0 / BIG, float(P), ALU.mult, ALU.add))
                link(dve.tensor_tensor(prod[:], k.X[:], over_blocks(k.att_m[:, 0:D], [P, NB, D]), ALU.mult))
                link(dve.tensor_reduce(mt[:], prod[:], AX, ALU.add))
                link(dve.tensor_scalar(k.mx[:, :, 1], mt[:], k.att_bm[:], None, ALU.add))
                with dve.Fori(0, NB) as b:
                    dve.tensor_scalar(one[:], o.block_f[:], k.iota_row[:, ds(b, 1)], -BIG, ALU.not_equal, ALU.mult
                                      ).then_inc(sel, 1)
                    dve.wait_ge(sel, 4 * b + 1)
                    dve.tensor_tensor(two[:], one[:], k.tile_max[:], ALU.add).then_inc(sel, 1)
                    dve.wait_ge(sel, 4 * b + 2)
                    dve.tensor_reduce(mt[:, ds(b, 1)], two[:], AX, ALU.max).then_inc(part, 1)
                    dve.scalar_tensor_tensor(one[:], o.block_f[:], k.iota_row[:, ds(b, 1)], k.tile_deg[:],
                                             ALU.is_equal, ALU.mult).then_inc(sel, 1)
                    dve.wait_ge(sel, 4 * b + 3)
                    dve.tensor_reduce(k.deg[:, ds(b, 1)], one[:], AX, ALU.add).then_inc(sel, 1)
                    dve.wait_ge(sel, 4 * b + 4)
                dve.wait_ge(part, NB)
                link(dve.tensor_tensor(k.mx[:, :, 0], mt[:], k.mx[:, :, 1], ALU.add))
                link(dve.tensor_scalar(k.deg[:], k.deg[:], 1.0, None, ALU.max))
                dve.reciprocal(k.deg[:], k.deg[:]).then_inc(node, 1)
                dve.wait_ge(node, 1)


def blocks_of(k, eng, o, i):
    registers = [eng.alloc_register(f"block{k.taken + n}") for n in range(STEP // 2)]
    k.taken += STEP // 2
    k.registers += [(eng, reg) for reg in registers]
    eng.load(registers, o.block_i[0:1, ds(i * (STEP // 2), STEP // 2)])
    return [eng.snap(reg, donate=True, min_val=0, max_val=NB - 1) for reg in registers]


def add_pairs(dve, acc, blocks, i, p, first, added, sums):
    for q in range(G // 2):
        n = (Q * i + p) * (G // 2) + q
        b = blocks[p * (G // 2) + q]
        if q or p or not first:
            dve.wait_ge(added, n)
        dve.tensor_tensor(acc[:, ds(b, 1), :], acc[:, ds(b, 1), :], sums(q).unsqueeze(1), ALU.add).then_inc(added, 1)


def sum_pairs(pe, oh, rows, sums):
    for g in range(G):
        mm = pe.matmul(sums(g // 2), oh(g), rows(g), start=(g % 2 == 0), stop=(g % 2 == 1))
    return mm


def spread_nodes(pe, k, bank, lo):
    for g in range(G):
        mm = pe.matmul(bank[:, g * P:(g + 1) * P], lo[:, g:g + 1].to_broadcast([P, P]), k.ident_h[:], start=True, stop=True)
    return mm


def attention_sum_stage(k, o, acc, ids):
    nc = k.nc
    (cleared, staged, spread, onehots, looked_up, exponents, weights, weighted, summed, added, ones_put,
     shifted) = (k.sem("as_" + s) for s in ("cleared", "staged", "spread", "onehots", "looked_up", "exponents",
                                            "weights", "weighted", "summed", "added", "ones_put", "shifted"))
    features_in = [k.sem(f"as_features_in{p}") for p in range(Q)]
    rows_dram = o.rows_dram.rearrange("(e j) w -> e j w", e=P)
    with ExitStack() as c:
        ids = ids(c)
        rows = k.sb("as_rows", [P, Q, G, RW], F32, c)
        lo = k.sb("as_lo", [P, Q, G], BF16, c)
        lof = k.sb("as_lof", [P, Q, G], F32, c)
        sg = k.sb("as_sg", [P, Q, G], F32, c)
        oht = k.sb("as_oht", [P, Q, G, P], F32, c)
        ohw = k.sb("as_ohw", [P, Q, G, P], F32, c)
        d1 = k.sb("as_d1", [P, Q, G], F32, c)
        d2 = k.sb("as_d2", [P, Q, G], F32, c)
        wt = k.sb("as_wt", [P, Q, G], F32, c)
        node_bc = k.ps("as_node", [P, 2, 512], c)
        found = k.ps("as_found", [P, 2, 512], c)
        sums = k.ps("as_sums", [P, 4, 512], c)
        with k.block() as block:
            @block.sync
            def _(sp):
                def body(i, first):
                    for p in range(Q):
                        after(sp, summed, i, p, Q, first)
                        sp.dma_start(rows[:, p], rows_dram[:, ds(i * STEP + p * G, G), :]).then_inc(features_in[p], 16)
                steps(sp, LOOPS, body)

            @block.gpsimd
            def _(pool):
                ids.gpsimd(pool)

            @block.tensor
            def _(pe):
                def body(i, first):
                    blocks = blocks_of(k, pe, o, i)
                    for p in range(Q):
                        pe.wait_ge(staged, (Q * i + p + 1) * 3)
                        after(pe, onehots, i, p, 2, first)
                        spread_nodes(pe, k, node_bc[:, p % 2], lo[:, p]).then_inc(spread, 1)
                    for p in range(Q):
                        pe.wait_ge(onehots, Q * i + p + 1)
                        after(pe, exponents, i, p, 2, first)
                        for g in range(G):
                            b = blocks[(p * G + g) // 2]
                            mm = pe.matmul(found[:, p % 2, 2 * g:2 * g + 2], oht[:, p, g, :], k.mx[:, ds(b, 1), :],
                                           start=True, stop=True)
                        mm.then_inc(looked_up, 1)
                    for p in range(Q):
                        pe.wait_ge(weighted, Q * i + p + 1)
                        pe.wait_ge(ones_put, Q * i + p + 1)
                        after(pe, added, i, p, 4, first, each=G // 2)
                        sum_pairs(pe, lambda g: ohw[:, p, g, :], lambda g: rows[:, p, g, :],
                                  lambda q: sums[:, p, q * RW:(q + 1) * RW]).then_inc(summed, 1)
                steps(pe, LOOPS, body)

            @block.scalar
            def _(act):
                def body(i, first):
                    for p in range(Q):
                        after(act, spread, i, p, Q, first)
                        after(act, exponents, i, p, Q, first)
                        after(act, weighted, i, p, Q, first)
                        at = ds(i * STEP + p * G, G)
                        nc.scalar.copy(lo[:, p], o.slot[:, at, 0]).then_inc(staged, 1)
                        nc.scalar.copy(lof[:, p], o.slot[:, at, 0]).then_inc(staged, 1)
                        nc.scalar.copy(sg[:, p], k.scores[:, at]).then_inc(staged, 1)
                    for p in range(Q):
                        act.wait_ge(features_in[p], 16 * (i + 1))
                        nc.scalar.activation(rows[:, p, :, DE + 1:RW], rows[:, p, :, DE + 1:RW], ACT.Copy, bias=1.0, scale=0.0
                                             ).then_inc(ones_put, 1)
                        act.wait_ge(exponents, Q * i + p + 1)
                        nc.scalar.activation(wt[:, p], d2[:, p], ACT.Exp).then_inc(weights, 1)
                steps(act, LOOPS, body)

            @block.vector
            def _(dve):
                dve.memset(acc[:], 0.0).then_inc(cleared, 1)
                dve.wait_ge(cleared, 1)

                def body(i, first):
                    blocks = blocks_of(k, dve, o, i)
                    for p in range(Q):
                        dve.wait_ge(spread, Q * i + p + 1)
                        after(dve, looked_up, i, p, Q, first)
                        dve.tensor_scalar(oht[:, p], node_bc[:, p % 2].rearrange("p (g e) -> p g e", g=G), k.iota_col[:],
                                          None, ALU.is_equal).then_inc(onehots, 1)
                    for p in range(Q):
                        f = found[:, p % 2, 0:2 * G].rearrange("p (g t) -> p g t", t=2)
                        dve.wait_ge(looked_up, Q * i + p + 1)
                        dve.tensor_tensor(d1[:, p], sg[:, p], f[:, :, 1], ALU.add).then_inc(shifted, 1)
                        dve.wait_ge(shifted, Q * i + p + 1)
                        after(dve, weights, i, p, Q, first)
                        dve.tensor_tensor(d2[:, p], d1[:, p], f[:, :, 0], ALU.subtract).then_inc(exponents, 1)
                    for p in range(Q):
                        dve.wait_ge(weights, Q * i + p + 1)
                        after(dve, summed, i, p, Q, first)
                        for g in range(G):
                            ins = dve.tensor_scalar(ohw[:, p, g, :], k.iota_row[:], lof[:, p, g:g + 1],
                                                    wt[:, p, g:g + 1], ALU.is_equal, ALU.mult)
                        ins.then_inc(weighted, 1)
                    for p in range(Q):
                        dve.wait_ge(summed, Q * i + p + 1)
                        add_pairs(dve, acc, blocks, i, p, first, added, lambda q: sums[:, p, q * RW:(q + 1) * RW])
                steps(dve, LOOPS, body)



def far_ends_stage(k, o, so):
    slots_in = k.sem("fe_slots_in")
    with k.block() as block:
        @block.sync
        def _(sp):
            sp.dma_start(so.slot[:], so.ids_dram.rearrange("(e j) w -> e j w", e=P)).then_inc(slots_in, 16)

        @block.vector
        def _(dve):
            dve.tensor_copy(o.far_i[:], o.slot[:, :, 1])
            dve.tensor_copy(o.lo[:], o.slot[:, :, 0])
            dve.wait_ge(slots_in, 16)
            dve.tensor_copy(so.far_i[:], so.slot[:, :, 1])
            dve.tensor_copy(so.lo[:], so.slot[:, :, 0])


def stage_ids(act, o, far, i, p):
    return act.copy(far[:, p], o.far_i[:, ds(i * STEP + p * G, G)])


def gather_rows(pool, table, rows, far, p, rows_in):
    for g in range(G):
        pool.indirect_dma_start(rows[:, p, g, :], None, table,
                                bass.IndirectOffsetOnAxis(ap=far[:, p, g:g + 1], axis=0)).then_inc(rows_in[p], 16)


def end_onehots(dve, k, o, oh, i, p):
    return dve.tensor_tensor(oh[:, p], over_blocks(k.iota_row[:], [P, G, P]),
                             wide(o.lo[:, ds(i * STEP + p * G, G)], G, [P, G, P]), ALU.is_equal)


def gather_sum_stage(k, name, o, table, acc):
    nc = k.nc
    cleared, staged, onehots, summed, added, begun = (k.sem(f"{name}_{s}") for s in (
        "cleared", "staged", "onehots", "summed", "added", "begun"))
    rows_in = [k.sem(f"{name}_rows_in{p}") for p in range(Q)]
    with ExitStack() as c:
        rows = k.sb(name + "_rows", [P, Q, G, D], F32, c)
        far = k.sb(name + "_far", [P, Q, G], I32, c)
        oh = k.sb(name + "_oh", [P, Q, G, P], F32, c)
        sums = k.ps(name + "_sums", [P, Q, 512], c)
        with k.block() as block:
            @block.scalar
            def _(act):
                def body(i, first):
                    for p in range(Q):
                        if not first:
                            act.wait_ge(rows_in[p], 16 * G * i)
                        stage_ids(act, o, far, i, p).then_inc(staged, 1)
                steps(act, LOOPS, body)

            @block.gpsimd
            def _(pool):
                def body(i, first):
                    for p in range(Q):
                        pool.wait_ge(staged, Q * i + p + 1)
                        after(pool, summed, i, p, Q, first)
                        pool.sem_inc(begun, 1)
                        gather_rows(pool, table, rows, far, p, rows_in)
                steps(pool, LOOPS, body)

            @block.tensor
            def _(pe):
                def body(i, first):
                    for p in range(Q):
                        pe.wait_ge(onehots, Q * i + p + 1)
                        pe.wait_ge(rows_in[p], 16 * G * (i + 1))
                        after(pe, added, i, p, Q, first, each=G // 2)
                        sum_pairs(pe, lambda g: oh[:, p, g, :], lambda g: rows[:, p, g, :],
                                  lambda q: sums[:, p, q * P:(q + 1) * P]).then_inc(summed, 1)
                steps(pe, LOOPS, body)

            @block.vector
            def _(dve):
                dve.memset(acc[:], 0.0).then_inc(cleared, 1)
                dve.wait_ge(cleared, 1)

                def body(i, first):
                    blocks = blocks_of(k, dve, o, i)
                    for p in range(Q):
                        after(dve, summed, i, p, Q, first)
                        end_onehots(dve, k, o, oh, i, p).then_inc(onehots, 1)
                    for p in range(Q):
                        dve.wait_ge(summed, Q * i + p + 1)
                        add_pairs(dve, acc, blocks, i, p, first, added, lambda q: sums[:, p, q * P:(q + 1) * P])
                steps(dve, LOOPS, body)



VW = 3 * DE


def tanh_stage(k, o, table, qky, edges_dram):
    nc = k.nc
    (staged, spread, onehots, looked_up, pre, tanhs, prods, scored, begun) = (k.sem("th_" + s) for s in (
        "staged", "spread", "onehots", "looked_up", "pre", "tanhs", "prods", "scored", "begun"))
    rows_in = [k.sem(f"th_rows_in{p}") for p in range(Q)]
    stored = [k.sem(f"th_stored{p}") for p in range(Q)]
    out_rows = edges_dram.rearrange("(e j) w -> e j w", e=P)
    with ExitStack() as c:
        rows = k.sb("th_rows", [P, Q, G, VW], F32, c)
        far = k.sb("th_far", [P, Q, G], I32, c)
        lo = k.sb("th_lo", [P, Q, G], BF16, c)
        oht = k.sb("th_oht", [P, Q, G, P], F32, c)
        sumqk = k.sb("th_sum", [P, Q, G, DE], F32, c)
        prod = k.sb("th_prod", [P, Q, G, DE], F32, c)
        node_bc = k.ps("th_node", [P, 4, 512], c)
        query = k.ps("th_query", [P, 4, 512], c)
        with k.block() as block:
            @block.scalar
            def _(act):
                def body(i, first):
                    for p in range(Q):
                        if not first:
                            act.wait_ge(rows_in[p], 16 * G * i)
                        after(act, spread, i, p, Q, first)
                        stage_ids(act, o, far, i, p).then_inc(staged, 1)
                        nc.scalar.copy(lo[:, p], o.lo[:, ds(i * STEP + p * G, G)]).then_inc(staged, 1)
                    for p in range(Q):
                        act.wait_ge(pre, Q * i + p + 1)
                        nc.scalar.activation(rows[:, p, :, 0:DE], sumqk[:, p], ACT.Tanh).then_inc(tanhs, 1)
                steps(act, LOOPS, body)

            @block.sync
            def _(sp):
                def body(i, first):
                    for p in range(Q):
                        sp.wait_ge(tanhs, Q * i + p + 1)
                        sp.dma_start(out_rows[:, ds(i * STEP + p * G, G), :], rows[:, p]).then_inc(stored[p], 16)
                steps(sp, LOOPS, body)
                for p in range(Q):
                    sp.wait_ge(stored[p], 16 * LOOPS)

            @block.gpsimd
            def _(pool):
                def body(i, first):
                    for p in range(Q):
                        pool.wait_ge(staged, (Q * i + p) * 2 + 1)
                        if not first:
                            pool.wait_ge(stored[p], 16 * i)
                        after(pool, prods, i, p, Q, first)
                        pool.sem_inc(begun, 1)
                        gather_rows(pool, table, rows, far, p, rows_in)
                steps(pool, LOOPS, body)

            @block.tensor
            def _(pe):
                def body(i, first):
                    blocks = blocks_of(k, pe, o, i)
                    for p in range(Q):
                        pe.wait_ge(staged, (Q * i + p + 1) * 2)
                        after(pe, onehots, i, p, 4, first)
                        spread_nodes(pe, k, node_bc[:, p], lo[:, p]).then_inc(spread, 1)
                    for p in range(Q):
                        pe.wait_ge(onehots, Q * i + p + 1)
                        after(pe, pre, i, p, 4, first)
                        for g in range(G):
                            b = blocks[(p * G + g) // 2]
                            mm = pe.matmul(query[:, p, g * DE:(g + 1) * DE], oht[:, p, g, :], qky[:, ds(b, 1), 0:DE],
                                           start=True, stop=True)
                        mm.then_inc(looked_up, 1)
                steps(pe, LOOPS, body)

            @block.vector
            def _(dve):
                phi = k.r["phi"][:].unsqueeze(1).to_broadcast([P, G, DE])

                def body(i, first):
                    for p in range(Q):
                        dve.wait_ge(spread, Q * i + p + 1)
                        after(dve, looked_up, i, p, Q, first)
                        dve.tensor_scalar(oht[:, p], node_bc[:, p].rearrange("p (g e) -> p g e", g=G), k.iota_col[:],
                                          None, ALU.is_equal).then_inc(onehots, 1)
                    for p in range(Q):
                        dve.wait_ge(looked_up, Q * i + p + 1)
                        dve.wait_ge(rows_in[p], 16 * G * (i + 1))
                        after(dve, tanhs, i, p, Q, first)
                        dve.tensor_tensor(sumqk[:, p], query[:, p, 0:G * DE].rearrange("p (g f) -> p g f", g=G),
                                          rows[:, p, :, 0:DE], ALU.add).then_inc(pre, 1)
                    for p in range(Q):
                        dve.wait_ge(tanhs, Q * i + p + 1)
                        after(dve, scored, i, p, Q, first)
                        dve.tensor_tensor(prod[:, p], rows[:, p, :, 0:DE], phi, ALU.mult).then_inc(prods, 1)
                    for p in range(Q):
                        dve.wait_ge(prods, Q * i + p + 1)
                        dve.tensor_reduce(k.scores[:, ds(i * STEP + p * G, G)], prod[:, p], AX, ALU.add).then_inc(scored, 1)
                steps(dve, LOOPS, body)


def softmax_weights_stage(k, o):
    nc = k.nc
    step, largest, spread, shifted, done = (k.sem("sw_" + s) for s in ("step", "largest", "spread", "shifted", "done"))
    with ExitStack() as c:
        none = k.sb("sw_none", [P, J], F32, c)
        col = k.sb("sw_col", [P, 1], F32, c)
        top = k.sb("sw_top", [P, 1], F32, c)
        neg = k.sb("sw_neg", [P, 1], F32, c)
        with k.block() as block:
            @block.vector
            def _(dve):
                dve.tensor_scalar(none[:], o.lo[:], 0.0, -BIG, ALU.is_lt, ALU.mult).then_inc(step, 1)
                dve.wait_ge(step, 1)
                dve.tensor_tensor(k.scores[:], k.scores[:], none[:], ALU.add).then_inc(step, 1)
                dve.wait_ge(step, 2)
                dve.tensor_reduce(col[:], k.scores[:], AX, ALU.max).then_inc(largest, 1)
                dve.wait_ge(spread, 1)
                dve.tensor_scalar(neg[:], top[:], -1.0, None, ALU.mult).then_inc(shifted, 1)

            @block.gpsimd
            def _(pool):
                pool.wait_ge(largest, 1)
                nc.gpsimd.partition_all_reduce(top[:], col[:], P, RMAX).then_inc(spread, 1)

            @block.scalar
            def _(act):
                act.wait_ge(shifted, 1)
                nc.scalar.activation(k.scores[:], k.scores[:], ACT.Exp, bias=neg[:]).then_inc(done, 1)


def weighted_sum_stage(k, o, edges_dram, acc):
    nc = k.nc
    W = VW + 1
    (cleared, staged, weighted, summed, added, ones_put) = (k.sem("ws_" + s) for s in (
        "cleared", "staged", "weighted", "summed", "added", "ones_put"))
    rows_in = [k.sem(f"ws_rows_in{p}") for p in range(Q)]
    rows_dram = edges_dram.rearrange("(e j) w -> e j w", e=P)
    with ExitStack() as c:
        rows = k.sb("ws_rows", [P, Q, G, W], F32, c)
        ohw = k.sb("ws_ohw", [P, Q, G, P], F32, c)
        wt = k.sb("ws_wt", [P, Q, G], F32, c)
        lo = k.sb("ws_lo", [P, Q, G], F32, c)
        sums = k.ps("ws_sums", [P, Q, G // 2, 256], c)
        with k.block() as block:
            @block.sync
            def _(sp):
                sp.wait_ge(ones_put, 1)

                def body(i, first):
                    for p in range(Q):
                        after(sp, summed, i, p, Q, first)
                        sp.dma_start(rows[:, p, :, 0:VW], rows_dram[:, ds(i * STEP + p * G, G), :]).then_inc(rows_in[p], 16)
                steps(sp, LOOPS, body)

            @block.scalar
            def _(act):
                def body(i, first):
                    for p in range(Q):
                        after(act, weighted, i, p, Q, first)
                        nc.scalar.copy(wt[:, p], k.scores[:, ds(i * STEP + p * G, G)]).then_inc(staged, 1)
                        nc.scalar.copy(lo[:, p], o.lo[:, ds(i * STEP + p * G, G)]).then_inc(staged, 1)
                steps(act, LOOPS, body)

            @block.tensor
            def _(pe):
                def body(i, first):
                    for p in range(Q):
                        pe.wait_ge(weighted, Q * i + p + 1)
                        pe.wait_ge(rows_in[p], 16 * (i + 1))
                        after(pe, added, i, p, Q, first, each=G // 2)
                        sum_pairs(pe, lambda g: ohw[:, p, g, :], lambda g: rows[:, p, g, :],
                                  lambda q: sums[:, p, q, 0:W]).then_inc(summed, 1)
                steps(pe, LOOPS, body)

            @block.vector
            def _(dve):
                dve.memset(rows[:, :, :, VW:W], 1.0).then_inc(ones_put, 1)
                dve.memset(acc[:], 0.0).then_inc(cleared, 1)
                dve.wait_ge(cleared, 1)

                def body(i, first):
                    blocks = blocks_of(k, dve, o, i)
                    for p in range(Q):
                        dve.wait_ge(staged, (Q * i + p + 1) * 2)
                        after(dve, summed, i, p, Q, first)
                        for g in range(G):
                            ins = dve.tensor_scalar(ohw[:, p, g, :], k.iota_row[:], lo[:, p, g:g + 1],
                                                    wt[:, p, g:g + 1], ALU.is_equal, ALU.mult)
                        ins.then_inc(weighted, 1)
                    for p in range(Q):
                        dve.wait_ge(summed, Q * i + p + 1)
                        add_pairs(dve, acc, blocks, i, p, first, added, lambda q: sums[:, p, q, 0:W])
                steps(dve, LOOPS, body)



def message_stage(k, o, table, ab, acc):
    nc = k.nc
    (cleared, staged, spread, turned, onehots, features_t, first_part, hidden, hidden_turned, hidden_t, second,
     biased, messages, endhots, summed, added, begun) = (k.sem("ms_" + s) for s in (
         "cleared", "staged", "spread", "turned", "onehots", "features_t", "first_part", "hidden", "hidden_turned",
         "hidden_t", "second", "biased", "messages", "endhots", "summed", "added", "begun"))
    rows_in = [k.sem(f"ms_rows_in{p}") for p in range(Q)]
    features_in = [k.sem(f"ms_features_in{p}") for p in range(Q)]
    rows_dram = o.rows_dram.rearrange("(e j) w -> e j w", e=P)

    def four(ap):
        return ap.rearrange("p (g f) -> p g f", g=G)

    with ExitStack() as c:
        feat = k.sb("ms_feat", [P, Q, G, DE], F32, c)
        rows = k.sb("ms_rows", [P, Q, G, D], F32, c)
        far = k.sb("ms_far", [P, Q, G], I32, c)
        lo = k.sb("ms_lo", [P, Q, G], BF16, c)
        oht = k.sb("ms_oht", [P, Q, G, P], F32, c)
        oh = k.sb("ms_oh", [P, Q, G, P], F32, c)
        ft = k.sb("ms_ft", [DE, Q, G * P], F32, c)
        h = rows
        ht = k.sb("ms_ht", [P, Q, G * P], F32, c)
        m = k.sb("ms_m", [P, Q, G, D], F32, c)
        pa = k.ps("ms_pa", [P, 2, 512], c)
        pb = k.ps("ms_pb", [P, 2, 512], c)
        pc = k.ps("ms_pc", [P, 2, 512], c)
        pd = k.ps("ms_pd", [P, 2, 512], c)
        with k.block() as block:
            @block.sync
            def _(sp):
                def body(i, first):
                    for p in range(Q):
                        after(sp, turned, i, p, Q, first)
                        sp.dma_start(feat[:, p], rows_dram[:, ds(i * STEP + p * G, G), 0:DE]).then_inc(features_in[p], 16)
                steps(sp, LOOPS, body)

            @block.gpsimd
            def _(pool):
                def body(i, first):
                    for p in range(Q):
                        pool.wait_ge(staged, (Q * i + p) * 2 + 1)
                        after(pool, hidden_turned, i, p, Q, first)
                        pool.sem_inc(begun, 1)
                        gather_rows(pool, table, rows, far, p, rows_in)
                steps(pool, LOOPS, body)

            @block.tensor
            def _(pe):
                def body(i, first):
                    blocks = blocks_of(k, pe, o, i)
                    for p in range(Q):
                        pe.wait_ge(staged, (Q * i + p + 1) * 2)
                        pe.wait_ge(features_in[p], 16 * (i + 1))
                        if p < 2:
                            after(pe, hidden_t, i, p, 2, first)
                            after(pe, biased, i, p, 2, first)
                        else:
                            pe.wait_ge(onehots, Q * i + p - 1)
                            pe.wait_ge(features_t, Q * i + p - 1)
                        spread_nodes(pe, k, pa[:, p % 2], lo[:, p]).then_inc(spread, 1)
                        for g in range(G):
                            mm = pe.transpose(pb[0:DE, p % 2, g * P:(g + 1) * P], feat[:, p, g, :], k.ident[:])
                        mm.then_inc(turned, 1)
                    for p in range(Q):
                        pe.wait_ge(onehots, Q * i + p + 1)
                        pe.wait_ge(features_t, Q * i + p + 1)
                        after(pe, first_part, i, p, 2, first)
                        for g in range(G):
                            b = blocks[(p * G + g) // 2]
                            pe.matmul(pc[:, p % 2, g * P:(g + 1) * P], oht[:, p, g, :], ab[:, ds(b, 1), D:2 * D],
                                      start=True, stop=False)
                            mm = pe.matmul(pc[:, p % 2, g * P:(g + 1) * P], ft[:, p, g * P:(g + 1) * P], k.w["W1c"][:],
                                           start=False, stop=True)
                        mm.then_inc(hidden, 1)
                    for p in range(Q):
                        pe.wait_ge(first_part, Q * i + p + 1)
                        if p < 2:
                            pe.wait_ge(onehots, Q * i + p + 3)
                        else:
                            pe.wait_ge(hidden_t, Q * i + p - 1)
                        for g in range(G):
                            mm = pe.transpose(pa[:, p % 2, g * P:(g + 1) * P], h[:, p, g, :], k.ident[:])
                        mm.then_inc(hidden_turned, 1)
                    for p in range(Q):
                        pe.wait_ge(hidden_t, Q * i + p + 1)
                        if p < 2:
                            pe.wait_ge(features_t, Q * i + p + 3)
                        else:
                            pe.wait_ge(biased, Q * i + p - 1)
                        for g in range(G):
                            mm = pe.matmul(pb[:, p % 2, g * P:(g + 1) * P], ht[:, p, g * P:(g + 1) * P], k.w["W2"][:],
                                           start=True, stop=True)
                        mm.then_inc(second, 1)
                    for p in range(Q):
                        pe.wait_ge(messages, Q * i + p + 1)
                        pe.wait_ge(endhots, Q * i + p + 1)
                        after(pe, added, i, p, 2, first, each=G // 2)
                        sum_pairs(pe, lambda g: oh[:, p, g, :], lambda g: m[:, p, g, :],
                                  lambda q: pd[:, p % 2, q * P:(q + 1) * P]).then_inc(summed, 1)
                steps(pe, LOOPS, body)

            @block.scalar
            def _(act):
                def body(i, first):
                    for p in range(Q):
                        if not first:
                            act.wait_ge(rows_in[p], 16 * G * i)
                        after(act, spread, i, p, Q, first)
                        stage_ids(act, o, far, i, p).then_inc(staged, 1)
                        nc.scalar.copy(lo[:, p], o.lo[:, ds(i * STEP + p * G, G)]).then_inc(staged, 1)
                    for p in range(Q):
                        act.wait_ge(turned, Q * i + p + 1)
                        after(act, hidden, i, p, Q, first)
                        nc.scalar.copy(ft[:, p], pb[0:DE, p % 2]).then_inc(features_t, 1)
                    for p in range(Q):
                        act.wait_ge(hidden_turned, Q * i + p + 1)
                        after(act, second, i, p, Q, first)
                        nc.scalar.activation(ht[:, p], pa[:, p % 2], ACT.Relu).then_inc(hidden_t, 1)
                    for p in range(Q):
                        act.wait_ge(biased, Q * i + p + 1)
                        nc.scalar.activation(m[:, p], m[:, p], ACT.Relu).then_inc(messages, 1)
                steps(act, LOOPS, body)

            @block.vector
            def _(dve):
                dve.memset(acc[:], 0.0).then_inc(cleared, 1)
                dve.wait_ge(cleared, 1)

                def body(i, first):
                    blocks = blocks_of(k, dve, o, i)
                    for p in range(Q):
                        dve.wait_ge(spread, Q * i + p + 1)
                        after(dve, hidden, i, p, Q, first)
                        dve.tensor_scalar(oht[:, p], four(pa[:, p % 2]), k.iota_col[:], None, ALU.is_equal
                                          ).then_inc(onehots, 1)
                    for p in range(Q):
                        dve.wait_ge(hidden, Q * i + p + 1)
                        dve.wait_ge(rows_in[p], 16 * G * (i + 1))
                        dve.tensor_tensor(h[:, p], four(pc[:, p % 2]), rows[:, p], ALU.add).then_inc(first_part, 1)
                    for p in range(Q):
                        after(dve, summed, i, p, Q, first)
                        end_onehots(dve, k, o, oh, i, p).then_inc(endhots, 1)
                    for p in range(Q):
                        dve.wait_ge(second, Q * i + p + 1)
                        after(dve, summed, i, p, Q, first)
                        dve.tensor_tensor(m[:, p], four(pb[:, p % 2]), over_blocks(k.r["b2"][:], [P, G, D]), ALU.add
                                          ).then_inc(biased, 1)
                    for p in range(Q):
                        dve.wait_ge(summed, Q * i + p + 1)
                        add_pairs(dve, acc, blocks, i, p, first, added, lambda q: pd[:, p % 2, q * P:(q + 1) * P])
                steps(dve, LOOPS, body)



def product_stage(k, name, terms, out, width, bias):
    nc = k.nc
    T = len(terms)
    stride = P if width <= P else 2 * P
    staged, turned, turned_in, made, written = (k.sem(f"{name}_{s}") for s in (
        "staged", "turned", "turned_in", "made", "written"))
    with ExitStack() as c:
        st = [k.sb(f"{name}_st{t}", [P, NCH, K], F32, c) for t, (_, K, _) in enumerate(terms)]
        xt = [k.sb(f"{name}_xt{t}", [K, NCH * P], F32, c) for t, (_, K, _) in enumerate(terms)]
        pt = [k.ps(f"{name}_pt{t}", [P, 1024], c) for t in range(T)]
        po = k.ps(f"{name}_po", [P, 1024 if stride == P else 1536], c)
        pov = po[:, 0:NCH * stride].rearrange("p (b f) -> p b f", b=NCH)
        with k.block() as block:
            @block.scalar
            def _(act):
                def body(i, first):
                    for t, (x, K, _) in enumerate(terms):
                        if not first:
                            act.wait_ge(turned, T * i)
                        nc.scalar.copy(st[t][:], x[:, ds(i * NCH, NCH), :]).then_inc(staged, 1)
                steps(act, NB // NCH, body)

            @block.tensor
            def _(pe):
                def body(i, first):
                    for t, (_, K, _) in enumerate(terms):
                        pe.wait_ge(staged, T * i + t + 1)
                        if not first:
                            pe.wait_ge(turned_in, T * i)
                        for q in range(NCH):
                            mm = pe.transpose(pt[t][0:K, q * P:(q + 1) * P], st[t][:, q, :], k.ident[:])
                        mm.then_inc(turned, 1)
                    pe.wait_ge(turned_in, T * i + T)
                    if not first:
                        pe.wait_ge(written, i)
                    for q in range(NCH):
                        for t, (_, K, w) in enumerate(terms):
                            mm = pe.matmul(pov[:, q, 0:width], xt[t][:, q * P:(q + 1) * P], w, start=(t == 0), stop=(t == T - 1))
                    mm.then_inc(made, 1)
                steps(pe, NB // NCH, body)

            @block.vector
            def _(dve):
                def body(i, first):
                    for t, (_, K, _) in enumerate(terms):
                        dve.wait_ge(turned, T * i + t + 1)
                        if not first:
                            dve.wait_ge(made, i)
                        dve.tensor_copy(xt[t][:], pt[t][0:K, 0:NCH * P]).then_inc(turned_in, 1)
                    dve.wait_ge(made, i + 1)
                    dve.tensor_tensor(out[:, ds(i * NCH, NCH), 0:width], pov[:, :, 0:width],
                                      over_blocks(bias[:, 0:width], [P, NCH, width]), ALU.add).then_inc(written, 1)
                steps(dve, NB // NCH, body)


class Chain:

    def __init__(self, dve, step, variances=None, roots=None):
        self.dve, self.step, self.n = dve, step, 0
        self.variances, self.roots, self.rooted = variances, roots, 0

    def root(self, ins, place):
        self.rooted += 1
        ins.then_inc(self.variances, 1)
        self.dve.wait_ge(self.roots, self.rooted)
        self(self.dve.reciprocal(place, place))

    def __call__(self, ins):
        self.n += 1
        ins.then_inc(self.step, 1)
        self.dve.wait_ge(self.step, self.n)

    def norm(self, k, out, x, sq, col, gain=None, bias=None, eps=1e-5):
        dve, full = self.dve, [P, NB, D]
        self(dve.tensor_reduce(col[:, 0, :], x[:], AX, ALU.add))
        self(dve.tensor_scalar(col[:, 0, :], col[:, 0, :], 1.0 / D, None, ALU.mult))
        self(dve.tensor_tensor(out[:], x[:], wide(col[:, 0, :], D, full), ALU.subtract))
        self(dve.tensor_tensor(sq[:], out[:], out[:], ALU.mult))
        self(dve.tensor_reduce(col[:, 1, :], sq[:], AX, ALU.add))
        self.root(dve.tensor_scalar(col[:, 1, :], col[:, 1, :], 1.0 / D, eps, ALU.mult, ALU.add), col[:, 1, :])
        self(dve.tensor_tensor(out[:], out[:], wide(col[:, 1, :], D, full), ALU.mult))
        if gain is not None:
            self(dve.tensor_tensor(out[:], out[:], over_blocks(gain[:], full), ALU.mult))
            self(dve.tensor_tensor(out[:], out[:], over_blocks(bias[:], full), ALU.add))


def root_program(act, variances, roots, places):
    for n, ap in enumerate(places):
        act.wait_ge(variances, n + 1)
        act.activation(ap, ap, ACT.Sqrt).then_inc(roots, 1)


def node_stage(k, name, program, norms=0):
    step, variances, roots = (k.sem(f"{name}_{s}") for s in ("step", "variances", "roots"))
    with k.block() as block:
        @block.scalar
        def _(act):
            root_program(act, variances, roots, [k.col[:, 1, :]] * norms)

        @block.vector
        def _(dve):
            program(Chain(dve, step, variances, roots), dve)


def store_stage(k, name, pairs):
    stored = k.sem(name + "_stored")
    with k.block() as block:
        @block.sync
        def _(sp):
            for table, x in pairs:
                sp.dma_start(table.rearrange("(b p) f -> p b f", p=P), x).then_inc(stored, 16)
            sp.wait_ge(stored, 16 * len(pairs))


def global_token_stage(k):
    nc = k.nc
    step, summed, token, spread = (k.sem("gt_" + s) for s in ("step", "summed", "token", "spread"))
    with ExitStack() as c:
        part = k.sb("gt_part", [P, D], F32, c)
        g = k.sb("gt_g", [P, 1], F32, c)
        row = k.sb("gt_row", [P, D], F32, c)
        pg = k.ps("gt_pg", [P, 512], c)
        pr = k.ps("gt_pr", [P, 512], c)
        with k.block() as block:
            @block.tensor
            def _(pe):
                pe.wait_ge(summed, 1)
                pe.matmul(pg[:, 0:1], part[:], k.ones[:, 0:1], start=True, stop=True).then_inc(token, 1)
                pe.wait_ge(summed, 2)
                pe.matmul(pr[:, 0:D], g[:].to_broadcast([P, P]), k.w["Wg"][:], start=True, stop=True).then_inc(spread, 1)

            @block.vector
            def _(dve):
                link = Chain(dve, step)
                link(dve.tensor_scalar(k.X[:, NB - 1, :], k.X[:, NB - 1, :], k.last_rows[:], None, ALU.mult))
                dve.tensor_reduce(part[:], k.X[:].rearrange("p b f -> p f b"), AX, ALU.add).then_inc(summed, 1)
                dve.wait_ge(token, 1)
                dve.tensor_scalar(g[:], pg[:, 0:1], 1.0 / N, k.gtok[:], ALU.mult, ALU.add).then_inc(summed, 1)
                dve.wait_ge(spread, 1)
                link(dve.tensor_tensor(row[:], pr[:, 0:D], k.r["Wg"][:], ALU.add))
                link(dve.tensor_tensor(k.X[:], k.X[:], over_blocks(row[:], [P, NB, D]), ALU.add))


def batch_norm_stage(k, name, x, sq, gain, bias):
    nc, full = k.nc, [P, NB, D]
    step, summed, spread, variances, roots = (k.sem(f"{name}_{s}") for s in (
        "step", "summed", "spread", "variances", "roots"))
    with ExitStack() as c:
        part = k.sb(name + "_part", [P, 2, D], F32, c)
        row = k.sb(name + "_row", [P, 2, D], F32, c)
        pr = k.ps(name + "_pr", [P, 2, 512], c)
        with k.block() as block:
            @block.tensor
            def _(pe):
                for t in range(2):
                    pe.wait_ge(summed, t + 1)
                    pe.matmul(pr[:, t, 0:D], k.ones[:], part[:, t, :], start=True, stop=True).then_inc(spread, 1)

            @block.scalar
            def _(act):
                root_program(act, variances, roots, [row[:, 1]])

            @block.vector
            def _(dve):
                link = Chain(dve, step, variances, roots)
                link(dve.tensor_scalar(x[:, NB - 1, :], x[:, NB - 1, :], k.last_rows[:], None, ALU.mult))
                dve.tensor_reduce(part[:, 0], x[:].rearrange("p b f -> p f b"), AX, ALU.add).then_inc(summed, 1)
                dve.wait_ge(spread, 1)
                link(dve.tensor_scalar(row[:, 0], pr[:, 0, 0:D], 1.0 / N, None, ALU.mult))
                link(dve.tensor_tensor(x[:], x[:], over_blocks(row[:, 0], full), ALU.subtract))
                link(dve.tensor_tensor(sq[:], x[:], x[:], ALU.mult))
                link(dve.tensor_scalar(sq[:, NB - 1, :], sq[:, NB - 1, :], k.last_rows[:], None, ALU.mult))
                dve.tensor_reduce(part[:, 1], sq[:].rearrange("p b f -> p f b"), AX, ALU.add).then_inc(summed, 1)
                dve.wait_ge(spread, 2)
                link.root(dve.tensor_scalar(row[:, 1], pr[:, 1, 0:D], 1.0 / N, 1e-5, ALU.mult, ALU.add), row[:, 1])
                link(dve.tensor_tensor(row[:, 1], row[:, 1], gain[:], ALU.mult))
                link(dve.tensor_tensor(x[:], x[:], over_blocks(row[:, 1], full), ALU.mult))
                link(dve.tensor_tensor(x[:], x[:], over_blocks(bias[:], full), ALU.add))



class Order:

    def __init__(self, k, name):
        self.name = name
        self.lo = k.sb(name + "_lo", [P, J])
        self.far_i = k.sb(name + "_far_i", [P, J], I32)
        self.block_i = k.sb(name + "_block_i", [P, J // 2], I32)


def build(nc, a, out):
    with ExitStack() as ctx:
        k = Core(nc, ctx)
        early = k.early = ExitStack()
        by_dst, by_src = Order(k, "dst"), Order(k, "src")
        k.scores = k.sb("scores", [P, J])
        k.deg = k.sb("deg", [P, NB])
        k.mx = k.sb("mx", [P, NB, 2])
        acc = k.sb("acc", [P, NB, VW + 1])
        load_stage(k, a)
        for o in (by_dst, by_src):
            o.slot = k.sb(o.name + "_slot", [P, J, 2], F32, early)
            o.block_f = k.sb(o.name + "_block_f", [P, J], F32, early)
            o.row = k.sb(o.name + "_row", [EP, EC], I32, early)
            o.meta = k.sb(o.name + "_meta", [EP, EC, 2], F32, early)
        by_dst.rows_dram = nc.dram_tensor("rows_by_dst", (P * J, RW), F32).ap()
        by_src.ids_dram = nc.dram_tensor("ids_by_src", (P * J, 2), F32).ap()
        edges_dram = nc.dram_tensor("edges_by_src", (P * J, VW), F32).ap()
        tables = [nc.dram_tensor(f"table{n}", (P * NB, D), F32).ap() for n in range(5)]
        table_kv = nc.dram_tensor("table_kv", (P * NB, VW), F32).ap()
        order_stage(k, by_dst, a["dst"], a["src"])
        order_stage(k, by_src, a["src"], a["dst"], lambda c: FeatureScatter(k, by_dst, a["edge_attr_64"], c))
        blank_ids_stage(k, by_src)
        rounds = EC // (2 * CW)
        score_stage(k, by_dst, lambda c: IdScatter(k, by_src, c, "ia", 0, rounds // 2))
        node_maximum_stage(k, by_dst)
        sum0 = acc[:].rearrange("p b w -> p (b w)")[:, 0:NB * RW].rearrange("p (b w) -> p b w", b=NB)
        attention_sum_stage(k, by_dst, sum0, lambda c: IdScatter(k, by_src, c, "ib", rounds // 2, rounds))
        far_ends_stage(k, by_dst, by_src)
        early.close()

        X, full = k.X, [P, NB, D]
        A = k.sb("A", full)
        B = k.sb("B", full)
        wide2 = k.sb("wide2", [P, NB, 2 * D])
        col = k.col = k.sb("col", [P, 2, NB])
        relu_tmp = ALU.max


        def shares0(link, dve):
            link(dve.tensor_scalar(col[:, 0, :], sum0[:, :, DE + 1], 1e-6, None, ALU.add))
            link(dve.reciprocal(col[:, 0, :], col[:, 0, :]))
            link(dve.tensor_copy(sum0[:, :, DE], sum0[:, :, DE + 1]))
            link(dve.tensor_tensor(sum0[:, :, 0:DE + 1], sum0[:, :, 0:DE + 1], wide(col[:, 0, :], DE + 1, [P, NB, DE + 1]), ALU.mult))
        node_stage(k, "shares0", shares0)
        product_stage(k, "ev", [(sum0[:, :, 0:DE + 1], DE + 1, k.w["ev"][:])], A, D, k.r["none"])
        product_stage(k, "out1", [(A, D, k.w["out1"][:])], B, D, k.r["out1"])
        node_stage(k, "relu0", lambda link, dve: link(dve.tensor_scalar(B[:], B[:], 0.0, None, relu_tmp)))
        product_stage(k, "out2", [(B, D, k.w["out2"][:])], A, D, k.r["out2"])

        def end0(link, dve):
            link(dve.tensor_tensor(A[:], A[:], X[:], ALU.add))
            link(dve.tensor_tensor(A[:], A[:], X[:], ALU.add))
            link.norm(k, X, A, B, col)
        node_stage(k, "end0", end0, norms=1)

        node_stage(k, "keep1", lambda link, dve: link(dve.tensor_copy(A[:], X[:])))
        global_token_stage(k)
        node_stage(k, "ln1", lambda link, dve: link.norm(k, B, X, wide2[:, :, 0:D], col, k.r["ln1g"], k.r["ln1b"]), norms=1)
        product_stage(k, "msg", [(B, D, k.w["msg"][:])], wide2, D, k.r["msg"])
        store_stage(k, "msg_table", [(tables[0], wide2[:, :, 0:D])])
        gather_sum_stage(k, "gs1", by_src, tables[0], acc[:, :, 0:D])

        def mix1(link, dve):
            link(dve.tensor_scalar(k.eps[:], k.eps[:], 1.0, None, ALU.add))
            link(dve.scalar_tensor_tensor(B[:], B[:], k.eps[:], acc[:, :, 0:D], ALU.mult, ALU.add))
        node_stage(k, "mix1", mix1)
        product_stage(k, "lin", [(B, D, k.w["lin"][:])], wide2, D, k.r["lin"])

        def ln2(link, dve):
            link(dve.tensor_scalar(wide2[:, :, 0:D], wide2[:, :, 0:D], 0.0, None, ALU.max))
            link(dve.tensor_tensor(X[:], X[:], wide2[:, :, 0:D], ALU.add))
            link.norm(k, B, X, wide2[:, :, 0:D], col, k.r["ln2g"], k.r["ln2b"])
        node_stage(k, "ln2", ln2, norms=1)
        product_stage(k, "qky", [(B, D, k.w["qky"][:])], wide2, 2 * D, k.r["qky"])
        store_stage(k, "kv_table", [(table_kv, wide2[:, :, DE:2 * D])])
        tanh_stage(k, by_src, table_kv, wide2, edges_dram)
        softmax_weights_stage(k, by_src)
        weighted_sum_stage(k, by_src, edges_dram, acc)

        def shares1(link, dve):
            link(dve.tensor_scalar(col[:, 0, :], acc[:, :, VW], 1e-9, None, ALU.add))
            link(dve.reciprocal(col[:, 0, :], col[:, 0, :]))
            link(dve.tensor_tensor(acc[:], acc[:], wide(col[:, 0, :], VW + 1, [P, NB, VW + 1]), ALU.mult))
            link(dve.tensor_tensor(X[:], X[:], acc[:, :, DE:VW], ALU.add))
            link(dve.tensor_copy(acc[:, :, DE], acc[:, :, VW]))
        node_stage(k, "shares1", shares1)
        product_stage(k, "We", [(acc[:, :, 0:DE + 1], DE + 1, k.w["We"][:])], wide2, D, k.r["none"])

        def ln3(link, dve):
            link(dve.tensor_tensor(X[:], X[:], wide2[:, :, 0:D], ALU.add))
            link.norm(k, B, X, wide2[:, :, 0:D], col, k.r["ln3g"], k.r["ln3b"])
        node_stage(k, "ln3", ln3, norms=1)
        product_stage(k, "ffn1", [(B, D, k.w["ffn1"][:])], wide2, 2 * D, k.r["ffn1"])
        node_stage(k, "relu1", lambda link, dve: link(dve.tensor_scalar(wide2[:], wide2[:], 0.0, None, ALU.max)))
        product_stage(k, "ffn2", [(wide2[:, :, 0:D], D, k.w["ffn2"][:, 0:D]), (wide2[:, :, D:2 * D], D, k.w["ffn2"][:, D:2 * D])],
                      B, D, k.r["ffn2"])

        def end1(link, dve):
            link(dve.tensor_tensor(B[:], B[:], X[:], ALU.add))
            link(dve.tensor_tensor(A[:], A[:], B[:], ALU.add))
            link.norm(k, X, A, B, col)
        node_stage(k, "end1", end1, norms=1)

        product_stage(k, "ab", [(X, D, k.w["W1ab"][:])], wide2, 2 * D, k.r["ab"])
        store_stage(k, "a_table", [(tables[1], wide2[:, :, 0:D])])
        message_stage(k, by_dst, tables[1], wide2, acc[:, :, 0:D])
        node_stage(k, "copy2", lambda link, dve: link(dve.tensor_copy(A[:], acc[:, :, 0:D])))
        product_stage(k, "bn", [(A, D, k.w["Wn"][:])], B, D, k.r["bn"])

        def end2(link, dve):
            link(dve.tensor_scalar(B[:], B[:], 0.0, None, ALU.max))
            link(dve.tensor_tensor(B[:], B[:], X[:], ALU.add))
            link.norm(k, A, B, wide2[:, :, 0:D], col, k.r["gamma"], k.r["beta"])
            link(dve.tensor_tensor(B[:], A[:], X[:], ALU.add))
            link.norm(k, X, B, wide2[:, :, 0:D], col)
        node_stage(k, "end2", end2, norms=2)

        H = wide2[:, :, 0:D]
        T = wide2[:, :, D:2 * D]

        def sage(name, x, table, w_self, w_neigh, bias, dst):
            store_stage(k, name + "_table", [(table, x[:])])
            gather_sum_stage(k, name + "_gs", by_dst, table, acc[:, :, 0:D])
            node_stage(k, name + "_mean", lambda link, dve: link(dve.tensor_tensor(
                acc[:, :, 0:D], acc[:, :, 0:D], wide(k.deg[:], D, full), ALU.mult)))
            product_stage(k, name + "_pr", [(x, D, w_self[:]), (acc[:, :, 0:D], D, w_neigh[:])], dst, D, bias)

        sage("sg1", X, tables[2], k.w["s1"], k.w["n1"], k.r["s1"], A)
        node_stage(k, "relu3", lambda link, dve: link(dve.tensor_scalar(A[:], A[:], 0.0, None, ALU.max)))
        batch_norm_stage(k, "bn1", A, B, k.r["bn1g"], k.r["bn1b"])
        sage("sg2", A, tables[3], k.w["s2"], k.w["n2"], k.r["s2"], B)

        def res3(link, dve):
            link(dve.tensor_scalar(B[:], B[:], 0.0, None, ALU.max))
            link(dve.tensor_tensor(A[:], A[:], B[:], ALU.add))
        node_stage(k, "res3", res3)
        batch_norm_stage(k, "bn2", A, B, k.r["bn2g"], k.r["bn2b"])
        sage("sg3", A, tables[4], k.w["s3"], k.w["n3"], k.r["s3"], B)

        def end3(link, dve):
            link.norm(k, A, B, H, col, k.r["lng"], k.r["lnb"])
            link(dve.tensor_tensor(A[:], A[:], X[:], ALU.add))
            link.norm(k, B, A, H, col)
        node_stage(k, "end3", end3, norms=2)

        written = k.sem("written")
        with k.block() as block:
            @block.sync
            def _(sp):
                sp.dma_start(out[0:(NB - 1) * P, :].rearrange("(b p) f -> p b f", p=P), B[:, 0:NB - 1, :]).then_inc(written, 16)
                sp.dma_start(out[(NB - 1) * P:N, :], B[0:LAST, NB - 1, :]).then_inc(written, 16)
                sp.wait_ge(written, 32)


def kernel(**inputs):
    import numpy as np
    import concourse.bacc as bacc
    from concourse.bass_utils import run_bass_kernel_spmd

    nc = bacc.Bacc("TRN2", target_bir_lowering=False, num_devices=1)
    arrays, a = {}, {}
    for name in inputs:
        v = np.ascontiguousarray(inputs[name])
        if v.ndim == 0:
            v = v.reshape(1)
        arrays["in_" + name] = v
        a[name] = nc.dram_tensor("in_" + name, v.shape, mybir.dt.from_np(v.dtype), kind="ExternalInput").ap()
    out = nc.dram_tensor("out", (N, D), F32, kind="ExternalOutput").ap()
    build(nc, a, out)
    return run_bass_kernel_spmd(nc, [arrays], core_ids=[0]).results[0]["out"]
```

```python
from contextlib import ExitStack, contextmanager

import concourse.bass as bass
from concourse import mybir

ALU = mybir.AluOpType
ACT = mybir.ActivationFunctionType
F32 = mybir.dt.float32
BF16 = mybir.dt.bfloat16
I32 = mybir.dt.int32
AX = mybir.AxisListType.X
RMAX = bass.bass_isa.ReduceOp.max
ds = bass.ds

P = 128
N = 3125
E = 100000
D = 128
DE = 64
NB = -(-N // P)
LAST = N - (NB - 1) * P
EP, EC = 125, 800
G = 4
Q = 4
STEP = Q * G
J = -(-2 * ((E + NB * (2 * P - 1)) // (2 * P)) // STEP) * STEP
LOOPS = J // STEP
RW = DE + 2
BIG = 2.0 ** 100
NCH = 4


class Core:

    def __init__(self, nc, ctx):
        self.nc, self.ctx, self.stage_sems = nc, ctx, []
        self.taken = 0

    def sb(self, name, shape, dt=F32, ctx=None):
        return (ctx or self.ctx).enter_context(self.nc.sbuf_tensor(name, shape, dt))

    def ps(self, name, shape, ctx, dt=F32):
        return ctx.enter_context(self.nc.psum_tensor(name, shape, dt))

    def sem(self, name):
        self.stage_sems.append(self.nc.alloc_semaphore(name))
        return self.stage_sems[-1]

    @contextmanager
    def block(self):
        with self.nc.Block() as block:
            yield block
        self.nc.clear_and_free_semaphores(self.stage_sems)
        self.nc.all_engine_barrier()
        self.stage_sems = []


def wide(ap, n, shape):
    return ap.unsqueeze(2).to_broadcast(shape)


def over_blocks(ap, shape):
    return ap.unsqueeze(1).to_broadcast(shape)


def steps(eng, count, body):
    body(0, True)
    with eng.Fori(1, count) as i:
        body(i, False)


def rounds(eng, body):
    body(0)
    body(1)
    with eng.Fori(2, LOOPS) as i:
        body(i)
    body(LOOPS)


def group(i, p, lag=0):
    n = Q * i + p - lag
    if not isinstance(i, int) or 0 <= n < Q * LOOPS:
        yield n, (p - lag) % Q, i + (p - lag) // Q


def reuse(eng, sem, n, depth, each=1):
    if not isinstance(n, int) or n >= depth:
        eng.wait_ge(sem, (n - depth + 1) * each)



def constants_stage(k, a):
    nc = k.nc
    k.iota_row = k.sb("iota_row", [P, P])
    k.iota_col = k.sb("iota_col", [P, 1])
    k.ident = k.sb("ident", [P, P])
    k.ident_h = k.sb("ident_h", [P, P], BF16)
    k.far_off = k.sb("far_off", [P, P], BF16)
    k.ones = k.sb("ones", [P, P])
    k.ones_h = k.sb("ones_h", [P, P], BF16)
    k.before = k.sb("before", [P, P])
    k.before_h = k.sb("before_h", [P, P], BF16)
    k.last_rows = k.sb("last_rows", [P, 1])
    k.X = k.sb("X", [P, NB, D])
    k.att_b = k.sb("att_b", [P, 4])
    k.att_m = k.sb("att_m", [P, D + DE])
    k.att_bm = k.sb("att_bm", [P, 1])
    w = {}

    def weight(name, rows, cols):
        w[name] = k.sb("w_" + name, [rows, cols])
        return w[name]

    loads = [(k.X[0:LAST, NB - 1, :], a["x"][(NB - 1) * P:N, :])]
    weight("ev", DE + 1, D)
    loads += [(w["ev"][0:DE, :], a["L0_gnn_ev_W"]), (w["ev"][DE:DE + 1, :], a["L0_gnn_ev_b"].unsqueeze(0))]
    weight("We", DE + 1, D)
    loads += [(w["We"][0:DE, :], a["L1_gnn_We_w"]), (w["We"][DE:DE + 1, :], a["L1_gnn_We_b"].unsqueeze(0))]
    for n, s in (("out1", "L0_gnn_out1_W"), ("out2", "L0_gnn_out2_W"), ("Wg", "L1_gnn_Wg_in_w"),
                 ("msg", "L1_gnn_msg_w"), ("lin", "L1_gnn_lin_w"), ("W2", "L2_gnn_W2"), ("Wn", "L2_gnn_Wn"),
                 ("s1", "L3_gnn_w1_self"), ("n1", "L3_gnn_w1_neigh"), ("s2", "L3_gnn_w2_self"),
                 ("n2", "L3_gnn_w2_neigh"), ("s3", "L3_gnn_w3_self"), ("n3", "L3_gnn_w3_neigh")):
        loads.append((weight(n, P, D)[:], a[s]))
    weight("qky", P, 2 * D)
    loads += [(w["qky"][:, 0:64], a["L1_gnn_Wq"]), (w["qky"][:, 64:128], a["L1_gnn_Wk"]),
              (w["qky"][:, 128:256], a["L1_gnn_Wy_w"])]
    loads.append((weight("ffn1", P, 2 * D)[:], a["L1_gnn_ffn_w1"]))
    weight("ffn2", P, 2 * D)
    loads += [(w["ffn2"][:, 0:D], a["L1_gnn_ffn_w2"][0:P, :]), (w["ffn2"][:, D:2 * D], a["L1_gnn_ffn_w2"][P:2 * P, :])]
    weight("W1ab", P, 2 * D)
    loads += [(w["W1ab"][:, 0:D], a["L2_gnn_W1"][0:P, :]), (w["W1ab"][:, D:2 * D], a["L2_gnn_W1"][P:2 * P, :])]
    k.w1c = k.sb("w1c", [P, 2, D])
    for t in range(2):
        loads.append((k.w1c[t * DE:(t + 1) * DE, t, :], a["L2_gnn_W1"][2 * P:2 * P + DE, :]))
    k.gtok = k.sb("gtok", [P, 1])
    loads.append((k.gtok[:], a["L1_gnn_g_token"].rearrange("a d -> d a")))
    k.w = w

    rows = {"out1": "L0_gnn_out1_b", "out2": "L0_gnn_out2_b", "Wg": "L1_gnn_Wg_in_b", "ln1g": "L1_gnn_ln1_g",
            "ln1b": "L1_gnn_ln1_b", "msg": "L1_gnn_msg_b", "lin": "L1_gnn_lin_b", "ln2g": "L1_gnn_ln2_g",
            "ln2b": "L1_gnn_ln2_b", "phi": "L1_gnn_Wphi", "ln3g": "L1_gnn_ln3_g", "ln3b": "L1_gnn_ln3_b",
            "ffn1": "L1_gnn_ffn_b1", "ffn2": "L1_gnn_ffn_b2", "b2": "L2_gnn_b2", "bn": "L2_gnn_bn",
            "gamma": "L2_gnn_gamma", "beta": "L2_gnn_beta", "s1": "L3_gnn_b1", "s2": "L3_gnn_b2",
            "s3": "L3_gnn_b3", "bn1g": "L3_gnn_bn1_g", "bn1b": "L3_gnn_bn1_b", "bn2g": "L3_gnn_bn2_g",
            "bn2b": "L3_gnn_bn2_b", "lng": "L3_gnn_ln_g", "lnb": "L3_gnn_ln_b"}
    k.r = {}
    for n, s in rows.items():
        k.r[n] = k.sb("r_" + n, [P, a[s].shape[0]])
        loads.append((k.r[n][:], a[s].partition_broadcast(P)))
    k.r["ab"] = k.sb("r_ab", [P, 2 * D])
    k.r["qky"] = k.sb("r_qky", [P, 2 * D])
    k.r["none"] = k.sb("r_none", [P, D])
    loads.append((k.r["ab"][:, 0:D], a["L2_gnn_b1"].partition_broadcast(P)))
    loads.append((k.r["qky"][:, D:2 * D], a["L1_gnn_Wy_b"].partition_broadcast(P)))
    k.eps = k.sb("eps", [P, 1])
    loads.append((k.eps[:], a["L1_gnn_eps"].partition_broadcast(P)))
    k.blank_ids = k.sb("blank_ids", [P, 8, 2], F32, k.early)
    k.blank_row = k.sb("blank_row", [P, 8, RW], F32, k.early)
    k.iota_tile = k.sb("iota_tile", [P, J], F32, k.early)
    k.pair_max = k.sb("pair_max", [P, J // 2], F32, k.early)
    k.att = k.sb("att", [P, D + DE, 4], F32, k.early)
    loads.append((k.att[:], a["L0_gnn_attn_W"].partition_broadcast(P)))
    loads.append((k.att_b[:], a["L0_gnn_attn_b"].partition_broadcast(P)))
    loads.append((k.X[:, 0:NB - 1, :], a["x"][0:(NB - 1) * P, :].rearrange("(b p) f -> p b f", p=P)))

    iotas = k.sem("iotas")
    k.loads = loads
    with k.block() as block:
        @block.gpsimd
        def _(pool):
            nc.gpsimd.iota(k.iota_row[:], [[1, P]], base=0, channel_multiplier=0,
                           allow_small_or_imprecise_dtypes=True).then_inc(iotas, 1)
            nc.gpsimd.iota(k.iota_tile[:], [[1, J]], base=0, channel_multiplier=0,
                           allow_small_or_imprecise_dtypes=True).then_inc(iotas, 1)
            nc.gpsimd.iota(k.iota_col[:], [[1, 1]], base=0, channel_multiplier=1,
                           allow_small_or_imprecise_dtypes=True).then_inc(iotas, 1)

        @block.vector
        def _(dve):
            dve.memset(k.X[:, NB - 1, :], 0.0)
            dve.memset(k.w1c[:], 0.0)
            dve.memset(k.ones[:], 1.0)
            dve.memset(k.ones_h[:], 1.0)
            dve.memset(k.r["ab"][:, D:2 * D], 0.0)
            dve.memset(k.r["qky"][:, 0:D], 0.0)
            dve.memset(k.r["none"][:], 0.0)
            dve.memset(k.blank_ids[:, :, 0:1], -1.0)
            dve.memset(k.blank_ids[:, :, 1:2], 0.0)
            dve.memset(k.blank_row[:, :, 0:DE], 0.0)
            dve.memset(k.blank_row[:, :, DE:DE + 1], -1.0)
            dve.memset(k.blank_row[:, :, DE + 1:RW], 0.0)
            dve.wait_ge(iotas, 3)
            dve.tensor_scalar(k.ident[:], k.iota_row[:], k.iota_col[:], None, ALU.is_equal)
            dve.tensor_scalar(k.ident_h[:], k.iota_row[:], k.iota_col[:], None, ALU.is_equal)
            dve.tensor_scalar(k.far_off[:], k.iota_row[:], k.iota_col[:], -BIG, ALU.is_equal, ALU.mult)
            dve.tensor_scalar(k.before[:], k.iota_row[:], k.iota_col[:], None, ALU.is_gt)
            dve.tensor_scalar(k.before_h[:], k.iota_row[:], k.iota_col[:], None, ALU.is_gt)
            dve.tensor_scalar(k.last_rows[:], k.iota_col[:], float(LAST), None, ALU.is_lt)

def heads_stage(k):
    def mean(link, dve):
        link(dve.tensor_reduce(k.att_m[:], k.att[:], AX, ALU.add))
        link(dve.tensor_reduce(k.att_bm[:], k.att_b[:], AX, ALU.add))
        link(dve.tensor_scalar(k.att_m[:], k.att_m[:], 0.25, None, ALU.mult))
        link(dve.tensor_scalar(k.att_bm[:], k.att_bm[:], 0.25, None, ALU.mult))
    node_stage(k, "heads", mean)



def order_stage(k, o, key_i, other_i, beside):
    nc, n = k.nc, o.name
    keys_in, blocks, mask1, mask2, placed, step, masks_used, sums_used, base = (
        k.sem(f"{n}_{s}") for s in ("keys_in", "blocks", "mask1", "mask2", "placed", "step",
                                    "masks_used", "sums_used", "base"))
    H = EC // 2
    JH = J // 2
    with ExitStack() as c:
        ki = k.sb(n + "_ki", [EP, EC], I32, c)
        oi = k.sb(n + "_oi", [EP, EC], I32, c)
        bi = k.sb(n + "_bi", [EP, EC], I32, c)
        bf = k.sb(n + "_bf", [EP, EC], F32, c)
        mask = k.sb(n + "_mask", [EP, 2, EC], BF16, c)
        pick = k.sb(n + "_pick", [EP, 2 * NB - 1], BF16, c)
        totals = k.sb(n + "_totals", [NB, EC], F32, c)
        upto = k.sb(n + "_upto", [NB, EC], F32, c)
        first = k.sb(n + "_first", [NB, EC], F32, c)
        onesr = k.sb(n + "_onesr", [NB, EC], F32, c)
        tiles_i = k.sb(n + "_tiles_i", [NB, 1], I32, c)
        tiles = k.sb(n + "_tiles", [NB, 1], F32, c)
        start = k.sb(n + "_start", [NB, 2], F32, c)
        past = k.sb(n + "_past", [NB, J], BF16, c)
        rank = k.sb(n + "_rank", [EP, EC], F32, c)
        part = k.sb(n + "_part", [EP, EC], F32, c)
        low = k.sb(n + "_low", [EP, EC], I32, c)
        pt = k.ps(n + "_pt", [P, 2, 512], c)
        pr = k.ps(n + "_pr", [P, 2, 2, 512], c)
        pb = k.ps(n + "_pb", [P, 2, 512], c)
        beside = beside(c)
        with k.block() as block:
            @block.sync
            def _(sp):
                sp.dma_start(ki[:], key_i.rearrange("(p c) -> p c", p=EP)).then_inc(keys_in, 16)
                sp.dma_start(oi[:], other_i.rearrange("(p c) -> p c", p=EP)).then_inc(keys_in, 16)
                sp.wait_ge(keys_in, 32)
                beside.sync(sp)

            if isinstance(beside, FeatureScatter):
                @block.gpsimd
                def _(pool):
                    beside.gpsimd(pool)

                @block.scalar
                def _(act):
                    beside.scalar(act)

            @block.tensor
            def _(pe):
                for b in range(NB):
                    pe.wait_ge(mask1, b + 1)
                    for h in range(2):
                        mm = pe.matmul(pt[0:NB, h, 0:H], pick[:, NB - 1 - b:2 * NB - 1 - b],
                                       mask[:, b % 2, h * H:(h + 1) * H], start=(b == 0), stop=(b == NB - 1))
                    mm.then_inc(masks_used, 1)
                pe.wait_ge(blocks, 1)
                pe.matmul(pb[0:NB, 0, 0:1], k.before[0:NB, 0:NB], tiles[:], start=True, stop=True).then_inc(base, 1)
                pe.wait_ge(blocks, 2)
                for h in range(2):
                    mm = pe.matmul(pb[:, h, 0:JH], k.ones_h[0:NB, :], past[:, h * JH:(h + 1) * JH],
                                   start=True, stop=True)
                mm.then_inc(base, 1)
                for b in range(NB):
                    pe.wait_ge(mask2, b + 1)
                    if b >= 2:
                        pe.wait_ge(sums_used, b - 1)
                    for h in range(2):
                        pe.matmul(pr[0:EP, b % 2, h, 0:H], k.before_h[0:EP, 0:EP],
                                  mask[:, b % 2, h * H:(h + 1) * H], start=True, stop=False)
                        mm = pe.matmul(pr[0:EP, b % 2, h, 0:H], k.ident[0:NB, b:b + 1].to_broadcast([NB, EP]),
                                       first[:, h * H:(h + 1) * H], start=False, stop=True)
                    mm.then_inc(placed, 1)

            @block.vector
            def _(dve):
                done = [0]

                def link(ins):
                    done[0] += 1
                    ins.then_inc(step, 1)
                    dve.wait_ge(step, done[0])

                dve.memset(pick[:], 0.0)
                dve.memset(rank[:], 0.0)
                link(dve.memset(onesr[:], 1.0))
                link(dve.memset(pick[:, NB - 1:NB], 1.0))
                dve.wait_ge(keys_in, 32)
                link(dve.tensor_scalar(bi[:], ki[:], 7, None, ALU.arith_shift_right))
                link(dve.tensor_scalar(low[:], ki[:], P - 1, None, ALU.bitwise_and))
                link(dve.tensor_copy(bf[:], bi[:]))
                dve.tensor_copy(o.meta[:, :, 0], low[:])
                dve.tensor_copy(o.meta[:, :, 1], oi[:])
                for b in range(NB):
                    if b >= 2:
                        dve.wait_ge(masks_used, b - 1)
                    dve.tensor_scalar(mask[:, b % 2, :], bf[:], float(b), None, ALU.is_equal).then_inc(mask1, 1)
                dve.wait_ge(masks_used, NB)
                link(dve.tensor_copy(totals[:].rearrange("b (h c) -> b h c", h=2), pt[0:NB, :, 0:H]))
                link(dve.tensor_tensor_scan(upto[:], onesr[:], totals[:], 0.0, ALU.mult, ALU.add))
                link(dve.tensor_tensor(first[:], upto[:], totals[:], ALU.subtract))
                link(dve.tensor_scalar(tiles[:], upto[:, EC - 1:EC], float(2 * P - 1), None, ALU.add))
                link(dve.tensor_copy(tiles_i[:], tiles[:]))
                link(dve.tensor_scalar(tiles_i[:], tiles_i[:], 8, None, ALU.arith_shift_right))
                link(dve.tensor_scalar(tiles_i[:], tiles_i[:], 1, None, ALU.arith_shift_left))
                dve.tensor_copy(tiles[:], tiles_i[:]).then_inc(blocks, 1)
                dve.wait_ge(base, 1)
                link(dve.tensor_copy(start[:, 0:1], pb[0:NB, 0, 0:1]))
                link(dve.tensor_tensor(start[:, 1:2], start[:, 0:1], tiles[:], ALU.add))
                dve.tensor_scalar(past[:], k.iota_tile[0:NB, :], start[:, 1:2], None, ALU.is_ge).then_inc(blocks, 1)
                link(dve.tensor_scalar(start[:, 0:1], start[:, 0:1], float(P), None, ALU.mult))
                link(dve.tensor_scalar(first[:], first[:], start[:, 0:1], None, ALU.add))
                dve.wait_ge(base, 2)
                link(dve.tensor_scalar(o.block_f[:].rearrange("p (h j) -> p h j", h=2), pb[:, :, 0:JH],
                                       float(NB - 1), None, ALU.min))
                dve.tensor_copy(o.block_i[:], o.block_f[:].rearrange("p (n t) -> p n t", t=2)[:, :, 0])

                def make_mask(b):
                    if b >= 2:
                        dve.wait_ge(placed, b - 1)
                    dve.tensor_scalar(mask[:, b % 2, :], bf[:], float(b), None, ALU.is_equal).then_inc(mask2, 1)

                make_mask(0)
                for b in range(NB):
                    if b + 1 < NB:
                        make_mask(b + 1)
                    dve.wait_ge(placed, b + 1)
                    dve.wait_ge(mask2, b + 1)
                    ins = dve.tensor_tensor(part[:].rearrange("p (h c) -> p h c", h=2), pr[0:EP, b % 2, :, 0:H],
                                            mask[:, b % 2, :].rearrange("p (h c) -> p h c", h=2), ALU.mult)
                    ins.then_inc(sums_used, 1)
                    dve.wait_ge(sums_used, b + 1)
                    link(dve.tensor_tensor(rank[:], rank[:], part[:], ALU.add))
                link(dve.tensor_copy(bi[:], rank[:]))
                link(dve.tensor_scalar(low[:], bi[:], P - 1, None, ALU.bitwise_and))
                link(dve.tensor_scalar(bi[:], bi[:], 7, None, ALU.arith_shift_right))
                link(dve.tensor_scalar(low[:], low[:], J, None, ALU.mult))
                dve.tensor_tensor(o.row[:], low[:], bi[:], ALU.add)


CW = 8


class BlankRows:

    def __init__(self, k, o, so, c):
        self.k, self.o, self.so = k, o, so
        self.blanked = k.sem("blanked")
        self.loaded = k.sem("loaded")

    def sync(self, sp):
        for table, blank, width in ((self.o.rows_dram, self.k.blank_row, RW), (self.so.ids_dram, self.k.blank_ids, 2)):
            sp.dma_start(table.rearrange("(p r j) w -> p r (j w)", p=P, j=8),
                         blank[:].rearrange("p j w -> p (j w)").unsqueeze(1).to_broadcast([P, J // 8, 8 * width])
                         ).then_inc(self.blanked, 16)
        for dst, src in self.k.loads:
            sp.dma_start(dst, src).then_inc(self.loaded, 16)
        sp.wait_ge(self.blanked, 32)
        sp.wait_ge(self.loaded, 16 * len(self.k.loads))


class FeatureScatter:

    def __init__(self, k, o, edge_attr, c):
        self.k, self.o = k, o
        self.attr = edge_attr.rearrange("(p c) f -> p c f", p=EP)
        self.staged, self.begun = k.sem("f_staged"), k.sem("f_begun")
        self.features_in = [k.sem(f"f_features_in{p}") for p in range(2)]
        self.sent = [k.sem(f"f_sent{p}") for p in range(2)]
        self.rows = k.sb("f_rows", [EP, 2, CW, RW], F32, c)
        self.at = k.sb("f_at", [EP, 2, CW], I32, c)

    def sync(self, sp):
        def body(i, first):
            for p in range(2):
                if not first:
                    sp.wait_ge(self.sent[p], 16 * CW * i)
                sp.dma_start(self.rows[:, p, :, 0:DE], self.attr[:, ds(i * 2 * CW + p * CW, CW), :]
                             ).then_inc(self.features_in[p], 16)
        steps(sp, EC // (2 * CW), body)

    def scalar(self, act):
        def body(i, first):
            for p in range(2):
                if not first:
                    act.wait_ge(self.sent[p], 16 * CW * i)
                c0 = i * 2 * CW + p * CW
                act.copy(self.at[:, p, :], self.o.row[:, ds(c0, CW)]).then_inc(self.staged, 1)
                act.copy(self.rows[:, p, :, DE:RW], self.o.meta[:, ds(c0, CW), :]).then_inc(self.staged, 1)
        steps(act, EC // (2 * CW), body)

    def gpsimd(self, pool):
        def body(i, first):
            for p in range(2):
                pool.wait_ge(self.features_in[p], 16 * (i + 1))
                pool.wait_ge(self.staged, 4 * i + 2 * p + 2)
                pool.sem_inc(self.begun, 1)
                for q in range(CW):
                    pool.indirect_dma_start(
                        self.o.rows_dram, bass.IndirectOffsetOnAxis(ap=self.at[:, p, q:q + 1], axis=0),
                        self.rows[:, p, q, :], None).then_inc(self.sent[p], 16)
        steps(pool, EC // (2 * CW), body)
        for p in range(2):
            pool.wait_ge(self.sent[p], 16 * EC // 2)


class IdScatter:

    def __init__(self, k, so, c, name, lo, hi):
        self.so, self.lo, self.hi = so, lo, hi
        self.staged, self.begun = k.sem(name + "_staged"), k.sem(name + "_begun")
        self.sent = [k.sem(f"{name}_sent{p}") for p in range(2)]
        self.at = k.sb(name + "_at", [EP, 2, CW], I32, c)
        self.ids = k.sb(name + "_ids", [EP, 2, CW, 2], F32, c)

    def gpsimd(self, pool):
        def body(i, first):
            for p in range(2):
                if not first:
                    pool.wait_ge(self.sent[p], 16 * CW * i)
                c0 = i * 2 * CW + (2 * CW * self.lo + p * CW)
                pool.tensor_copy(self.at[:, p, :], self.so.row[:, ds(c0, CW)]).then_inc(self.staged, 1)
                pool.tensor_copy(self.ids[:, p], self.so.meta[:, ds(c0, CW), :]).then_inc(self.staged, 1)
                pool.wait_ge(self.staged, 4 * i + 2 * p + 2)
                pool.sem_inc(self.begun, 1)
                for q in range(CW):
                    pool.indirect_dma_start(
                        self.so.ids_dram, bass.IndirectOffsetOnAxis(ap=self.at[:, p, q:q + 1], axis=0),
                        self.ids[:, p, q, :], None).then_inc(self.sent[p], 16)
        steps(pool, self.hi - self.lo, body)
        for p in range(2):
            pool.wait_ge(self.sent[p], 16 * CW * (self.hi - self.lo))



def score_stage(k, o, ids):
    nc = k.nc
    taken, scored, others, spread, scores_kept, products, maxima = (k.sem("sc_" + s) for s in (
        "taken", "scored", "others", "spread", "scores_kept", "products", "maxima"))
    features_in = [k.sem(f"sc_features_in{p}") for p in range(Q)]
    rows_dram = o.rows_dram.rearrange("(e j) w -> e j w", e=P)
    with ExitStack() as c:
        ids = ids(c)
        rows = k.sb("sc_rows", [P, Q, G, RW], F32, c)
        prod = k.sb("sc_prod", [P, Q, G, DE], F32, c)
        sg = k.sb("sc_sg", [P, Q, G], F32, c)
        other = k.sb("sc_other", [P, Q, G, P], BF16, c)
        score_bc = k.ps("sc_score", [P, 4, 512], c)
        with k.block() as block:
            @block.sync
            def _(sp):
                def body(i):
                    for p in range(Q):
                        for n, s, _ in group(i, p):
                            reuse(sp, taken, n, Q, each=2)
                            reuse(sp, scored, n, Q)
                            reuse(sp, others, n, Q)
                            sp.dma_start(rows[:, s], rows_dram[:, ds(n * G, G), :]).then_inc(features_in[s], 16)
                rounds(sp, body)

            @block.gpsimd
            def _(pool):
                ids.gpsimd(pool)

            @block.tensor
            def _(pe):
                def body(i):
                    for p in range(Q):
                        for n, s, _ in group(i, p, lag=1):
                            pe.wait_ge(others, n + 1)
                            pe.wait_ge(scored, n + 1)
                            reuse(pe, maxima, n, 4)
                            for g in range(G):
                                tile = score_bc[:, s, g * P:(g + 1) * P]
                                pe.matmul(tile, other[:, s, g, :], k.far_off[:], start=True, stop=False)
                                mm = pe.matmul(tile, sg[:, s, g:g + 1].to_broadcast([P, P]), k.ident[:],
                                               start=False, stop=True)
                            mm.then_inc(spread, 1)
                rounds(pe, body)

            @block.scalar
            def _(act):
                def body(i):
                    for p in range(Q):
                        for n, s, r in group(i, p):
                            act.wait_ge(features_in[s], 16 * (r + 1))
                            nc.scalar.copy(o.slot[:, ds(n * G, G), :], rows[:, s, :, DE:RW]).then_inc(taken, 1)
                            nc.scalar.copy(o.lo_h[:, ds(n * G, G)], rows[:, s, :, DE]).then_inc(taken, 1)
                        for n, s, _ in group(i, p, lag=1):
                            act.wait_ge(scored, n + 1)
                            nc.scalar.copy(k.scores[:, ds(n * G, G)], sg[:, s, :]).then_inc(scores_kept, 1)
                rounds(act, body)

            @block.vector
            def _(dve):
                w2 = k.att_m[:, D:D + DE].unsqueeze(1).to_broadcast([P, G, DE])

                def body(i):
                    for p in range(Q):
                        for n, s, r in group(i, p):
                            dve.wait_ge(features_in[s], 16 * (r + 1))
                            dve.tensor_tensor(prod[:, s], rows[:, s, :, 0:DE], w2, ALU.mult).then_inc(products, 1)
                            reuse(dve, spread, n, Q)
                            dve.tensor_tensor(other[:, s], over_blocks(k.iota_row[:], [P, G, P]),
                                              wide(rows[:, s, :, DE], G, [P, G, P]), ALU.not_equal).then_inc(others, 1)
                            reuse(dve, scores_kept, n, Q)
                            dve.wait_ge(products, n + 1)
                            dve.tensor_reduce(sg[:, s], prod[:, s], AX, ALU.add).then_inc(scored, 1)
                        for n, s, _ in group(i, p, lag=2):
                            dve.wait_ge(spread, n + 1)
                            dve.tensor_reduce(k.pair_max[:, ds(n * (G // 2), G // 2)],
                                              score_bc[:, s].rearrange("p (q e) -> p q e", q=G // 2), AX, ALU.max
                                              ).then_inc(maxima, 1)
                rounds(dve, body)


def node_maximum_stage(k, o):
    tops, step = k.sem("nm_tops"), k.sem("nm_step")
    with ExitStack() as c:
        one = k.sb("nm_one", [P, 2, J // 2], F32, c)
        two = k.sb("nm_two", [P, 2, J // 2], F32, c)
        pair_block = k.sb("nm_pair_block", [P, J // 2], F32, c)
        prod = k.sb("nm_prod", [P, NB, D], F32, c)
        mt = k.sb("nm_mt", [P, NB], F32, c)
        own = k.sb("nm_own", [P, NB], F32, c)
        with k.block() as block:
            @block.vector
            def _(dve):
                link = Chain(dve, step)
                link(dve.tensor_copy(pair_block[:], o.block_f[:].rearrange("p (n t) -> p n t", t=2)[:, :, 0]))
                link(dve.tensor_tensor(prod[:], k.X[:], over_blocks(k.att_m[:, 0:D], [P, NB, D]), ALU.mult))
                link(dve.tensor_reduce(mt[:], prod[:], AX, ALU.add))
                link(dve.tensor_scalar(own[:], mt[:], k.att_bm[:], None, ALU.add))
                for b in range(NB):
                    link(dve.tensor_scalar(one[:, b % 2], pair_block[:], float(b), -BIG, ALU.not_equal, ALU.mult))
                    link(dve.tensor_tensor(two[:, b % 2], one[:, b % 2], k.pair_max[:], ALU.add))
                    dve.tensor_reduce(mt[:, b:b + 1], two[:, b % 2], AX, ALU.max).then_inc(tops, 1)
                dve.wait_ge(tops, NB)
                link(dve.tensor_tensor(mt[:], mt[:], own[:], ALU.add))
                link(dve.tensor_tensor(own[:], own[:], mt[:], ALU.subtract))
                link(dve.tensor_copy(k.shift[:, :, 0], own[:]))
                link(dve.tensor_tensor(own[:], own[:], k.shift[:, :, 0], ALU.subtract))
                link(dve.tensor_copy(k.shift[:, :, 1], own[:]))
                link(dve.tensor_tensor(own[:], own[:], k.shift[:, :, 1], ALU.subtract))
                link(dve.tensor_copy(k.shift[:, :, 2], own[:]))


@contextmanager
def blocks_of(k, eng, o, i, lag=0):
    back = -(-lag // 2) * 2
    start = Q * i - back
    skip = max(0, -start) if isinstance(i, int) else 0
    count = back - lag + Q - skip
    if isinstance(i, int):
        count = min(count, Q * LOOPS - start - skip)
    registers = [eng.alloc_register(f"block{k.taken + n}") for n in range(count * (G // 2))]
    k.taken += len(registers)
    if registers:
        eng.load(registers, o.block_i[0:1, ds((start + skip) * (G // 2), len(registers))])
    values = [eng.snap(reg, donate=True, min_val=0, max_val=NB - 1) for reg in registers]
    yield lambda p, q: values[(p - lag + back - skip) * (G // 2) + q]
    for reg in registers:
        eng.free_register(reg)


def add_pair(dve, acc, blocks, n, p, q, added, sums):
    b = blocks(p, q)
    if q or not isinstance(n, int) or n:
        dve.wait_ge(added, n * (G // 2) + q)
    dve.tensor_tensor(acc[:, ds(b, 1), :], acc[:, ds(b, 1), :], sums.unsqueeze(1), ALU.add).then_inc(added, 1)


def sum_pairs(pe, oh, rows, sums):
    for g in range(G):
        mm = pe.matmul(sums(g // 2), oh(g), rows(g), start=(g % 2 == 0), stop=(g % 2 == 1))
    return mm


def spread_nodes(pe, k, o, bank, n):
    for g in range(G):
        mm = pe.matmul(bank[:, g * P:(g + 1) * P], o.lo_h[:, ds(n * G + g, 1)].to_broadcast([P, P]), k.ident_h[:],
                       start=True, stop=True)
    return mm


def attention_sum_stage(k, o, acc, ids):
    nc = k.nc
    (cleared, spread, onehots, looked_up, exponents, weights, weighted, summed, added, ones_put,
     shifted, endhots) = (k.sem("as_" + s) for s in ("cleared", "spread", "onehots", "looked_up", "exponents",
                                            "weights", "weighted", "summed", "added", "ones_put", "shifted", "endhots"))
    features_in = [k.sem(f"as_features_in{p}") for p in range(Q)]
    rows_dram = o.rows_dram.rearrange("(e j) w -> e j w", e=P)
    with ExitStack() as c:
        ids = ids(c)
        rows = k.sb("as_rows", [P, Q, G, RW], F32, c)
        oht = k.sb("as_oht", [P, Q, G, P], BF16, c)
        oh = k.sb("as_oh", [P, Q, G, P], F32, c)
        wrows = k.sb("as_wrows", [P, Q, G, RW], F32, c)
        d1 = k.sb("as_d1", [P, Q, G], F32, c)
        d2 = k.sb("as_d2", [P, Q, G], F32, c)
        wt = k.sb("as_wt", [P, Q, G], F32, c)
        node_bc = k.ps("as_node", [P, 2, 512], c)
        found = k.ps("as_found", [P, 2, 512], c)
        sums = k.ps("as_sums", [P, 4, 512], c)
        with k.block() as block:
            @block.sync
            def _(sp):
                def body(i):
                    for p in range(Q):
                        for n, s, _ in group(i, p):
                            reuse(sp, weighted, n, Q)
                            sp.dma_start(rows[:, s], rows_dram[:, ds(n * G, G), :]).then_inc(features_in[s], 16)
                rounds(sp, body)

            @block.gpsimd
            def _(pool):
                ids.gpsimd(pool)

            @block.tensor
            def _(pe):
                def body(i):
                    with blocks_of(k, pe, o, i, lag=1) as blocks:
                        for p in range(Q):
                            for n, s, _ in group(i, p, lag=4):
                                pe.wait_ge(weighted, n + 1)
                                pe.wait_ge(endhots, n + 1)
                                reuse(pe, added, n, 4, each=G // 2)
                                sum_pairs(pe, lambda g: oh[:, s, g, :], lambda g: wrows[:, s, g, :],
                                          lambda q: sums[:, s, q * RW:(q + 1) * RW]).then_inc(summed, 1)
                            for n, s, _ in group(i, p, lag=1):
                                pe.wait_ge(onehots, n + 1)
                                reuse(pe, shifted, n, 2)
                                for g in range(G):
                                    mm = pe.matmul(found[:, s % 2, 3 * g:3 * g + 3], oht[:, s, g, :],
                                                   k.shift[:, ds(blocks(p, g // 2), 1), :], start=True, stop=True)
                                mm.then_inc(looked_up, 1)
                            for n, s, _ in group(i, p):
                                reuse(pe, onehots, n, 2)
                                spread_nodes(pe, k, o, node_bc[:, s % 2], n).then_inc(spread, 1)
                rounds(pe, body)

            @block.scalar
            def _(act):
                def body(i):
                    for p in range(Q):
                        for n, s, r in group(i, p, lag=2):
                            act.wait_ge(features_in[s], 16 * (r + 1))
                            nc.scalar.activation(rows[:, s, :, DE + 1:RW], rows[:, s, :, DE + 1:RW], ACT.Copy, bias=1.0,
                                                 scale=0.0).then_inc(ones_put, 1)
                            act.wait_ge(exponents, n + 1)
                            reuse(act, weighted, n, Q)
                            nc.scalar.activation(wt[:, s], d2[:, s], ACT.Exp).then_inc(weights, 1)
                        for n, s, _ in group(i, p, lag=3):
                            act.wait_ge(ones_put, n + 1)
                            act.wait_ge(weights, n + 1)
                            reuse(act, summed, n, Q)
                            for g in range(G):
                                ins = nc.scalar.activation(wrows[:, s, g, :], rows[:, s, g, :], ACT.Copy, scale=wt[:, s, g:g + 1])
                            ins.then_inc(weighted, 1)
                rounds(act, body)

            @block.vector
            def _(dve):
                dve.memset(acc[:], 0.0).then_inc(cleared, 1)
                dve.wait_ge(cleared, 1)

                def body(i):
                    with blocks_of(k, dve, o, i, lag=4) as blocks:
                        for p in range(Q):
                            for n, s, _ in group(i, p, lag=3):
                                reuse(dve, summed, n, Q)
                                dve.tensor_tensor(oh[:, s], over_blocks(k.iota_row[:], [P, G, P]),
                                                  wide(o.slot[:, ds(n * G, G), 0], G, [P, G, P]), ALU.is_equal
                                                  ).then_inc(endhots, 1)
                            for n, s, _ in group(i, p, lag=1):
                                dve.wait_ge(looked_up, n + 1)
                                dve.tensor_reduce(d1[:, s], found[:, s % 2, 0:3 * G].rearrange("p (g t) -> p g t", t=3), AX,
                                                  ALU.add).then_inc(shifted, 1)
                            for n, s, _ in group(i, p, lag=4):
                                dve.wait_ge(summed, n + 1)
                                add_pair(dve, acc, blocks, n, p, 0, added, sums[:, s, 0:RW])
                            for n, s, _ in group(i, p, lag=1):
                                dve.wait_ge(shifted, n + 1)
                                reuse(dve, weights, n, Q)
                                dve.tensor_tensor(d2[:, s], d1[:, s], k.scores[:, ds(n * G, G)], ALU.add).then_inc(exponents, 1)
                            for n, s, _ in group(i, p):
                                dve.wait_ge(spread, n + 1)
                                reuse(dve, looked_up, n, Q)
                                dve.tensor_scalar(oht[:, s], node_bc[:, s % 2].rearrange("p (g e) -> p g e", g=G),
                                                  k.iota_col[:], None, ALU.is_equal).then_inc(onehots, 1)
                            for n, s, _ in group(i, p, lag=4):
                                add_pair(dve, acc, blocks, n, p, 1, added, sums[:, s, RW:2 * RW])
                rounds(dve, body)



def far_ends_stage(k, o, so):
    slots_in = k.sem("fe_slots_in")
    with k.block() as block:
        @block.sync
        def _(sp):
            sp.dma_start(so.slot[:], so.ids_dram.rearrange("(e j) w -> e j w", e=P)).then_inc(slots_in, 16)

        @block.vector
        def _(dve):
            dve.tensor_copy(o.far_i[:], o.slot[:, :, 1])
            dve.tensor_copy(o.lo[:], o.slot[:, :, 0])
            dve.wait_ge(slots_in, 16)
            dve.tensor_copy(so.far_i[:], so.slot[:, :, 1])
            dve.tensor_copy(so.lo[:], so.slot[:, :, 0])
            dve.tensor_copy(so.lo_h[:], so.slot[:, :, 0])


def stage_ids(act, o, far, n, s):
    return act.copy(far[:, s], o.far_i[:, ds(n * G, G)])


def gather_rows(pool, table, rows, far, s, rows_in):
    for g in range(G):
        pool.indirect_dma_start(rows[:, s, g, 0:table.shape[1]], None, table,
                                bass.IndirectOffsetOnAxis(ap=far[:, s, g:g + 1], axis=0)).then_inc(rows_in[s], 16)


def end_onehots(dve, k, o, oh, n, s):
    return dve.tensor_tensor(oh[:, s], over_blocks(k.iota_row[:], [P, G, P]),
                             wide(o.lo[:, ds(n * G, G)], G, [P, G, P]), ALU.is_equal)


def gather_sum_stage(k, name, o, table, acc, W=D):
    cleared, staged, onehots, summed, added, begun = (k.sem(f"{name}_{s}") for s in (
        "cleared", "staged", "onehots", "summed", "added", "begun"))
    rows_in = [k.sem(f"{name}_rows_in{p}") for p in range(Q)]
    with ExitStack() as c:
        rows = k.sb(name + "_rows", [P, Q, G, W], F32, c)
        far = k.sb(name + "_far", [P, Q, G], I32, c)
        oh = k.sb(name + "_oh", [P, Q, G, P], F32, c)
        sums = k.ps(name + "_sums", [P, Q, 512], c)
        with k.block() as block:
            @block.scalar
            def _(act):
                def body(i):
                    for p in range(Q):
                        for n, s, r in group(i, p):
                            if not isinstance(r, int) or r:
                                act.wait_ge(rows_in[s], 16 * G * r)
                            stage_ids(act, o, far, n, s).then_inc(staged, 1)
                rounds(act, body)

            @block.gpsimd
            def _(pool):
                def body(i):
                    for p in range(Q):
                        for n, s, _ in group(i, p):
                            pool.wait_ge(staged, n + 1)
                            reuse(pool, summed, n, Q)
                            pool.sem_inc(begun, 1)
                            gather_rows(pool, table, rows, far, s, rows_in)
                rounds(pool, body)

            @block.tensor
            def _(pe):
                def body(i):
                    for p in range(Q):
                        for n, s, r in group(i, p):
                            if isinstance(n, int) and n == 0:
                                pe.wait_ge(cleared, 2 if W > D else 1)
                            pe.wait_ge(onehots, n + 1)
                            pe.wait_ge(rows_in[s], 16 * G * (r + 1))
                            reuse(pe, added, n, Q, each=G // 2)
                            sum_pairs(pe, lambda g: oh[:, s, g, :], lambda g: rows[:, s, g, :],
                                      lambda q: sums[:, s, 256 * q:256 * q + W]).then_inc(summed, 1)
                rounds(pe, body)

            @block.vector
            def _(dve):
                dve.memset(acc[:], 0.0).then_inc(cleared, 1)
                if W > D:
                    dve.memset(rows[:, :, :, D:W], 1.0).then_inc(cleared, 1)
                dve.wait_ge(cleared, 1)

                def body(i):
                    with blocks_of(k, dve, o, i, lag=2) as blocks:
                        for p in range(Q):
                            for n, s, _ in group(i, p):
                                reuse(dve, summed, n, Q)
                                end_onehots(dve, k, o, oh, n, s).then_inc(onehots, 1)
                            for n, s, _ in group(i, p, lag=2):
                                dve.wait_ge(summed, n + 1)
                                for q in range(G // 2):
                                    add_pair(dve, acc, blocks, n, p, q, added, sums[:, s, 256 * q:256 * q + W])
                rounds(dve, body)



VW = 3 * DE


def tanh_stage(k, o, table, qky, edges_dram):
    nc = k.nc
    (staged, spread, onehots, looked_up, pre, tanhs, prods, scored, begun) = (k.sem("th_" + s) for s in (
        "staged", "spread", "onehots", "looked_up", "pre", "tanhs", "prods", "scored", "begun"))
    rows_in = [k.sem(f"th_rows_in{p}") for p in range(Q)]
    stored = [k.sem(f"th_stored{p}") for p in range(Q)]
    out_rows = edges_dram.rearrange("(e j) w -> e j w", e=P)
    with ExitStack() as c:
        rows = k.sb("th_rows", [P, Q, G, VW], F32, c)
        far = k.sb("th_far", [P, Q, G], I32, c)
        oht = k.sb("th_oht", [P, Q, G, P], F32, c)
        sumqk = k.sb("th_sum", [P, Q, G, DE], F32, c)
        prod = k.sb("th_prod", [P, Q, G, DE], F32, c)
        node_bc = k.ps("th_node", [P, 4, 512], c)
        query = k.ps("th_query", [P, 4, 512], c)
        with k.block() as block:
            @block.scalar
            def _(act):
                def body(i):
                    for p in range(Q):
                        for n, s, r in group(i, p):
                            if not isinstance(r, int) or r:
                                act.wait_ge(rows_in[s], 16 * G * r)
                            stage_ids(act, o, far, n, s).then_inc(staged, 1)
                        for n, s, _ in group(i, p, lag=2):
                            act.wait_ge(pre, n + 1)
                            nc.scalar.activation(rows[:, s, :, 0:DE], sumqk[:, s], ACT.Tanh).then_inc(tanhs, 1)
                rounds(act, body)

            @block.sync
            def _(sp):
                def body(i):
                    for p in range(Q):
                        for n, s, _ in group(i, p):
                            sp.wait_ge(tanhs, n + 1)
                            sp.dma_start(out_rows[:, ds(n * G, G), :], rows[:, s]).then_inc(stored[s], 16)
                rounds(sp, body)
                for p in range(Q):
                    sp.wait_ge(stored[p], 16 * LOOPS)

            @block.gpsimd
            def _(pool):
                def body(i):
                    for p in range(Q):
                        for n, s, r in group(i, p):
                            pool.wait_ge(staged, n + 1)
                            if not isinstance(r, int) or r:
                                pool.wait_ge(stored[s], 16 * r)
                            reuse(pool, prods, n, Q)
                            pool.sem_inc(begun, 1)
                            gather_rows(pool, table, rows, far, s, rows_in)
                rounds(pool, body)

            @block.tensor
            def _(pe):
                def body(i):
                    with blocks_of(k, pe, o, i, lag=1) as blocks:
                        for p in range(Q):
                            for n, s, _ in group(i, p):
                                reuse(pe, onehots, n, 4)
                                spread_nodes(pe, k, o, node_bc[:, s], n).then_inc(spread, 1)
                            for n, s, _ in group(i, p, lag=1):
                                pe.wait_ge(onehots, n + 1)
                                reuse(pe, pre, n, 4)
                                for g in range(G):
                                    mm = pe.matmul(query[:, s, g * DE:(g + 1) * DE], oht[:, s, g, :],
                                                   qky[:, ds(blocks(p, g // 2), 1), 0:DE], start=True, stop=True)
                                mm.then_inc(looked_up, 1)
                rounds(pe, body)

            @block.vector
            def _(dve):
                phi = k.r["phi"][:].unsqueeze(1).to_broadcast([P, G, DE])

                def body(i):
                    for p in range(Q):
                        for n, s, _ in group(i, p):
                            dve.wait_ge(spread, n + 1)
                            reuse(dve, looked_up, n, Q)
                            dve.tensor_scalar(oht[:, s], node_bc[:, s].rearrange("p (g e) -> p g e", g=G), k.iota_col[:],
                                              None, ALU.is_equal).then_inc(onehots, 1)
                        for n, s, _ in group(i, p, lag=3):
                            dve.wait_ge(tanhs, n + 1)
                            reuse(dve, scored, n, Q)
                            dve.tensor_tensor(prod[:, s], rows[:, s, :, 0:DE], phi, ALU.mult).then_inc(prods, 1)
                        for n, s, r in group(i, p, lag=2):
                            dve.wait_ge(looked_up, n + 1)
                            dve.wait_ge(rows_in[s], 16 * G * (r + 1))
                            reuse(dve, tanhs, n, Q)
                            dve.tensor_tensor(sumqk[:, s], query[:, s, 0:G * DE].rearrange("p (g f) -> p g f", g=G),
                                              rows[:, s, :, 0:DE], ALU.add).then_inc(pre, 1)
                        for n, s, _ in group(i, p, lag=3):
                            dve.wait_ge(prods, n + 1)
                            dve.tensor_reduce(k.scores[:, ds(n * G, G)], prod[:, s], AX, ALU.add).then_inc(scored, 1)
                rounds(dve, body)


def softmax_weights_stage(k, o):
    nc = k.nc
    step, largest, spread, shifted, done = (k.sem("sw_" + s) for s in ("step", "largest", "spread", "shifted", "done"))
    with ExitStack() as c:
        none = k.sb("sw_none", [P, J], F32, c)
        col = k.sb("sw_col", [P, 1], F32, c)
        top = k.sb("sw_top", [P, 1], F32, c)
        neg = k.sb("sw_neg", [P, 1], F32, c)
        with k.block() as block:
            @block.vector
            def _(dve):
                dve.tensor_scalar(none[:], o.lo[:], 0.0, -BIG, ALU.is_lt, ALU.mult).then_inc(step, 1)
                dve.wait_ge(step, 1)
                dve.tensor_tensor(k.scores[:], k.scores[:], none[:], ALU.add).then_inc(step, 1)
                dve.wait_ge(step, 2)
                dve.tensor_reduce(col[:], k.scores[:], AX, ALU.max).then_inc(largest, 1)
                dve.wait_ge(spread, 1)
                dve.tensor_scalar(neg[:], top[:], -1.0, None, ALU.mult).then_inc(shifted, 1)

            @block.gpsimd
            def _(pool):
                pool.wait_ge(largest, 1)
                nc.gpsimd.partition_all_reduce(top[:], col[:], P, RMAX).then_inc(spread, 1)

            @block.scalar
            def _(act):
                act.wait_ge(shifted, 1)
                nc.scalar.activation(k.scores[:], k.scores[:], ACT.Exp, bias=neg[:]).then_inc(done, 1)


def weighted_sum_stage(k, o, edges_dram, acc):
    nc = k.nc
    W = VW + 1
    cleared, staged, onehots, weighted, summed, added, ones_put = (k.sem("ws_" + s) for s in (
        "cleared", "staged", "onehots", "weighted", "summed", "added", "ones_put"))
    rows_in = [k.sem(f"ws_rows_in{p}") for p in range(Q)]
    rows_dram = edges_dram.rearrange("(e j) w -> e j w", e=P)
    with ExitStack() as c:
        rows = k.sb("ws_rows", [P, Q, G, W], F32, c)
        wrows = k.sb("ws_wrows", [P, Q, G, W], F32, c)
        oh = k.sb("ws_oh", [P, Q, G, P], F32, c)
        wt = k.sb("ws_wt", [P, Q, G], F32, c)
        sums = k.ps("ws_sums", [P, Q, G // 2, 256], c)
        with k.block() as block:
            @block.sync
            def _(sp):
                sp.wait_ge(ones_put, 1)

                def body(i):
                    for p in range(Q):
                        for n, s, _ in group(i, p):
                            reuse(sp, weighted, n, Q)
                            sp.dma_start(rows[:, s, :, 0:VW], rows_dram[:, ds(n * G, G), :]).then_inc(rows_in[s], 16)
                rounds(sp, body)

            @block.scalar
            def _(act):
                def body(i):
                    for p in range(Q):
                        for n, s, r in group(i, p):
                            reuse(act, weighted, n, Q)
                            nc.scalar.copy(wt[:, s], k.scores[:, ds(n * G, G)]).then_inc(staged, 1)
                            act.wait_ge(rows_in[s], 16 * (r + 1))
                            reuse(act, summed, n, Q)
                            act.wait_ge(staged, n + 1)
                            for g in range(G):
                                ins = nc.scalar.activation(wrows[:, s, g, :], rows[:, s, g, :], ACT.Copy, scale=wt[:, s, g:g + 1])
                            ins.then_inc(weighted, 1)
                rounds(act, body)

            @block.tensor
            def _(pe):
                def body(i):
                    for p in range(Q):
                        for n, s, _ in group(i, p):
                            pe.wait_ge(weighted, n + 1)
                            pe.wait_ge(onehots, n + 1)
                            reuse(pe, added, n, Q, each=G // 2)
                            sum_pairs(pe, lambda g: oh[:, s, g, :], lambda g: wrows[:, s, g, :],
                                      lambda q: sums[:, s, q, 0:W]).then_inc(summed, 1)
                rounds(pe, body)

            @block.vector
            def _(dve):
                dve.memset(rows[:, :, :, VW:W], 1.0).then_inc(ones_put, 1)
                dve.memset(acc[:], 0.0).then_inc(cleared, 1)
                dve.wait_ge(cleared, 1)

                def body(i):
                    with blocks_of(k, dve, o, i, lag=2) as blocks:
                        for p in range(Q):
                            for n, s, _ in group(i, p, lag=2):
                                dve.wait_ge(summed, n + 1)
                                add_pair(dve, acc, blocks, n, p, 0, added, sums[:, s, 0, 0:W])
                            for n, s, _ in group(i, p):
                                reuse(dve, summed, n, Q)
                                end_onehots(dve, k, o, oh, n, s).then_inc(onehots, 1)
                            for n, s, _ in group(i, p, lag=2):
                                add_pair(dve, acc, blocks, n, p, 1, added, sums[:, s, 1, 0:W])
                rounds(dve, body)



def split_stage(k, x, parts, rest):
    def split(link, dve):
        link(dve.tensor_copy(parts[:, 0], x))
        link(dve.tensor_tensor(rest, x, parts[:, 0], ALU.subtract))
        link(dve.tensor_copy(parts[:, 1], rest))
        link(dve.tensor_tensor(rest, rest, parts[:, 1], ALU.subtract))
        link(dve.tensor_copy(parts[:, 2], rest))
    node_stage(k, "split", split)


def message_stage(k, o, table, b_parts, acc):
    nc = k.nc
    (cleared, staged, spread, turned, onehots, features_t, hidden, hidden_t, second, biased, messages, endhots,
     summed, added, begun) = (k.sem("ms_" + s) for s in (
         "cleared", "staged", "spread", "turned", "onehots", "features_t", "hidden", "hidden_t", "second", "biased",
         "messages", "endhots", "summed", "added", "begun"))
    rows_in = [k.sem(f"ms_rows_in{p}") for p in range(Q)]
    features_in = [k.sem(f"ms_features_in{p}") for p in range(Q)]
    rows_dram = o.rows_dram.rearrange("(e j) w -> e j w", e=P)

    def four(ap):
        return ap.rearrange("p (g f) -> p g f", g=G)

    with ExitStack() as c:
        feat = k.sb("ms_feat", [P, Q, G, DE], F32, c)
        rows = k.sb("ms_rows", [P, Q, G, D], F32, c)
        far = k.sb("ms_far", [P, Q, G], I32, c)
        oht = k.sb("ms_oht", [P, Q, G, P], BF16, c)
        oh = k.sb("ms_oh", [P, Q, G, P], F32, c)
        ft = k.sb("ms_ft", [P, Q, G // 2, P], F32, c)
        ht = k.sb("ms_ht", [P, Q, G, P], F32, c)
        m = k.sb("ms_m", [P, Q, G, D], F32, c)
        nodes = k.ps("ms_nodes", [P, 2, 512], c)
        pfeat = k.ps("ms_pfeat", [P, 512], c)
        phid = k.ps("ms_phid", [P, 2, 512], c)
        pm = k.ps("ms_pm", [P, 2, 512], c)
        sums = k.ps("ms_sums", [P, 512], c)
        with k.block() as block:
            @block.sync
            def _(sp):
                def body(i):
                    for p in range(Q):
                        for n, s, _ in group(i, p):
                            reuse(sp, turned, n, Q)
                            sp.dma_start(feat[:, s], rows_dram[:, ds(n * G, G), 0:DE]).then_inc(features_in[s], 16)
                rounds(sp, body)

            @block.gpsimd
            def _(pool):
                def body(i):
                    for p in range(Q):
                        for n, s, _ in group(i, p):
                            pool.wait_ge(staged, n + 1)
                            reuse(pool, hidden, n, Q)
                            pool.sem_inc(begun, 1)
                            gather_rows(pool, table, rows, far, s, rows_in)
                rounds(pool, body)

            @block.tensor
            def _(pe):
                def body(i):
                    with blocks_of(k, pe, o, i, lag=2) as blocks:
                        for p in range(Q):
                            for n, s, r in group(i, p):
                                reuse(pe, onehots, n, 2)
                                spread_nodes(pe, k, o, nodes[:, s % 2], n).then_inc(spread, 1)
                                pe.wait_ge(features_in[s], 16 * (r + 1))
                                reuse(pe, features_t, n, 1)
                                for q in range(G // 2):
                                    mm = pe.transpose(pfeat[:, q * P:(q + 1) * P],
                                                      feat[:, s, 2 * q:2 * q + 2, :].rearrange("p g f -> p (g f)"), k.ident[:])
                                mm.then_inc(turned, 1)
                            for n, s, _ in group(i, p, lag=4):
                                pe.wait_ge(messages, n + 1)
                                pe.wait_ge(endhots, n + 1)
                                reuse(pe, added, n, 1, each=G // 2)
                                sum_pairs(pe, lambda g: oh[:, s, g, :], lambda g: m[:, s, g, :],
                                          lambda q: sums[:, q * P:(q + 1) * P]).then_inc(summed, 1)
                            for n, s, _ in group(i, p, lag=3):
                                pe.wait_ge(hidden_t, n + 1)
                                reuse(pe, biased, n, 2)
                                for g in range(G):
                                    mm = pe.matmul(pm[:, s % 2, g * P:(g + 1) * P], ht[:, s, g, :], k.w["W2"][:],
                                                   start=True, stop=True)
                                mm.then_inc(second, 1)
                            for n, s, r in group(i, p, lag=2):
                                pe.wait_ge(onehots, n + 1)
                                pe.wait_ge(features_t, n + 1)
                                reuse(pe, hidden_t, n, 2)
                                pe.wait_ge(rows_in[s], 16 * G * (r + 1))
                                for q in range(G // 2):
                                    pair = phid[:, s % 2, 2 * q * P:2 * (q + 1) * P]
                                    both = oht[:, s, 2 * q:2 * q + 2, :].rearrange("p g e -> p (g e)")
                                    for part in range(3):
                                        if part == 2:
                                            for t in range(2):
                                                tile = pair[:, t * P:(t + 1) * P]
                                                pe.matmul(tile, k.w1c[:, t, :], ft[:, s, q, :], start=False, stop=False)
                                                pe.matmul(tile, rows[:, s, 2 * q + t, :], k.ident[:], start=False, stop=False)
                                        mm = pe.matmul(pair, b_parts[:, part, ds(blocks(p, q), 1), :].rearrange("p b f -> p (b f)"),
                                                       both, start=(part == 0), stop=(part == 2))
                                mm.then_inc(hidden, 1)
                rounds(pe, body)

            @block.scalar
            def _(act):
                def body(i):
                    for p in range(Q):
                        for n, s, r in group(i, p):
                            if not isinstance(r, int) or r:
                                act.wait_ge(rows_in[s], 16 * G * r)
                            stage_ids(act, o, far, n, s).then_inc(staged, 1)
                            act.wait_ge(turned, n + 1)
                            reuse(act, hidden, n, Q)
                            nc.scalar.copy(ft[:, s], pfeat[:, 0:(G // 2) * P].rearrange("p (q e) -> p q e", q=G // 2)
                                           ).then_inc(features_t, 1)
                        for n, s, _ in group(i, p, lag=3):
                            act.wait_ge(biased, n + 1)
                            nc.scalar.activation(m[:, s], m[:, s], ACT.Relu).then_inc(messages, 1)
                        for n, s, _ in group(i, p, lag=2):
                            act.wait_ge(hidden, n + 1)
                            reuse(act, second, n, Q)
                            nc.scalar.activation(ht[:, s], four(phid[:, s % 2]), ACT.Relu).then_inc(hidden_t, 1)
                rounds(act, body)

            @block.vector
            def _(dve):
                dve.memset(acc[:], 0.0).then_inc(cleared, 1)
                dve.wait_ge(cleared, 1)

                def body(i):
                    with blocks_of(k, dve, o, i, lag=4) as blocks:
                        for p in range(Q):
                            for n, s, _ in group(i, p):
                                dve.wait_ge(spread, n + 1)
                                reuse(dve, hidden, n, Q)
                                dve.tensor_scalar(oht[:, s], four(nodes[:, s % 2]), k.iota_col[:], None, ALU.is_equal
                                                  ).then_inc(onehots, 1)
                            for n, s, _ in group(i, p, lag=3):
                                reuse(dve, summed, n, Q)
                                end_onehots(dve, k, o, oh, n, s).then_inc(endhots, 1)
                                dve.wait_ge(second, n + 1)
                                dve.tensor_tensor(m[:, s], four(pm[:, s % 2]), over_blocks(k.r["b2"][:], [P, G, D]),
                                                  ALU.add).then_inc(biased, 1)
                            for n, s, _ in group(i, p, lag=4):
                                dve.wait_ge(summed, n + 1)
                                for q in range(G // 2):
                                    add_pair(dve, acc, blocks, n, p, q, added, sums[:, q * P:(q + 1) * P])
                rounds(dve, body)



def product_stage(k, name, terms, out, width, bias, relu=False):
    nc = k.nc
    T = len(terms)
    stride = P if width <= P else 2 * P
    chunks = [(c, min(NCH, NB - c)) for c in range(0, NB, NCH)]
    turned, turned_in, made, written, clipped = (k.sem(f"{name}_{s}") for s in (
        "turned", "turned_in", "made", "written", "clipped"))
    with ExitStack() as c:
        xt = k.sb(f"{name}_xt", [P, 2, T, NCH * P], F32, c)
        pt = k.ps(f"{name}_pt", [P, 2, T, 512], c)
        po = k.ps(f"{name}_po", [P, 2, NCH * stride], c)
        with k.block() as block:
            @block.tensor
            def _(pe):
                def turn(j):
                    b, m = chunks[j]
                    if j >= 2:
                        pe.wait_ge(turned_in, j - 1)
                    for t, (x, K, _) in enumerate(terms):
                        for q in range(m):
                            mm = pe.transpose(pt[0:K, j % 2, t, q * P:(q + 1) * P], x[:, b + q, :], k.ident[:])
                    mm.then_inc(turned, 1)

                turn(0)
                for j, (b, m) in enumerate(chunks):
                    if j + 1 < len(chunks):
                        turn(j + 1)
                    pe.wait_ge(turned_in, j + 1)
                    if j >= 2:
                        pe.wait_ge(written, j - 1)
                    for q in range(m):
                        for t, (_, K, w) in enumerate(terms):
                            mm = pe.matmul(po[:, j % 2, q * stride:q * stride + width], xt[0:K, j % 2, t, q * P:(q + 1) * P],
                                           w, start=(t == 0), stop=(t == T - 1))
                    mm.then_inc(made, 1)

            @block.scalar
            def _(act):
                K = terms[0][1]

                def clip(j):
                    b, m = chunks[j]
                    act.wait_ge(written, j + 1)
                    nc.scalar.activation(out[:, b:b + m, 0:width], out[:, b:b + m, 0:width], ACT.Relu).then_inc(clipped, 1)

                for j, (b, m) in enumerate(chunks):
                    act.wait_ge(turned, j + 1)
                    if j >= 2:
                        act.wait_ge(made, j - 1)
                    nc.scalar.copy(xt[0:K, j % 2, :, 0:m * P], pt[0:K, j % 2, :, 0:m * P]).then_inc(turned_in, 1)
                    if relu and j >= 1:
                        clip(j - 1)
                if relu:
                    clip(len(chunks) - 1)

            @block.vector
            def _(dve):
                for j, (b, m) in enumerate(chunks):
                    dve.wait_ge(made, j + 1)
                    dve.tensor_tensor(out[:, b:b + m, 0:width],
                                      po[:, j % 2, 0:m * stride].rearrange("p (b f) -> p b f", b=m)[:, :, 0:width],
                                      over_blocks(bias[:, 0:width], [P, m, width]), ALU.add).then_inc(written, 1)


class Chain:

    def __init__(self, dve, step, variances=None, roots=None):
        self.dve, self.step, self.n = dve, step, 0
        self.variances, self.roots, self.rooted = variances, roots, 0

    def root(self, ins, place):
        self.rooted += 1
        ins.then_inc(self.variances, 1)
        self.dve.wait_ge(self.roots, self.rooted)
        self(self.dve.reciprocal(place, place))

    def __call__(self, ins):
        self.n += 1
        ins.then_inc(self.step, 1)
        self.dve.wait_ge(self.step, self.n)

    def norm(self, k, out, x, sq, col, gain=None, bias=None, eps=1e-5):
        dve, full = self.dve, [P, NB, D]
        self(dve.tensor_reduce(col[:, 0, :], x[:], AX, ALU.add))
        self(dve.tensor_scalar(col[:, 0, :], col[:, 0, :], 1.0 / D, None, ALU.mult))
        self(dve.tensor_tensor(out[:], x[:], wide(col[:, 0, :], D, full), ALU.subtract))
        self(dve.tensor_tensor(sq[:], out[:], out[:], ALU.mult))
        self(dve.tensor_reduce(col[:, 1, :], sq[:], AX, ALU.add))
        self.root(dve.tensor_scalar(col[:, 1, :], col[:, 1, :], 1.0 / D, eps, ALU.mult, ALU.add), col[:, 1, :])
        self(dve.tensor_tensor(out[:], out[:], wide(col[:, 1, :], D, full), ALU.mult))
        if gain is not None:
            self(dve.tensor_tensor(out[:], out[:], over_blocks(gain[:], full), ALU.mult))
            self(dve.tensor_tensor(out[:], out[:], over_blocks(bias[:], full), ALU.add))


def root_program(act, variances, roots, places):
    for n, ap in enumerate(places):
        act.wait_ge(variances, n + 1)
        act.activation(ap, ap, ACT.Sqrt).then_inc(roots, 1)


def node_stage(k, name, program, norms=0):
    step, variances, roots = (k.sem(f"{name}_{s}") for s in ("step", "variances", "roots"))
    with k.block() as block:
        @block.scalar
        def _(act):
            root_program(act, variances, roots, [k.col[:, 1, :] for _ in range(norms)])

        @block.vector
        def _(dve):
            program(Chain(dve, step, variances, roots), dve)


def store_stage(k, name, pairs):
    stored = k.sem(name + "_stored")
    with k.block() as block:
        @block.sync
        def _(sp):
            for table, x in pairs:
                sp.dma_start(table.rearrange("(b p) f -> p b f", p=P), x).then_inc(stored, 16)
            sp.wait_ge(stored, 16 * len(pairs))


def global_token_stage(k):
    nc = k.nc
    step, summed, token, spread = (k.sem("gt_" + s) for s in ("step", "summed", "token", "spread"))
    with ExitStack() as c:
        part = k.sb("gt_part", [P, D], F32, c)
        g = k.sb("gt_g", [P, 1], F32, c)
        row = k.sb("gt_row", [P, D], F32, c)
        pg = k.ps("gt_pg", [P, 512], c)
        pr = k.ps("gt_pr", [P, 512], c)
        with k.block() as block:
            @block.tensor
            def _(pe):
                pe.wait_ge(summed, 1)
                pe.matmul(pg[:, 0:1], part[:], k.ones[:, 0:1], start=True, stop=True).then_inc(token, 1)
                pe.wait_ge(summed, 2)
                pe.matmul(pr[:, 0:D], g[:].to_broadcast([P, P]), k.w["Wg"][:], start=True, stop=True).then_inc(spread, 1)

            @block.vector
            def _(dve):
                link = Chain(dve, step)
                link(dve.tensor_scalar(k.X[:, NB - 1, :], k.X[:, NB - 1, :], k.last_rows[:], None, ALU.mult))
                dve.tensor_reduce(part[:], k.X[:].rearrange("p b f -> p f b"), AX, ALU.add).then_inc(summed, 1)
                dve.wait_ge(token, 1)
                dve.tensor_scalar(g[:], pg[:, 0:1], 1.0 / N, k.gtok[:], ALU.mult, ALU.add).then_inc(summed, 1)
                dve.wait_ge(spread, 1)
                link(dve.tensor_tensor(row[:], pr[:, 0:D], k.r["Wg"][:], ALU.add))
                link(dve.tensor_tensor(k.X[:], k.X[:], over_blocks(row[:], [P, NB, D]), ALU.add))


def batch_norm_stage(k, name, x, sq, gain, bias):
    nc, full = k.nc, [P, NB, D]
    step, summed, spread, variances, roots = (k.sem(f"{name}_{s}") for s in (
        "step", "summed", "spread", "variances", "roots"))
    with ExitStack() as c:
        part = k.sb(name + "_part", [P, 2, D], F32, c)
        row = k.sb(name + "_row", [P, 2, D], F32, c)
        pr = k.ps(name + "_pr", [P, 2, 512], c)
        with k.block() as block:
            @block.tensor
            def _(pe):
                for t in range(2):
                    pe.wait_ge(summed, t + 1)
                    pe.matmul(pr[:, t, 0:D], k.ones[:], part[:, t, :], start=True, stop=True).then_inc(spread, 1)

            @block.scalar
            def _(act):
                root_program(act, variances, roots, [row[:, 1]])

            @block.vector
            def _(dve):
                link = Chain(dve, step, variances, roots)
                link(dve.tensor_scalar(x[:, NB - 1, :], x[:, NB - 1, :], k.last_rows[:], None, ALU.mult))
                dve.tensor_reduce(part[:, 0], x[:].rearrange("p b f -> p f b"), AX, ALU.add).then_inc(summed, 1)
                dve.wait_ge(spread, 1)
                link(dve.tensor_scalar(row[:, 0], pr[:, 0, 0:D], 1.0 / N, None, ALU.mult))
                link(dve.tensor_tensor(x[:], x[:], over_blocks(row[:, 0], full), ALU.subtract))
                link(dve.tensor_tensor(sq[:], x[:], x[:], ALU.mult))
                link(dve.tensor_scalar(sq[:, NB - 1, :], sq[:, NB - 1, :], k.last_rows[:], None, ALU.mult))
                dve.tensor_reduce(part[:, 1], sq[:].rearrange("p b f -> p f b"), AX, ALU.add).then_inc(summed, 1)
                dve.wait_ge(spread, 2)
                link.root(dve.tensor_scalar(row[:, 1], pr[:, 1, 0:D], 1.0 / N, 1e-5, ALU.mult, ALU.add), row[:, 1])
                link(dve.tensor_tensor(row[:, 1], row[:, 1], gain[:], ALU.mult))
                link(dve.tensor_tensor(x[:], x[:], over_blocks(row[:, 1], full), ALU.mult))
                link(dve.tensor_tensor(x[:], x[:], over_blocks(bias[:], full), ALU.add))



class Order:

    def __init__(self, k, name):
        self.name = name
        self.lo = k.sb(name + "_lo", [P, J])
        self.lo_h = k.sb(name + "_lo_h", [P, J], BF16)
        self.far_i = k.sb(name + "_far_i", [P, J], I32)
        self.block_i = k.sb(name + "_block_i", [P, J // 2], I32)


def build(nc, a, out):
    with ExitStack() as ctx:
        k = Core(nc, ctx)
        early = k.early = ExitStack()
        by_dst, by_src = Order(k, "dst"), Order(k, "src")
        k.scores = k.sb("scores", [P, J])
        k.deg = k.sb("deg", [P, NB])
        k.shift = k.sb("shift", [P, NB, 3], BF16)
        acc = k.sb("acc", [P, NB, VW + 1])
        constants_stage(k, a)
        for o in (by_dst, by_src):
            o.slot = k.sb(o.name + "_slot", [P, J, 2], F32, early)
            o.block_f = k.sb(o.name + "_block_f", [P, J], F32, early)
            o.row = k.sb(o.name + "_row", [EP, EC], I32, early)
            o.meta = k.sb(o.name + "_meta", [EP, EC, 2], F32, early)
        by_dst.rows_dram = nc.dram_tensor("rows_by_dst", (P * J, RW), F32).ap()
        by_src.ids_dram = nc.dram_tensor("ids_by_src", (P * J, 2), F32).ap()
        edges_dram = nc.dram_tensor("edges_by_src", (P * J, VW), F32).ap()
        tables = [nc.dram_tensor(f"table{n}", (P * NB, D), F32).ap() for n in range(5)]
        table_kv = nc.dram_tensor("table_kv", (P * NB, VW), F32).ap()
        order_stage(k, by_dst, a["dst"], a["src"], lambda c: BlankRows(k, by_dst, by_src, c))
        heads_stage(k)
        order_stage(k, by_src, a["src"], a["dst"], lambda c: FeatureScatter(k, by_dst, a["edge_attr_64"], c))
        scatter_rounds = EC // (2 * CW)
        first_part = 21 * scatter_rounds // 50
        score_stage(k, by_dst, lambda c: IdScatter(k, by_src, c, "ia", 0, first_part))
        node_maximum_stage(k, by_dst)
        sum0 = acc[:].rearrange("p b w -> p (b w)")[:, 0:NB * RW].rearrange("p (b w) -> p b w", b=NB)
        attention_sum_stage(k, by_dst, sum0, lambda c: IdScatter(k, by_src, c, "ib", first_part, scatter_rounds))
        far_ends_stage(k, by_dst, by_src)
        early.close()

        X, full = k.X, [P, NB, D]
        A = k.sb("A", full)
        B = k.sb("B", full)
        wide2 = k.sb("wide2", [P, NB, 2 * D])
        col = k.col = k.sb("col", [P, 2, NB])


        def shares0(link, dve):
            link(dve.tensor_scalar(col[:, 0, :], sum0[:, :, DE + 1], 1e-6, None, ALU.add))
            link(dve.reciprocal(col[:, 0, :], col[:, 0, :]))
            link(dve.tensor_copy(sum0[:, :, DE], sum0[:, :, DE + 1]))
            link(dve.tensor_tensor(sum0[:, :, 0:DE + 1], sum0[:, :, 0:DE + 1], wide(col[:, 0, :], DE + 1, [P, NB, DE + 1]), ALU.mult))
        node_stage(k, "shares0", shares0)
        product_stage(k, "ev", [(sum0[:, :, 0:DE + 1], DE + 1, k.w["ev"][:])], A, D, k.r["none"])
        product_stage(k, "out1", [(A, D, k.w["out1"][:])], B, D, k.r["out1"], relu=True)
        product_stage(k, "out2", [(B, D, k.w["out2"][:])], A, D, k.r["out2"])

        def end0(link, dve):
            link(dve.tensor_tensor(A[:], A[:], X[:], ALU.add))
            link(dve.tensor_tensor(A[:], A[:], X[:], ALU.add))
            link.norm(k, X, A, B, col)
        node_stage(k, "end0", end0, norms=1)

        node_stage(k, "keep1", lambda link, dve: link(dve.tensor_copy(A[:], X[:])))
        global_token_stage(k)
        node_stage(k, "ln1", lambda link, dve: link.norm(k, B, X, wide2[:, :, 0:D], col, k.r["ln1g"], k.r["ln1b"]), norms=1)
        product_stage(k, "msg", [(B, D, k.w["msg"][:])], wide2, D, k.r["msg"])
        store_stage(k, "msg_table", [(tables[0], wide2[:, :, 0:D])])
        gather_sum_stage(k, "gs1", by_src, tables[0], acc[:, :, 0:D])

        def mix1(link, dve):
            link(dve.tensor_scalar(k.eps[:], k.eps[:], 1.0, None, ALU.add))
            link(dve.scalar_tensor_tensor(B[:], B[:], k.eps[:], acc[:, :, 0:D], ALU.mult, ALU.add))
        node_stage(k, "mix1", mix1)
        product_stage(k, "lin", [(B, D, k.w["lin"][:])], wide2, D, k.r["lin"], relu=True)

        def ln2(link, dve):
            link(dve.tensor_tensor(X[:], X[:], wide2[:, :, 0:D], ALU.add))
            link.norm(k, B, X, wide2[:, :, 0:D], col, k.r["ln2g"], k.r["ln2b"])
        node_stage(k, "ln2", ln2, norms=1)
        product_stage(k, "qky", [(B, D, k.w["qky"][:])], wide2, 2 * D, k.r["qky"])
        store_stage(k, "kv_table", [(table_kv, wide2[:, :, DE:2 * D])])
        tanh_stage(k, by_src, table_kv, wide2, edges_dram)
        softmax_weights_stage(k, by_src)
        weighted_sum_stage(k, by_src, edges_dram, acc)

        def shares1(link, dve):
            link(dve.tensor_scalar(col[:, 0, :], acc[:, :, VW], 1e-9, None, ALU.add))
            link(dve.reciprocal(col[:, 0, :], col[:, 0, :]))
            link(dve.tensor_tensor(acc[:], acc[:], wide(col[:, 0, :], VW + 1, [P, NB, VW + 1]), ALU.mult))
            link(dve.tensor_tensor(X[:], X[:], acc[:, :, DE:VW], ALU.add))
            link(dve.tensor_copy(acc[:, :, DE], acc[:, :, VW]))
        node_stage(k, "shares1", shares1)
        product_stage(k, "We", [(acc[:, :, 0:DE + 1], DE + 1, k.w["We"][:])], wide2, D, k.r["none"])

        def ln3(link, dve):
            link(dve.tensor_tensor(X[:], X[:], wide2[:, :, 0:D], ALU.add))
            link.norm(k, B, X, wide2[:, :, 0:D], col, k.r["ln3g"], k.r["ln3b"])
        node_stage(k, "ln3", ln3, norms=1)
        product_stage(k, "ffn1", [(B, D, k.w["ffn1"][:])], wide2, 2 * D, k.r["ffn1"], relu=True)
        product_stage(k, "ffn2", [(wide2[:, :, 0:D], D, k.w["ffn2"][:, 0:D]), (wide2[:, :, D:2 * D], D, k.w["ffn2"][:, D:2 * D])],
                      B, D, k.r["ffn2"])

        def end1(link, dve):
            link(dve.tensor_tensor(B[:], B[:], X[:], ALU.add))
            link(dve.tensor_tensor(A[:], A[:], B[:], ALU.add))
            link.norm(k, X, A, B, col)
        node_stage(k, "end1", end1, norms=1)

        product_stage(k, "ab", [(X, D, k.w["W1ab"][:])], wide2, 2 * D, k.r["ab"])
        store_stage(k, "a_table", [(tables[1], wide2[:, :, 0:D])])
        with ExitStack() as c:
            b_parts = k.sb("b_parts", [P, 3, NB, D], BF16, c)
            split_stage(k, wide2[:, :, D:2 * D], b_parts, B[:])
            message_stage(k, by_dst, tables[1], b_parts, acc[:, :, 0:D])
        product_stage(k, "bn", [(acc[:, :, 0:D], D, k.w["Wn"][:])], B, D, k.r["bn"], relu=True)

        def end2(link, dve):
            link(dve.tensor_tensor(B[:], B[:], X[:], ALU.add))
            link.norm(k, A, B, wide2[:, :, 0:D], col, k.r["gamma"], k.r["beta"])
            link(dve.tensor_tensor(B[:], A[:], X[:], ALU.add))
            link.norm(k, X, B, wide2[:, :, 0:D], col)
        node_stage(k, "end2", end2, norms=2)

        H = wide2[:, :, 0:D]
        T = wide2[:, :, D:2 * D]

        def sage(name, x, table, w_self, w_neigh, bias, dst, relu=True):
            store_stage(k, name + "_table", [(table, x[:])])
            counts = name == "sg1"
            gather_sum_stage(k, name + "_gs", by_dst, table, acc[:, :, 0:D + counts], D + counts)

            def mean(link, dve):
                if counts:
                    link(dve.tensor_scalar(k.deg[:], acc[:, :, D], 1.0, None, ALU.max))
                    link(dve.reciprocal(k.deg[:], k.deg[:]))
                link(dve.tensor_tensor(acc[:, :, 0:D], acc[:, :, 0:D], wide(k.deg[:], D, full), ALU.mult))
            node_stage(k, name + "_mean", mean)
            product_stage(k, name + "_pr", [(x, D, w_self[:]), (acc[:, :, 0:D], D, w_neigh[:])], dst, D, bias, relu)

        sage("sg1", X, tables[2], k.w["s1"], k.w["n1"], k.r["s1"], A)
        batch_norm_stage(k, "bn1", A, B, k.r["bn1g"], k.r["bn1b"])
        sage("sg2", A, tables[3], k.w["s2"], k.w["n2"], k.r["s2"], B)

        def res3(link, dve):
            link(dve.tensor_tensor(A[:], A[:], B[:], ALU.add))
        node_stage(k, "res3", res3)
        batch_norm_stage(k, "bn2", A, B, k.r["bn2g"], k.r["bn2b"])
        sage("sg3", A, tables[4], k.w["s3"], k.w["n3"], k.r["s3"], B, relu=False)

        def end3(link, dve):
            link.norm(k, A, B, H, col, k.r["lng"], k.r["lnb"])
            link(dve.tensor_tensor(A[:], A[:], X[:], ALU.add))
            link.norm(k, B, A, H, col)
        node_stage(k, "end3", end3, norms=2)

        written = k.sem("written")
        with k.block() as block:
            @block.sync
            def _(sp):
                sp.dma_start(out[0:(NB - 1) * P, :].rearrange("(b p) f -> p b f", p=P), B[:, 0:NB - 1, :]).then_inc(written, 16)
                sp.dma_start(out[(NB - 1) * P:N, :], B[0:LAST, NB - 1, :]).then_inc(written, 16)
                sp.wait_ge(written, 32)


def kernel(**inputs):
    import numpy as np
    import concourse.bacc as bacc
    from concourse.bass_utils import run_bass_kernel_spmd

    nc = bacc.Bacc("TRN2", target_bir_lowering=False, num_devices=1)
    arrays, a = {}, {}
    for name in inputs:
        v = np.ascontiguousarray(inputs[name])
        if v.ndim == 0:
            v = v.reshape(1)
        arrays["in_" + name] = v
        a[name] = nc.dram_tensor("in_" + name, v.shape, mybir.dt.from_np(v.dtype), kind="ExternalInput").ap()
    out = nc.dram_tensor("out", (N, D), F32, kind="ExternalOutput").ap()
    build(nc, a, out)
    return run_bass_kernel_spmd(nc, [arrays], core_ids=[0]).results[0]["out"]
```
